# Optimizing a Trainium2 kernel written in Bass

```python
import numpy as np
import jax
import jax.numpy as jnp

def _softmax(x, axis=-1):
    return jax.nn.softmax(x, axis=axis)

def _gelu(x):
    return jax.nn.gelu(x, approximate=True)

def _silu(x):
    return jax.nn.silu(x)

def _sigmoid(x):
    return jax.nn.sigmoid(x)

def _layernorm(x, axis=-1, eps=1e-05):
    m = jnp.mean(x, axis=axis, keepdims=True)
    v = jnp.var(x, axis=axis, keepdims=True)
    return (x - m) / jnp.sqrt(v + eps)

def _scatter_add(tgt, idx, src, axis=0):
    return tgt.at[idx].add(src)

def _segment_sum(src, seg, n):
    return jax.ops.segment_sum(src, seg, n)
kernel_name = 'mk_decoder_preln_d1_seqx_r8_e80117'

def setup_inputs(seed: int=0):
    np.random.seed(seed)
    _w = jnp.asarray

    def _rec_inputs():
        import jax
        import jax.numpy as jnp
        _rk = jax.random.key(seed)
        x = -7.109e-05 + 0.9999 * jax.random.normal(jax.random.fold_in(_rk, 1), (4, 256, 256), jnp.float32)
        _lenS = 256 - jax.random.randint(jax.random.fold_in(_rk, 7), (4,), 0, max(1, 256 // 4) + 1, jnp.int32)
        _lenS2 = 256 - jax.random.randint(jax.random.fold_in(_rk, 8), (4,), 0, max(1, 256 // 4) + 1, jnp.int32)
        _ctx_2048P = jax.random.normal(jax.random.fold_in(_rk, 11), (4, 16, 256), jnp.float32)
        _ctx_2048c = jax.random.dirichlet(jax.random.fold_in(_rk, 511), 0.3 * jnp.ones((16,), jnp.float32), (4, 256))
        _ctx_2048t = jnp.einsum('bsk,bkd->bsd', _ctx_2048c, _ctx_2048P)
        _ctx_2048t = _ctx_2048t * jax.lax.rsqrt(jnp.mean(jnp.square(_ctx_2048t)) + 1e-12) * 0.953939
        ctx_2048 = -3.05549e-07 + 0.0199987 * (_ctx_2048t + 0.3 * jax.random.normal(jax.random.fold_in(_rk, 611), (4, 256, 256), jnp.float32))
        return (x, ctx_2048)
    x, ctx_2048 = _rec_inputs()

    def _L0_attn_setup():
        import jax, jax.numpy as jnp
        import numpy as np
        D_MODEL = 256
        N_HEADS = 16
        D_HEAD = D_MODEL // N_HEADS
        B, S = (2, 256)
        EPS = 1e-05

        def _mhsa(X, ln_g, ln_b, Wq, bq, Wk, bk, Wv, bv, Wo, bo):
            n_ctx = X.shape[-2]
            mu = jnp.mean(X, axis=-1, keepdims=True)
            var = jnp.mean(jnp.square(X - mu), axis=-1, keepdims=True)
            Xn = (X - mu) * jax.lax.rsqrt(var + EPS) * ln_g + ln_b

            def split_heads(t):
                return t.reshape(t.shape[:-1] + (N_HEADS, D_HEAD)).swapaxes(-2, -3)
            Q = split_heads(Xn @ Wq + bq)
            K = split_heads(Xn @ Wk + bk)
            V = split_heads(Xn @ Wv + bv)
            scores = jnp.einsum('bhqd,bhkd->bhqk', Q, K) / jnp.sqrt(jnp.float32(D_HEAD))
            causal = jnp.tril(jnp.ones((n_ctx, n_ctx), dtype=bool))
            scores = jnp.where(causal, scores, jnp.float32(-jnp.inf))
            A = jax.nn.softmax(scores, axis=-1)
            AV = jnp.einsum('bhqk,bhkd->bhqd', A, V)
            AV = AV.swapaxes(-2, -3).reshape(X.shape[:-1] + (D_MODEL,))
            return AV @ Wo + bo
        key = jax.random.key(seed)
        ks = jax.random.split(key, 10)
        sd = 1.0 / np.sqrt(D_MODEL)
        inp = {'X': jax.random.normal(ks[0], (B, S, D_MODEL), dtype=jnp.float32), 'ln_g': jnp.ones((D_MODEL,), jnp.float32), 'ln_b': jnp.zeros((D_MODEL,), jnp.float32), 'Wq': jax.random.uniform(ks[1], (D_MODEL, D_MODEL), jnp.float32, -sd, sd), 'bq': jax.random.uniform(ks[2], (D_MODEL,), jnp.float32, -sd, sd), 'Wk': jax.random.uniform(ks[3], (D_MODEL, D_MODEL), jnp.float32, -sd, sd), 'bk': jax.random.uniform(ks[4], (D_MODEL,), jnp.float32, -sd, sd), 'Wv': jax.random.uniform(ks[5], (D_MODEL, D_MODEL), jnp.float32, -sd, sd), 'bv': jax.random.uniform(ks[6], (D_MODEL,), jnp.float32, -sd, sd), 'Wo': jax.random.uniform(ks[7], (D_MODEL, D_MODEL), jnp.float32, -sd, sd), 'bo': jax.random.uniform(ks[8], (D_MODEL,), jnp.float32, -sd, sd)}
        return inp
    _L0_attn_all = _L0_attn_setup()
    _L0_attn_in = {k: v for k, v in _L0_attn_all.items() if k in ('ln_g', 'ln_b', 'Wq', 'bq', 'Wk', 'bk', 'Wv', 'bv', 'Wo', 'bo')}
    del _L0_attn_all

    def _L0_xattn_setup():
        import jax, jax.numpy as jnp
        import numpy as np
        FP8_MAX = 448.0
        ACT_EPS = 0.0001
        W_EPS = 1e-06
        BLK = 128

        def quant_dequant_act_1x128(x):
            E, M, K = x.shape
            xb = x.reshape(E, M, K // BLK, BLK)
            amax = jnp.max(jnp.abs(xb), axis=-1, keepdims=True)
            safe = jnp.maximum(amax, ACT_EPS)
            q = (xb * (FP8_MAX / safe)).astype(jnp.float8_e4m3fn)
            return (q.astype(jnp.float32) * (safe / FP8_MAX)).reshape(E, M, K)

        def quant_dequant_weight_128x128(w):
            E, N, K = w.shape
            wb = w.reshape(E, N // BLK, BLK, K // BLK, BLK)
            amax = jnp.max(jnp.abs(wb), axis=(2, 4), keepdims=True)
            safe = jnp.maximum(amax, W_EPS)
            q = (wb * (FP8_MAX / safe)).astype(jnp.float8_e4m3fn)
            return (q.astype(jnp.float32) * (safe / FP8_MAX)).reshape(E, N, K)
        key = jax.random.key(seed)
        kx, kw = jax.random.split(key)
        E, M, K, N = (8, 512, 256, 256)
        x = jax.random.normal(kx, (E, M, K), dtype=jnp.float32)
        weight = jax.random.normal(kw, (E, N, K), dtype=jnp.float32) * 0.02
        return {'x': x, 'weight': weight}
    _L0_xattn_all = _L0_xattn_setup()
    _L0_xattn_in = {k: v for k, v in _L0_xattn_all.items() if k in ()}
    del _L0_xattn_all

    def _L0_ffn_setup():
        import jax, jax.numpy as jnp
        import numpy as np
        B, S, H, E, K, I = (2, 128, 256, 32, 8, 96)
        key = jax.random.key(seed)
        ks = jax.random.split(key, 5)
        scaled = lambda k, shp, fan: jax.random.normal(k, shp, jnp.float32) * fan ** (-0.5)
        return {'hidden_states': jax.random.normal(ks[0], (B, S, H), jnp.float32), 'router_w': scaled(ks[1], (E, H), H), 'w_gate': scaled(ks[2], (E, H, I), H), 'w_up': scaled(ks[3], (E, H, I), H), 'w_down': scaled(ks[4], (E, I, H), I)}
    _L0_ffn_all = _L0_ffn_setup()
    _L0_ffn_in = {k: v for k, v in _L0_ffn_all.items() if k in ('router_w', 'w_gate', 'w_up', 'w_down')}
    del _L0_ffn_all
    return {'x': x, 'ctx_2048': ctx_2048, 'L0_attn_ln_g': _L0_attn_in['ln_g'], 'L0_attn_ln_b': _L0_attn_in['ln_b'], 'L0_attn_Wq': _L0_attn_in['Wq'], 'L0_attn_bq': _L0_attn_in['bq'], 'L0_attn_Wk': _L0_attn_in['Wk'], 'L0_attn_bk': _L0_attn_in['bk'], 'L0_attn_Wv': _L0_attn_in['Wv'], 'L0_attn_bv': _L0_attn_in['bv'], 'L0_attn_Wo': _L0_attn_in['Wo'], 'L0_attn_bo': _L0_attn_in['bo'], 'L0_ffn_router_w': _L0_ffn_in['router_w'], 'L0_ffn_w_gate': _L0_ffn_in['w_gate'], 'L0_ffn_w_up': _L0_ffn_in['w_up'], 'L0_ffn_w_down': _L0_ffn_in['w_down']}

def reference(x, ctx_2048, L0_attn_ln_g, L0_attn_ln_b, L0_attn_Wq, L0_attn_bq, L0_attn_Wk, L0_attn_bk, L0_attn_Wv, L0_attn_bv, L0_attn_Wo, L0_attn_bo, L0_ffn_router_w, L0_ffn_w_gate, L0_ffn_w_up, L0_ffn_w_down):
    import jax
    import jax.numpy as jnp

    def _L0_attn_ref(X, ln_g, ln_b, Wq, bq, Wk, bk, Wv, bv, Wo, bo):
        import jax, jax.numpy as jnp
        import numpy as np
        D_MODEL = 256
        N_HEADS = 16
        D_HEAD = D_MODEL // N_HEADS
        B, S = (2, 256)
        EPS = 1e-05

        def _mhsa(X, ln_g, ln_b, Wq, bq, Wk, bk, Wv, bv, Wo, bo):
            n_ctx = X.shape[-2]
            mu = jnp.mean(X, axis=-1, keepdims=True)
            var = jnp.mean(jnp.square(X - mu), axis=-1, keepdims=True)
            Xn = (X - mu) * jax.lax.rsqrt(var + EPS) * ln_g + ln_b

            def split_heads(t):
                return t.reshape(t.shape[:-1] + (N_HEADS, D_HEAD)).swapaxes(-2, -3)
            Q = split_heads(Xn @ Wq + bq)
            K = split_heads(Xn @ Wk + bk)
            V = split_heads(Xn @ Wv + bv)
            scores = jnp.einsum('bhqd,bhkd->bhqk', Q, K) / jnp.sqrt(jnp.float32(D_HEAD))
            causal = jnp.tril(jnp.ones((n_ctx, n_ctx), dtype=bool))
            scores = jnp.where(causal, scores, jnp.float32(-jnp.inf))
            A = jax.nn.softmax(scores, axis=-1)
            AV = jnp.einsum('bhqk,bhkd->bhqd', A, V)
            AV = AV.swapaxes(-2, -3).reshape(X.shape[:-1] + (D_MODEL,))
            return AV @ Wo + bo
        return _mhsa(X, ln_g, ln_b, Wq, bq, Wk, bk, Wv, bv, Wo, bo)

    def _L0_xattn_ref(x, weight):
        import jax, jax.numpy as jnp
        import numpy as np
        FP8_MAX = 448.0
        ACT_EPS = 0.0001
        W_EPS = 1e-06
        BLK = 128

        def quant_dequant_act_1x128(x):
            E, M, K = x.shape
            xb = x.reshape(E, M, K // BLK, BLK)
            amax = jnp.max(jnp.abs(xb), axis=-1, keepdims=True)
            safe = jnp.maximum(amax, ACT_EPS)
            q = (xb * (FP8_MAX / safe)).astype(jnp.float8_e4m3fn)
            return (q.astype(jnp.float32) * (safe / FP8_MAX)).reshape(E, M, K)

        def quant_dequant_weight_128x128(w):
            E, N, K = w.shape
            wb = w.reshape(E, N // BLK, BLK, K // BLK, BLK)
            amax = jnp.max(jnp.abs(wb), axis=(2, 4), keepdims=True)
            safe = jnp.maximum(amax, W_EPS)
            q = (wb * (FP8_MAX / safe)).astype(jnp.float8_e4m3fn)
            return (q.astype(jnp.float32) * (safe / FP8_MAX)).reshape(E, N, K)
        xq = quant_dequant_act_1x128(x)
        wq = quant_dequant_weight_128x128(weight)
        return jnp.einsum('emk,enk->emn', xq, wq)

    def _L0_ffn_ref(hidden_states, router_w, w_gate, w_up, w_down):
        import jax, jax.numpy as jnp
        import numpy as np
        B, S, H, E, K, I = (2, 128, 256, 32, 8, 96)
        Bq, Sq, Hd = hidden_states.shape
        x = hidden_states.reshape(-1, Hd)
        logits = x @ router_w.T
        probs = jax.nn.softmax(logits.astype(jnp.float32), axis=-1)
        rw, sel = jax.lax.top_k(probs, K)
        rw = rw / jnp.sum(rw, axis=-1, keepdims=True)
        rw = rw.astype(x.dtype)

        def body(acc, operand):
            e, wg, wu, wd = operand
            w_e = jnp.sum(jnp.where(sel == e, rw, jnp.zeros_like(rw)), axis=-1)
            h = jax.nn.silu(x @ wg) * (x @ wu)
            return (acc + h @ wd * w_e[:, None], None)
        acc0 = jnp.zeros_like(x)
        acc, _ = jax.lax.scan(body, acc0, (jnp.arange(E), w_gate, w_up, w_down))
        return acc.reshape(Bq, Sq, Hd)
    x = x + _L0_attn_ref(_layernorm(x, axis=-1), L0_attn_ln_g, L0_attn_ln_b, L0_attn_Wq, L0_attn_bq, L0_attn_Wk, L0_attn_bk, L0_attn_Wv, L0_attn_bv, L0_attn_Wo, L0_attn_bo)
    x = x + _L0_xattn_ref(_layernorm(x, axis=-1), ctx_2048)
    x = x + _L0_ffn_ref(_layernorm(x, axis=-1), L0_ffn_router_w, L0_ffn_w_gate, L0_ffn_w_up, L0_ffn_w_down)
    return x

_drawn_inputs = setup_inputs


def setup_inputs(seed=0):
    import zlib

    import numpy as np

    out = dict(_drawn_inputs(seed))
    spreads = {'L0_attn_ln_g': (1.0, 0.6), 'L0_attn_ln_b': (0.0, 0.1)}
    factors = {'L0_attn_bq': 8.0, 'L0_attn_bk': 8.0}
    for name, (base, spread) in spreads.items():
        noise = np.random.default_rng([zlib.crc32(name.encode()), seed]).standard_normal(out[name].shape)
        drawn = base * np.exp(spread * noise) if base else spread * noise
        out[name] = jnp.asarray(drawn.astype(out[name].dtype))
    for name, factor in factors.items():
        out[name] = (out[name] * factor).astype(out[name].dtype)
    return out
```

```python
from contextlib import ExitStack

import concourse.bass as bass
from concourse import mybir

F32 = mybir.dt.float32
F32R = mybir.dt.float32r
BF16 = mybir.dt.bfloat16
U32 = mybir.dt.uint32
ALU = mybir.AluOpType
ACT = mybir.ActivationFunctionType
AX = mybir.AxisListType

P = 128
NB, S, D = 4, 256, 256
T = NB * S
NT = T // P
KT = D // P
HALF = T // 2
NH, DH = 16, 16
NPAIR = NH // 2
ROWS = 64
MAXROW = 3 * DH
VW = DH + 1
EPS = 1e-5
FP8_MAX, ACT_FLOOR, W_FLOOR = 448.0, 1e-4, 1e-6
NE, TOPK, NI = 32, 8, 96
GE = 4
GROUPS = NE // GE
GW = GE * NI
CH = GW // P
PERIOD = 2
NEG = -1e30
C_ID, C_QH, C_QL, C_KH, C_KL, C_MS, C_MT, C_ONE = range(8)
LAG = 11
STEPS = 54
AT = {"N": 0, "A": 0, "W": 1, "Q": 4, "X": 5, "Y": 8, "R": 9}


def host_constants():
    import numpy as np

    c = np.zeros((P, C_ONE * P + 2), np.float32)
    blk = [c[:, i * P:(i + 1) * P] for i in range(C_ONE)]
    blk[C_ID][:] = np.eye(P)
    r = np.arange(P)[:, None] % 32
    col = np.arange(P)[None, :]
    same = (col // ROWS == r // DH) & (col % DH == r % DH)
    copy = col % ROWS // DH
    blk[C_QH][:] = same & ((copy == 0) | (copy == 1))
    blk[C_QL][:] = same & (copy == 2)
    blk[C_KH][:] = same & ((copy == 0) | (copy == 2))
    blk[C_KL][:] = same & (copy == 1)
    q = np.arange(P)[:, None]
    k = np.arange(P)[None, :]
    blk[C_MS][:] = np.where(k <= q, 0.0, NEG)
    blk[C_MT][:] = np.where(q <= k, 0.0, NEG)
    c[:, C_ONE * P] = np.arange(P) % ROWS == MAXROW
    c[:, C_ONE * P + 1] = -0.5
    return c


def decoder_layer(nc, consts, x, ctx_2048, ln_g, ln_b, Wq, bq, Wk, bk, Wv, bv, Wo, bo,
                  router_w, w_gate, w_up, w_down, out):
    routing_dram = nc.dram_tensor("routing_t", [NE, T], F32).ap()

    base = nc.sbuf_base
    cursor = [base]
    address = {}

    def sb(name, shape, dt, over=None):
        size = {BF16: 2}.get(dt, 4)
        for s in shape[1:]:
            size *= s
        at = (cursor[0] + 31) // 32 * 32 if over is None else over
        cursor[0] = at + size if over is None else cursor[0]
        address[name] = at
        return nc.alloc_sbuf_tensor_at(name, shape, dt, offset=at)

    cst = sb("cst", [P, C_ONE * P + 2], F32)
    R = sb("R", [P, 4, P], F32R)
    ident_bf = sb("ident_bf", [P, P], BF16)
    mask_s = sb("mask_s", [P, 2, P], BF16)
    mask_t = sb("mask_t", [P, 2, P], BF16)
    zeros_bf = sb("zeros_bf", [P, HALF], BF16)
    xs = sb("xs", [P, NT, D], F32)
    zth = sb("zth", [P, KT, T], F32R)
    ztl = sb("ztl", [P, KT, T], F32R)
    wstage = sb("wstage", [P, 2, 3, 768], F32)
    prow = sb("prow", [8, P], F32)
    par = sb("par", [P, 8], F32)
    bvb = sb("bvb", [P, D], F32)
    bob = sb("bob", [P, D], F32)
    mx = sb("mx", [P, NB, 2, NH], F32)
    mneg = sb("mneg", [2 * NH, 2, P], F32R)
    stats = sb("stats", [P, 3, NT, 6], F32)
    mv = sb("mv", [P, 3, NT, 2], F32)
    rs_in = sb("rs_in", [P, 3, NT], F32)
    rstd = sb("rstd", [P, 3, NT], F32)
    rinv = sb("rinv", [P, NB, 2, NH], F32)
    cst_half = cst[:, C_ONE * P + 1:C_ONE * P + 2]
    cw = sb("cw", [P, 2 * NB, D], F32, over=address["wstage"])
    cm = sb("cm", [P, 2 * NB, D], F32, over=address["wstage"] + 2 * NB * D * 4)
    cq = sb("cq", [P, 2 * NB, D], BF16)
    cqt = sb("cqt", [P, NB, KT, D], BF16)
    wam = sb("wam", [P, 6, 16], F32)
    xam = sb("xam", [P, NB, 5, 4], F32)
    xsc = sb("xsc", [P, NB, 4, 2], F32)
    xq3 = sb("xq3", [P, 2, 4, P], F32)
    xqb = sb("xqb", [P, 2, 4, P], BF16)
    xqt = sb("xqt", [P, 2, KT, S], BF16)
    rw_sb = sb("rw_sb", [NE, D], F32)
    rwt = sb("rwt", [P, KT, NE], F32)
    lmx = sb("lmx", [P, NT], F32)
    esum = sb("esum", [P, NT], F32)
    erec = sb("erec", [P, NT], F32)
    ex = sb("ex", [P, NT, NE], F32)
    prob = sb("prob", [P, NT, NE], F32)
    top = sb("top", [P, NT, 8], F32)
    rep = sb("rep", [P, NT, NE], F32)
    wun = sb("wun", [P, NT, NE], F32)
    wsum = sb("wsum", [P, NT], F32)
    wrec = sb("wrec", [P, NT], F32)
    wrt = sb("wrt", [P, NT, NE], F32)
    shared = cursor[0]
    zs = sb("zs", [P, NT, D], F32)
    zf = sb("zf", [P, 2, KT, S], F32)
    wraw = sb("wraw", [P, 4, KT, D], F32)
    xq1 = sb("xq1", [P, 2, 4, P], F32, over=address["wraw"])
    xq2 = sb("xq2", [P, 2, 4, P], F32, over=address["wraw"] + 8 * P * 4)
    wh = sb("wh", [P, 4, KT, D], F32R)
    wl = sb("wl", [P, 4, KT, D], F32R)
    pf = sb("pf", [P, 2, HALF], F32)
    ph = sb("ph", [P, 2, HALF], F32R)
    pl = sb("pl", [P, 2, HALF], F32R)
    qst = sb("qst", [P, NPAIR, T], F32R)
    kst = sb("kst", [P, NPAIR, T], F32R)
    vs = sb("vs", [P, NT, NH, VW], F32)
    pt = sb("pt", [P, 2, 2, 384], F32)
    avn = zs
    cursor[0] = shared + 4 * NT * D * 1
    gh = sb("gh", [P, 2, 3, 768], F32R)
    gl = sb("gl", [P, 2, 3, 768], F32R)
    wb = sb("wb", [P, 2, CH, T], F32)
    sg = sb("sg", [P, 2, T], F32)
    tg = sb("tg", [P, 2, T], F32)
    hf = sb("hf", [P, 2, T], F32)
    hh = sb("hh", [P, 2, T], F32R)
    hl = sb("hl", [P, 2, T], F32R)
    yt = sb("yt", [P, KT, T], F32)
    wT_sb = sb("wT_sb", [NE, T], F32)
    ident = cst[:, C_ID * P:(C_ID + 1) * P]

    with ExitStack() as ctx:
        ps = ctx.enter_context(nc.psum_tensor("ps", [P, 8, 512], F32))

        def sem(name):
            return ctx.enter_context(nc.semaphore(name))

        SB = ps[:, 0:2, :]
        TB = ps[:, 2:4, :]
        OB = ps[:, 4:6, :]
        M0, M1 = 6, 7

        d_const, d_par, d_bias, d_ctx, d_rw = (sem(n) for n in ("d_const", "d_par", "d_bias", "d_ctx", "d_rw"))
        d_x = [sem(f"d_x{b}") for b in range(NB)]
        d_w = [sem(f"d_w{i}") for i in range(4)]
        d_max = [sem(f"d_max{b}") for b in range(NB)]
        d_wst = [sem(f"d_wst{i}") for i in range(2)]
        d_wb = [sem(f"d_wb{i}") for i in range(2)]
        d_rt, d_out = sem("d_rt"), sem("d_out")
        cvt = sem("cvt")
        names = ("ah al atp av_ready avt_n bias_x cab car cev cs1 cs2 cs3 cs4 csb csc csf ctp down e_ready "
                 "ers exs fin ftp gate ghi glo hhi hlo hmul lg lmxs mng mtp pff phh pj pll prb qam qev qs1 qs2 "
                 "qs3 qs4 qsb qsc qsf qtp reps rev rev2 rin rp rtp rwt s_max s_ready silu t_ready tmul tps "
                 "up vev vpj whi wlo wo wrs wrts wss wte wtp wus x1 x2 xmm xscs yev yh yl ytp yzero zff zh zl "
                 "ztp").split()
        g = {n: sem("s_" + n) for n in names}

        ln_bn, ln_ag, ln_ri, ln_rs, ln_zn = ([sem(f"ln{i}_{n}") for i in range(3)]
                                             for n in ("bn", "ag", "ri", "rs", "zn"))

        block = ctx.enter_context(nc.Block())

        def bs(b):
            return slice(b * S, (b + 1) * S)

        def rows_of(step, name):
            b = step - (LAG + 9) - AT[name]
            return b // 8 if b >= 0 and b % 8 == 0 and b // 8 < NB else None

        def load_group(sp, n, buf):
            for k, w in enumerate((w_gate, w_up)):
                for kt in range(KT):
                    sp.dma_start(wstage[:, buf, k, kt * GW:(kt + 1) * GW].rearrange("p (e i) -> p e i", e=GE),
                                 w[bass.ds(n * GE, GE), kt * P:(kt + 1) * P, :].rearrange("e p i -> p e i")
                                 ).then_inc(d_wst[buf], 16)
            sp.dma_start(wstage[:, buf, 2, :].rearrange("p (c d) -> p c d", c=CH),
                         w_down.rearrange("e i d -> (e i) d")[bass.ds(n * GW, GW), :]
                         .rearrange("(c p) d -> p c d", p=P)).then_inc(d_wst[buf], 16)

        def load_routing(sp, n, buf):
            for c in range(CH):
                lo = c * P
                while lo < (c + 1) * P:
                    e = lo // NI
                    hi = min((e + 1) * NI, (c + 1) * P)
                    sp.dma_start(wb[lo - c * P:hi - c * P, buf, c, :],
                                 routing_dram[bass.ds(n * GE + e, 1), :].partition_broadcast(hi - lo)
                                 ).then_inc(d_wb[buf], 16)
                    lo = hi

        WB_DMAS = 6
        WST_DMAS = 5

        def rsqrt(pool, ln, b):
            pool.wait_ge(ln_ri[ln], b + 1)
            t = slice(2 * b, 2 * b + 2)
            pool.tensor_tensor(rstd[:, ln, t], rs_in[:, ln, t], cst_half.to_broadcast([P, 2]), ALU.pow
                               ).then_inc(ln_rs[ln], 1)

        def split_lo(pool, n, buf, part):
            pool.wait_ge(g["ghi"], 3 * n + part + 1)
            pool.tensor_tensor(gl[:, buf, part], wstage[:, buf, part], gh[:, buf, part].bitcast(F32), ALU.subtract
                               ).then_inc(g["glo"], 1)

        def pool_experts(pool):
            for part in range(3):
                split_lo(pool, 0, 0, part)

            def period(i, last):
                for pg in range(PERIOD):
                    n = i * PERIOD + pg
                    pool.wait_ge(d_wb[pg], (i + 1) * (16 * WB_DMAS))
                    for c in range(CH):
                        for h in range(2):
                            k = (n * CH + c) * 2 + h
                            hs = slice(h * HALF, (h + 1) * HALF)
                            j = (pg * CH + c) % 2
                            pool.wait_ge(g["silu"], k + 1)
                            pool.tensor_tensor(tg[:, j, hs], sg[:, j, hs], wb[:, pg, c, hs], ALU.mult
                                               ).then_inc(g["tmul"], 1)
                        if not (last and pg == PERIOD - 1):
                            split_lo(pool, n + 1, 1 - pg, c)

            with pool.Fori(0, GROUPS // PERIOD - 1) as i:
                period(i, False)
            period(GROUPS // PERIOD - 1, True)

        def bf16_bank(bank):
            return ps[:, bank, 0:256].bitcast(BF16)

        def stack_evac(eng, u, which_eng):
            half, which, mt = u // 4, u % 4 // 2, u % 2
            dst = kst if which else qst
            for lp in range(which_eng, 4, 2):
                k = 4 * u + lp
                eng.wait_ge(g["rp"], k + 1)
                o = dst[:, 4 * mt + lp, half * HALF:(half + 1) * HALF]
                i = ps[:, 2 + k % 4, :]
                one = cst[:, C_ONE * P:C_ONE * P + 1]
                if which_eng == 0:
                    if which:
                        ins = eng.activation(o, i, ACT.Identity, bias=one)
                    else:
                        ins = eng.activation(o, i, ACT.Copy)
                    ins.then_inc(g["rev"], 1)
                else:
                    if which:
                        ins = eng.tensor_scalar(o, i, one, None, ALU.add)
                    else:
                        ins = eng.tensor_copy(o, i)
                    ins.then_inc(g["rev2"], 1)

        def act_experts(act):
            def period(i):
                for pg in range(PERIOD):
                    for c in range(CH):
                        n = (i * PERIOD + pg) * CH + c
                        j = (pg * CH + c) % 2
                        for h in range(2):
                            hs = slice(h * HALF, (h + 1) * HALF)
                            act.wait_ge(g["gate"], n * 2 + (h + 1))
                            act.activation(sg[:, j, hs], ps[:, h, :], ACT.Silu).then_inc(g["silu"], 1)
                        for h in range(2):
                            hs = slice(h * HALF, (h + 1) * HALF)
                            act.wait_ge(g["hmul"], n * 2 + (h + 1))
                            act.activation(hh[:, j, hs], hf[:, j, hs], ACT.Copy).then_inc(g["hhi"], 1)

            with act.Fori(0, GROUPS // PERIOD) as i:
                period(i)

        def pe_experts(pe, f32_product):
            ks = range(KT)

            def hidden(n, buf, c, first=False):
                for h in range(2):
                    hs = slice(h * HALF, (h + 1) * HALF)
                    for part, done in ((0, "silu"), (1, "hmul")):
                        if not first:
                            pe.wait_ge(g[done], (n - 1) * 2 + (h + 1))
                        cs = [slice(k * GW + c * P, k * GW + (c + 1) * P) for k in ks]
                        f32_product(ps[:, 2 * part + h, :], [gh[:, buf, part, s] for s in cs],
                                    [gl[:, buf, part, s] for s in cs], [zth[:, k, hs] for k in ks],
                                    [ztl[:, k, hs] for k in ks], True, True
                                    ).then_inc(g["gate" if part == 0 else "up"], 1)

            def output(n, buf, c):
                j = (buf * CH + c) % 2
                for h in range(2):
                    hs = slice(h * HALF, (h + 1) * HALF)
                    pe.wait_ge(g["hhi"], n * 2 + (h + 1))
                    pe.wait_ge(g["hlo"], n * 2 + (h + 1))
                    for k in ks:
                        w = slice(c * D + k * P, c * D + (k + 1) * P)
                        mm = f32_product(ps[:, 4 + 2 * k + h, :], [gh[:, buf, 2, w]], [gl[:, buf, 2, w]],
                                         [hh[:, j, hs]], [hl[:, j, hs]], False, True)
                mm.then_inc(g["down"], 1)

            def weights(n):
                pe.wait_ge(g["ghi"], n * 3 + 3)
                pe.wait_ge(g["glo"], n * 3 + 3)

            pe.wait_ge(g["wte"], 2)
            pe.wait_ge(g["yzero"], 2)
            pe.wait_ge(g["avt_n"], 2 * NB)
            for k in range(4):
                mm = pe.matmul(ps[:, 4 + k, :], zeros_bf[:, 0:P], zeros_bf[:, :], start=True, stop=False,
                               skip_group_check=True)
            mm.then_inc(g["down"], 1)
            pe.wait_ge(g["yh"], NB)
            pe.wait_ge(g["yl"], NB)
            weights(0)
            hidden(0, 0, 0, first=True)

            def period(i, last):
                for pg in range(PERIOD):
                    for c in range(CH):
                        grp = i * PERIOD + pg
                        n = grp * CH + c
                        if not (last and pg == PERIOD - 1 and c == CH - 1):
                            if c == CH - 1:
                                weights(grp + 1)
                                hidden(n + 1, 1 - pg, 0)
                            else:
                                hidden(n + 1, pg, c + 1)
                        output(n, pg, c)

            with pe.Fori(0, GROUPS // PERIOD - 1) as i:
                period(i, False)
            period(GROUPS // PERIOD - 1, True)

        def quant_scales(dve, am, floor, ready, s_safe, s_scale, n):
            src = am[:, 1, :] if ready == "car" else am[:, 0, :]
            dve.wait_ge(g[ready], n)
            dve.tensor_scalar(am[:, 2, :], src, floor, None, ALU.max).then_inc(g[s_safe], 1)
            dve.wait_ge(g[s_safe], 3 * n - 2)
            dve.tensor_scalar(am[:, 3, :], am[:, 2, :], 1.0 / FP8_MAX, None, ALU.mult).then_inc(g[s_safe], 1)
            dve.reciprocal(am[:, 0, :], am[:, 2, :]).then_inc(g[s_safe], 1)
            dve.wait_ge(g[s_safe], 3 * n)
            dve.tensor_scalar(am[:, 4, :], am[:, 0, :], FP8_MAX, None, ALU.mult).then_inc(g[s_scale], 1)
            dve.wait_ge(g[s_scale], n)

        def round_step(dve, src, dst, s_exp, s_magic, n):
            dve.tensor_scalar(dst.bitcast(U32), src.bitcast(U32), 0x7F800000, None, ALU.bitwise_and
                              ).then_inc(g[s_exp], 1)
            dve.wait_ge(g[s_exp], n)
            dve.tensor_scalar(dst, dst, 2.0 ** -6, 1.5 * 2.0 ** 20, ALU.max, ALU.mult).then_inc(g[s_magic], 1)

        def route(dve, b):
            t2 = slice(2 * b, 2 * b + 2)
            dve.wait_ge(g["lg"], b + 1)
            dve.tensor_reduce(lmx[:, t2], ps[:, M1, 0:2 * NE].rearrange("p (t e) -> p t e", t=2), AX.X, ALU.max,
                              negate=True).then_inc(g["lmxs"], 1)
            dve.wait_ge(g["exs"], 2 * b + 2)
            dve.reciprocal(erec[:, t2], esum[:, t2]).then_inc(g["ers"], 1)
            dve.wait_ge(g["ers"], b + 1)
            for t in (2 * b, 2 * b + 1):
                dve.tensor_scalar(prob[:, t], ex[:, t], erec[:, t:t + 1], None, ALU.mult).then_inc(g["prb"], 1)
            dve.wait_ge(g["prb"], 2 * b + 2)
            for t in (2 * b, 2 * b + 1):
                dve.max(top[:, t], prob[:, t]).then_inc(g["tps"], 1)
            dve.wait_ge(g["tps"], 2 * b + 2)
            for t in (2 * b, 2 * b + 1):
                dve.match_replace(rep[:, t], top[:, t], prob[:, t], -1.0).then_inc(g["reps"], 1)
            dve.wait_ge(g["reps"], 2 * b + 2)
            dve.scalar_tensor_tensor(out=wun[:, t2], in0=rep[:, t2], scalar=0.0, in1=prob[:, t2],
                                     op0=ALU.is_lt, op1=ALU.mult).then_inc(g["wus"], 1)
            dve.wait_ge(g["wus"], b + 1)
            dve.tensor_reduce(wsum[:, t2], wun[:, t2], AX.X, ALU.add).then_inc(g["wss"], 1)
            dve.wait_ge(g["wss"], b + 1)
            dve.reciprocal(wrec[:, t2], wsum[:, t2]).then_inc(g["wrs"], 1)
            dve.wait_ge(g["wrs"], b + 1)
            for t in (2 * b, 2 * b + 1):
                dve.tensor_scalar(wrt[:, t], wun[:, t], wrec[:, t:t + 1], None, ALU.mult).then_inc(g["wrts"], 1)

        def split_hi(dve, n, buf, part, i):
            dve.wait_ge(d_wst[buf], (i + 1) * (16 * WST_DMAS))
            dve.tensor_copy(gh[:, buf, part], wstage[:, buf, part]).then_inc(g["ghi"], 1)

        def dve_experts(dve):
            for part in range(3):
                split_hi(dve, 0, 0, part, 0)

            def period(i, last):
                for pg in range(PERIOD):
                    for c in range(CH):
                        n = (i * PERIOD + pg) * CH + c
                        j = (pg * CH + c) % 2
                        for h in range(2):
                            hs = slice(h * HALF, (h + 1) * HALF)
                            dve.wait_ge(g["up"], n * 2 + (h + 1))
                            dve.wait_ge(g["tmul"], n * 2 + (h + 1))
                            dve.tensor_tensor(hf[:, j, hs], ps[:, 2 + h, :], tg[:, j, hs], ALU.mult
                                              ).then_inc(g["hmul"], 1)
                        for h in range(2):
                            hs = slice(h * HALF, (h + 1) * HALF)
                            dve.wait_ge(g["hhi"], n * 2 + (h + 1))
                            dve.tensor_tensor(hl[:, j, hs], hf[:, j, hs], hh[:, j, hs].bitcast(F32), ALU.subtract
                                              ).then_inc(g["hlo"], 1)
                        if not (last and pg == PERIOD - 1):
                            if c == 0:
                                dve.wait_ge(g["down"], (i * PERIOD + pg) * CH + 1)
                            split_hi(dve, 0, 1 - pg, c, i if pg == 0 else i + 1)

            with dve.Fori(0, GROUPS // PERIOD - 1) as i:
                period(i, False)
            period(GROUPS // PERIOD - 1, True)

        @block.sync
        def _(sp):
            for b in range(NB):
                sp.dma_start(xs[:, 2 * b:2 * b + 2, :], x[b].rearrange("(t p) d -> p t d", p=P)).then_inc(d_x[b], 16)
            for i, w in enumerate((Wq, Wk, Wv, Wo)):
                sp.dma_start(wraw[:, i], w.rearrange("(t p) n -> p t n", p=P)).then_inc(d_w[i], 16)
            sp.dma_start(cw[:, :, :], ctx_2048.rearrange("e (a p) k -> p (e a) k", p=P)).then_inc(d_ctx, 16)
            sp.wait_ge(g["csb"], 1)
            for par_g in range(2):
                load_group(sp, par_g, par_g)
            for b in range(NB):
                sp.wait_ge(g["mng"], b + 1)
                for a in range(2):
                    for qt in range(2):
                        r0 = ROWS * a + MAXROW
                        c0 = b * S + qt * P
                        sp.dma_start(qst[r0:r0 + 1, :, c0:c0 + P].bitcast(F32),
                                     mneg[qt * NH + a:(qt + 1) * NH:2, b % 2, :].bitcast(F32)).then_inc(d_max[b], 16)
            sp.wait_ge(g["wte"], 2)
            sp.dma_start(routing_dram, wT_sb[:, :]).then_inc(d_rt, 16)
            sp.wait_ge(d_rt, 16)
            for par_g in range(2):
                load_routing(sp, par_g, par_g)
            with sp.Fori(0, GROUPS // PERIOD - 1) as i:
                for pg in range(PERIOD):
                    done = i * PERIOD + (pg + 1)
                    sp.wait_ge(g["ghi"], done * 3)
                    sp.wait_ge(g["glo"], done * 3)
                    load_group(sp, (i + 1) * PERIOD + pg, pg)
                    sp.wait_ge(g["tmul"], done * (2 * CH))
                    load_routing(sp, (i + 1) * PERIOD + pg, pg)
            for b in range(NB):
                sp.wait_ge(g["fin"], b + 1)
                sp.dma_start(out[b].rearrange("(t p) d -> p t d", p=P), xs[:, 2 * b:2 * b + 2, :]).then_inc(d_out, 16)
            sp.wait_ge(d_out, 16 * NB)

        @block.gpsimd
        def _(pool):
            pool.memset(zeros_bf[:, :], 0.0).then_inc(g["yzero"], 1)
            pool.memset(vs[:, :, :, DH:VW], 1.0).then_inc(g["yzero"], 1)
            pool.wait_ge(d_const, 16)
            rsqrt(pool, 0, 0)
            for b in range(NB):
                if b + 1 < NB:
                    rsqrt(pool, 0, b + 1)
                pool.wait_ge(g["zh"], b + 1)
                pool.tensor_tensor(ztl[:, :, bs(b)], zf[:, b % 2], zth[:, :, bs(b)].bitcast(F32), ALU.subtract
                                   ).then_inc(g["zl"], 1)
            for i in (2, 3):
                pool.wait_ge(g["whi"], i + 1)
                pool.tensor_tensor(wl[:, i], wraw[:, i], wh[:, i].bitcast(F32), ALU.subtract).then_inc(g["wlo"], 1)
            pool.wait_ge(d_bias, 32)
            pool.wait_ge(ln_zn[0], NT)
            for t in range(NT):
                pool.tensor_tensor(xs[:, t], xs[:, t], bob[:, :], ALU.add).then_inc(g["bias_x"], 1)
            pool.wait_ge(g["cab"], 1)
            pool.partition_all_reduce(wam[:, 1, :], wam[:, 0, :], P, bass.bass_isa.ReduceOp.max).then_inc(g["car"], 1)
            cw4 = cw[:, :, :].rearrange("p a (k c) -> p (a k) c", c=P)
            cm4 = cm[:, :, :].rearrange("p a (k c) -> p (a k) c", c=P)
            pool.wait_ge(g["csc"], 1)
            pool.tensor_tensor(cw4, cw4, wam[:, 4, :].unsqueeze(2).to_broadcast([P, 16, P]), ALU.mult
                               ).then_inc(g["cs1"], 1)
            pool.wait_ge(g["cs3"], 1)
            pool.wait_ge(g["cs1"], 1)
            pool.tensor_tensor(cw4, cw4, cm4, ALU.add).then_inc(g["cs4"], 1)
            pool.wait_ge(g["cs4"], 1)
            pool.tensor_tensor(cq[:, :, :].rearrange("p a (k c) -> p (a k) c", c=P), cw4, cm4, ALU.subtract
                               ).then_inc(g["csb"], 1)
            for step in range(STEPS):
                for name, ln in (("W", 1), ("X", 2)):
                    b = rows_of(step, name)
                    if b is not None:
                        rsqrt(pool, ln, b)
            pool_experts(pool)

        @block.scalar
        def _(act):
            act.dma_start(cst[:, :], consts).then_inc(d_const, 16)
            for i, v in enumerate((ln_g, ln_b, bq, bk)):
                act.dma_start(prow[2 * i:2 * i + 2, :], v.rearrange("(t p) -> t p", p=P)).then_inc(d_par, 16)
            for dst, v in ((bvb, bv), (bob, bo)):
                act.dma_start(dst[:, :], v.rearrange("(a n) -> a n", a=1).partition_broadcast(P)).then_inc(d_bias, 16)
            act.dma_start(rw_sb[:, :], router_w).then_inc(d_rw, 16)
            act.wait_ge(g["rtp"], 1)
            act.activation(par[:, :], ps[:, M1, KT * NE:KT * NE + 8], ACT.Copy).then_inc(g["rwt"], 1)
            act.activation(rwt[:, :, :], ps[:, M1, 0:KT * NE].rearrange("p (k e) -> p k e", k=KT), ACT.Copy
                           ).then_inc(g["rwt"], 1)
            for i in range(4):
                act.wait_ge(d_w[i], 16)
                act.activation(wh[:, i], wraw[:, i], ACT.Copy).then_inc(g["whi"], 1)
            for b in range(NB):
                act.wait_ge(g["zff"], 2 * b + 2)
                act.activation(zth[:, :, bs(b)], zf[:, b % 2], ACT.Copy).then_inc(g["zh"], 1)
            act.wait_ge(g["rwt"], 1)
            for u in range(8):
                which, mt = u % 4 // 2, u % 2
                act.wait_ge(g["pj"], u + 1)
                if u >= 2:
                    act.wait_ge(g["pll"], u - 1)
                act.activation(pf[:, u % 2], ps[:, u % 2, :], ACT.Identity,
                               bias=par[:, 4 + 2 * which + mt:5 + 2 * which + mt]).then_inc(g["pff"], 1)
                if u >= 1:
                    stack_evac(act, u - 1, 0)
            stack_evac(act, 7, 0)
            for e in range(NB):
                act.wait_ge(g["ctp"], e + 1)
                act.activation(cqt[:, e].rearrange("p k n -> p (k n)"), bf16_bank(M0), ACT.Copy
                               ).then_inc(g["cev"], 1)
            for step in range(STEPS):
                if step % 8 == 0 and 1 <= step // 8 <= NB:
                    b = step // 8 - 1
                    act.wait_ge(g["mtp"], b + 1)
                    if b >= 2:
                        act.wait_ge(d_max[b - 2], 64)
                    act.activation(mneg[:, b % 2, :], ps[0:2 * NH, M1, 0:P], ACT.Copy, scale=-1.0
                                   ).then_inc(g["mng"], 1)
                m = step - LAG
                if 0 <= m < NB * NPAIR:
                    act.wait_ge(g["t_ready"], m + 1)
                    if m >= 2:
                        act.wait_ge(g["av_ready"], m - 1)
                    act.activation(pt[:, m % 2], TB[:, :, P:512], ACT.Exp, scale=DH ** -0.5).then_inc(g["e_ready"], 1)
                b = rows_of(step, "A")
                if b is not None:
                    act.wait_ge(g["atp"], b + 1)
                    act.activation(zth[:, :, bs(b)], ps[:, M0, :].rearrange("p (k s) -> p k s", k=KT), ACT.Copy
                                   ).then_inc(g["ah"], 1)
                b = rows_of(step, "Q")
                if b is not None:
                    act.wait_ge(g["qtp"], b + 1)
                    act.activation(xqt[:, b % 2].rearrange("p k s -> p (k s)"), bf16_bank(M0), ACT.Copy
                                   ).then_inc(g["qev"], 1)
                b = rows_of(step, "Y")
                if b is not None:
                    act.wait_ge(g["ytp"], b + 1)
                    act.activation(zth[:, :, bs(b)], ps[:, M0, :].rearrange("p (k s) -> p k s", k=KT), ACT.Copy
                                   ).then_inc(g["yh"], 1)
                b = rows_of(step, "R")
                if b is not None:
                    act.wait_ge(g["lmxs"], b + 1)
                    for t in range(2):
                        act.activation(ex[:, 2 * b + t], ps[:, M1, t * NE:(t + 1) * NE], ACT.Exp,
                                       bias=lmx[:, 2 * b + t:2 * b + t + 1],
                                       accum_out=esum[:, 2 * b + t:2 * b + t + 1]).then_inc(g["exs"], 1)
            for h in range(2):
                act.wait_ge(g["wtp"], h + 1)
                act.activation(wT_sb[:, h * HALF:(h + 1) * HALF], ps[0:NE, M0 + h, :], ACT.Copy).then_inc(g["wte"], 1)
            act_experts(act)
            for k in range(KT):
                for h in range(2):
                    if k + h == 0:
                        act.wait_ge(g["down"], GROUPS * CH + 1)
                    act.activation(yt[:, k, h * HALF:(h + 1) * HALF], ps[:, 4 + 2 * k + h, :], ACT.Copy
                                   ).then_inc(g["yev"], 1)

        @block.tensor
        def _(pe):
            last_read = {}

            def take(bank, reader, count):
                if bank in last_read:
                    pe.wait_ge(*last_read[bank])
                last_read[bank] = (g[reader], count)

            def f32_product(dst, lh, ll, rh, rl, first, last, check=False):
                n = len(lh)
                for k in range(n):
                    for j, (a, b) in enumerate(((lh[k], rh[k]), (lh[k], rl[k]), (ll[k], rh[k]))):
                        mm = pe.matmul(dst, a, b, start=first and k == 0 and j == 0,
                                       stop=last and k == n - 1 and j == 2, skip_group_check=True)
                return mm

            pe.wait_ge(d_const, 16)
            pe.wait_ge(d_rw, 16)
            take(M1, "rwt", 2)
            for k in range(KT):
                pe.transpose(ps[:, M1, k * NE:(k + 1) * NE], rw_sb[:, k * P:(k + 1) * P], ident[0:NE, 0:NE])
            pe.wait_ge(d_par, 64)
            pe.transpose(ps[:, M1, KT * NE:KT * NE + 8], prow[:, :], ident[0:8, 0:8]).then_inc(g["rtp"], 1)
            for b in range(NB):
                if b >= 2:
                    pe.wait_ge(g["zff"], 2 * (b - 1))
                for t in range(2):
                    pe.wait_ge(ln_zn[0], 2 * b + t + 1)
                    for k in range(KT):
                        mm = pe.transpose(OB[:, b % 2, k * S + t * P:k * S + (t + 1) * P],
                                          zs[:, 2 * b + t, k * P:(k + 1) * P], ident)
                mm.then_inc(g["ztp"], 1)

            def project(u):
                half, which, mt = u // 4, u % 4 // 2, u % 2
                if u % 4 == 0:
                    pe.wait_ge(g["zl"], 2 * half + 2)
                    pe.wait_ge(g["zh"], 2 * half + 2)
                if u < 4 and mt == 0:
                    pe.wait_ge(g["whi"], which + 1)
                    pe.wait_ge(cvt, which + 1)
                if u >= 2:
                    pe.wait_ge(g["pff"], u - 1)
                ks = range(KT)
                hs = slice(half * HALF, (half + 1) * HALF)
                ms = slice(mt * P, (mt + 1) * P)
                f32_product(ps[:, u % 2, :], [wh[:, which, k, ms] for k in ks], [wl[:, which, k, ms] for k in ks],
                            [zth[:, k, hs] for k in ks], [ztl[:, k, hs] for k in ks], True, True
                            ).then_inc(g["pj"], 1)

            def stack(u):
                which = u % 4 // 2
                if u == 0:
                    pe.wait_ge(cvt, 9)
                    pe.wait_ge(g["zff"], 2 * NB)
                pe.wait_ge(g["pll"], u + 1)
                for lp in range(4):
                    k = 4 * u + lp
                    if k >= 4:
                        pe.wait_ge(g["rev" if lp % 2 == 0 else "rev2"], 2 * (u - 1) + lp // 2 + 1)
                    rs = slice(32 * lp, 32 * lp + 32)
                    pe.matmul(ps[:, 2 + k % 4, :], R[rs, 2 * which], ph[rs, u % 2], start=True, stop=False)
                    pe.matmul(ps[:, 2 + k % 4, :], R[rs, 2 * which + 1], pl[rs, u % 2], start=False, stop=True
                              ).then_inc(g["rp"], 1)

            def values(t):
                take(M0 + t % 2, "vev", t + 1)
                if t == 0:
                    pe.wait_ge(g["whi"], 3)
                    pe.wait_ge(g["wlo"], 1)
                ks = range(KT)
                ts = slice(t * P, (t + 1) * P)
                f32_product(ps[:, M0 + t % 2, 0:D], [zth[:, k, ts] for k in ks], [ztl[:, k, ts] for k in ks],
                            [wh[:, 2, k] for k in ks], [wl[:, 2, k] for k in ks], True, True
                            ).then_inc(g["vpj"], 1)

            project(0)
            for u in range(8):
                if u < 7:
                    project(u + 1)
                values(u)
                stack(u)
            pe.wait_ge(g["csb"], 1)
            for e in range(NB):
                take(M0, "cev", e + 1)
                for kb in range(KT):
                    for nb in range(2):
                        mm = pe.transpose(bf16_bank(M0)[:, kb * D + nb * P:kb * D + (nb + 1) * P],
                                          cq[:, 2 * e + nb, kb * P:(kb + 1) * P], ident_bf[:, :])
                mm.then_inc(g["ctp"], 1)

            def scores(n):
                b, hp = n // NPAIR, n % NPAIR
                if n == 0:
                    pe.wait_ge(g["rev"], 16)
                    pe.wait_ge(g["rev2"], 16)
                else:
                    pe.wait_ge(g["s_max"], 2 * n)
                for a in range(2):
                    rs = slice(ROWS * a, ROWS * (a + 1))
                    for qt in range(2):
                        c0 = b * S + qt * P
                        pe.matmul(SB[:, a, qt * S:(qt + 1) * S], qst[rs, hp, c0:c0 + P], kst[rs, hp, bs(b)],
                                  start=(qt == 0), stop=False, skip_group_check=True)
                for a in range(2):
                    blocks = SB[:, a, :].rearrange("p (n c) -> p n c", c=P)[:, 0:4:3, :]
                    mm = pe.matmul(blocks, ident_bf[:, :], mask_s[:, :, :], start=False, stop=True,
                                   skip_group_check=True)
                mm.then_inc(g["s_ready"], 1)

            def scores_t(m):
                b, hp = m // NPAIR, m % NPAIR
                if hp == 0:
                    pe.wait_ge(d_max[b], 64)
                if m:
                    pe.wait_ge(g["e_ready"], m)
                for a in range(2):
                    rs = slice(ROWS * a, ROWS * (a + 1))
                    for half in range(2):
                        c0 = b * S + (1 - half) * P
                        pe.matmul(TB[:, a, half * S:(half + 1) * S], kst[rs, hp, c0:c0 + P], qst[rs, hp, bs(b)],
                                  start=(half == 0), stop=False, skip_group_check=True)
                for a in range(2):
                    mm = pe.matmul(TB[:, a, P:P + 2 * P], ident_bf[:, :],
                                   mask_t[:, :, :].rearrange("p n c -> p (n c)"), start=False, stop=True,
                                   skip_group_check=True)
                mm.then_inc(g["t_ready"], 1)

            def attend(m):
                b, hp = m // NPAIR, m % NPAIR
                pe.wait_ge(g["e_ready"], m + 1)
                if hp == 0 and b:
                    pe.wait_ge(g["avt_n"], 2 * b)
                if m == 0:
                    pe.wait_ge(g["vev"], NT)
                for a in range(2):
                    h = 2 * hp + a
                    for qt, kt, blk in ((0, 0, 1), (1, 0, 2), (1, 1, 0)):
                        mm = pe.matmul(OB[:, qt, h * VW:(h + 1) * VW], pt[:, m % 2, a, blk * P:(blk + 1) * P],
                                       vs[:, 2 * b + kt, h, :], start=(h == 0 and kt == 0),
                                       stop=True, skip_group_check=True)
                mm.then_inc(g["av_ready"], 1)

            for step in range(STEPS):
                if step % 8 == 0 and 1 <= step // 8 <= NB:
                    b = step // 8 - 1
                    take(M1, "mng", b + 1)
                    pe.wait_ge(g["s_max"], 2 * NPAIR * (b + 1))
                    pe.transpose(ps[0:2 * NH, M1, 0:P], mx[:, b].rearrange("p q h -> p (q h)"), ident
                                 ).then_inc(g["mtp"], 1)
                if step < NB * NPAIR:
                    scores(step)
                if 0 <= step - LAG < NB * NPAIR:
                    scores_t(step - LAG)
                if 0 <= step - LAG - 1 < NB * NPAIR:
                    attend(step - LAG - 1)
                b = rows_of(step, "A")
                if b is not None:
                    take(M0, "al", b + 1)
                    pe.wait_ge(g["avt_n"], 2 * b + 2)
                    for t in range(2):
                        for k in range(KT):
                            mm = pe.transpose(ps[:, M0, k * S + t * P:k * S + (t + 1) * P],
                                              avn[:, 2 * b + t, k * P:(k + 1) * P], ident)
                    mm.then_inc(g["atp"], 1)
                b = rows_of(step, "W")
                if b is not None:
                    take(M1, "x1", b + 1)
                    if b == 0:
                        pe.wait_ge(g["whi"], 4)
                        pe.wait_ge(g["wlo"], 2)
                    pe.wait_ge(g["ah"], b + 1)
                    pe.wait_ge(g["al"], b + 1)
                    ks = range(KT)
                    for t in range(2):
                        ts = slice((2 * b + t) * P, (2 * b + t + 1) * P)
                        mm = f32_product(ps[:, M1, t * D:(t + 1) * D], [zth[:, k, ts] for k in ks],
                                         [ztl[:, k, ts] for k in ks], [wh[:, 3, k] for k in ks],
                                         [wl[:, 3, k] for k in ks], t == 0, True)
                    mm.then_inc(g["wo"], 1)
                b = rows_of(step, "Q")
                if b is not None:
                    take(M0, "qev", b + 1)
                    pe.wait_ge(g["qsb"], b + 1)
                    for t in range(2):
                        for k in range(KT):
                            mm = pe.transpose(bf16_bank(M0)[:, k * S + t * P:k * S + (t + 1) * P],
                                              xqb[:, b % 2, 2 * t + k], ident_bf[:, :])
                    mm.then_inc(g["qtp"], 1)
                b = rows_of(step, "X")
                if b is not None:
                    pe.wait_ge(g["qev"], b + 1)
                    if b == 0:
                        pe.wait_ge(g["cev"], NB)
                    for t in range(2):
                        take(M0 + t, "x2", 8 * b + 6 + 2 * t)
                        for k in range(KT):
                            mm = pe.matmul(ps[:, M0 + t, k * D:(k + 1) * D], xqt[:, b % 2, k, t * P:(t + 1) * P],
                                           cqt[:, b, k], start=(k == 0), stop=True, skip_group_check=True)
                        mm.then_inc(g["xmm"], 1)
                b = rows_of(step, "Y")
                if b is not None:
                    take(M0, "yl", b + 1)
                    pe.wait_ge(ln_zn[2], 2 * b + 2)
                    for t in range(2):
                        for k in range(KT):
                            mm = pe.transpose(ps[:, M0, k * S + t * P:k * S + (t + 1) * P],
                                              zs[:, 2 * b + t, k * P:(k + 1) * P], ident)
                    mm.then_inc(g["ytp"], 1)
                b = rows_of(step, "R")
                if b is not None:
                    take(M1, "exs", 2 * b + 2)
                    pe.wait_ge(g["yh"], b + 1)
                    pe.wait_ge(g["yl"], b + 1)
                    for t in range(2):
                        ts = slice((2 * b + t) * P, (2 * b + t + 1) * P)
                        for j, z in enumerate((zth, ztl)):
                            for k in range(KT):
                                mm = pe.matmul(ps[:, M1, t * NE:(t + 1) * NE], z[:, k, ts].bitcast(F32), rwt[:, k],
                                               start=(t == 0 and j == 0 and k == 0), stop=True,
                                               skip_group_check=True)
                    mm.then_inc(g["lg"], 1)
            for h in range(2):
                take(M0 + h, "wte", h + 1)
                pe.wait_ge(g["wrts"], 4 * (h + 1))
                for t in range(4):
                    mm = pe.transpose(ps[0:NE, M0 + h, t * P:(t + 1) * P], wrt[:, 4 * h + t, :], ident)
                mm.then_inc(g["wtp"], 1)
            pe_experts(pe, f32_product)
            for b in range(NB):
                pe.wait_ge(g["yev"], 4)
                for t in range(2):
                    for k in range(KT):
                        mm = pe.transpose(ps[:, b, t * D + k * P:t * D + (k + 1) * P],
                                          yt[:, k, (2 * b + t) * P:(2 * b + t + 1) * P], ident)
                mm.then_inc(g["ftp"], 1)

        @block.vector
        def _(dve):
            dve.wait_ge(d_const, 16)

            def stats_of(ln, b):
                for t in (2 * b, 2 * b + 1):
                    dve.bn_stats(stats[:, ln, t], xs[:, t]).then_inc(ln_bn[ln], 1)
                dve.wait_ge(ln_bn[ln], 2 * b + 2)
                for t in (2 * b, 2 * b + 1):
                    dve.bn_aggr(mv[:, ln, t], stats[:, ln, t]).then_inc(ln_ag[ln], 1)
                dve.wait_ge(ln_ag[ln], 2 * b + 2)
                m, a = (1.0 + EPS, EPS * EPS) if ln == 0 else (1.0, EPS)
                dve.tensor_scalar(rs_in[:, ln, 2 * b:2 * b + 2], mv[:, ln, 2 * b:2 * b + 2, 1], m, a,
                                  ALU.mult, ALU.add).then_inc(ln_ri[ln], 1)

            def normalise(ln, b):
                dve.wait_ge(ln_rs[ln], b + 1)
                for t in (2 * b, 2 * b + 1):
                    dve.tensor_scalar(zs[:, t], xs[:, t], mv[:, ln, t, 0:1], rstd[:, ln, t:t + 1],
                                      ALU.subtract, ALU.mult).then_inc(ln_zn[ln], 1)

            dve.wait_ge(d_x[0], 16)
            stats_of(0, 0)
            for i in (0, 1):
                dve.wait_ge(g["whi"], i + 1)
                dve.tensor_tensor(wl[:, i], wraw[:, i], wh[:, i].bitcast(F32), ALU.subtract).then_inc(cvt, 1)
            normalise(0, 0)
            for i in range(4):
                dve.tensor_copy(R[:, i], cst[:, (C_QH + i) * P:(C_QH + i + 1) * P]).then_inc(cvt, 1)
            dve.tensor_copy(ident_bf[:, :], ident).then_inc(cvt, 1)
            for dst, i in ((mask_s, C_MS), (mask_t, C_MT)):
                dve.tensor_copy(dst[:, :, :], cst[:, i * P:(i + 1) * P].unsqueeze(1).to_broadcast([P, 2, P])
                                ).then_inc(cvt, 1)
            dve.wait_ge(g["rwt"], 1)

            def scaled(b):
                dve.wait_ge(g["ztp"], b + 1)
                if b >= 2:
                    dve.wait_ge(g["zl"], b - 1)
                for k in range(KT):
                    dve.tensor_scalar(zf[:, b % 2, k], OB[:, b % 2, k * S:(k + 1) * S], par[:, k:k + 1],
                                      par[:, 2 + k:3 + k], ALU.mult, ALU.add).then_inc(g["zff"], 1)

            for b in range(1, NB):
                dve.wait_ge(d_x[b], 16)
                stats_of(0, b)
                scaled(b - 1)
                normalise(0, b)
            scaled(NB - 1)
            dve.wait_ge(d_ctx, 16)
            cw4 = cw[:, :, :].rearrange("p a (k c) -> p (a k) c", c=P)
            dve.tensor_reduce(wam[:, 0, :], cw4, AX.X, ALU.max, apply_absolute_value=True).then_inc(g["cab"], 1)
            dve.wait_ge(d_bias, 32)

            def values_out(t):
                dve.wait_ge(g["vpj"], t + 1)
                if t == 0:
                    dve.wait_ge(g["yzero"], 2)
                dve.tensor_tensor(vs[:, t, :, 0:DH], ps[:, M0 + t % 2, 0:D].rearrange("p (h d) -> p h d", h=NH),
                                  bvb[:, :].rearrange("p (h d) -> p h d", h=NH), ALU.add
                                  ).then_inc(g["vev"], 1)

            for u in range(8):
                dve.wait_ge(g["pff"], u + 1)
                if u >= 2:
                    dve.wait_ge(g["rp"], 4 * (u - 1))
                dve.tensor_copy(ph[:, u % 2], pf[:, u % 2]).then_inc(g["phh"], 1)
                dve.wait_ge(g["phh"], u + 1)
                dve.tensor_tensor(pl[:, u % 2], pf[:, u % 2], ph[:, u % 2].bitcast(F32), ALU.subtract
                                  ).then_inc(g["pll"], 1)
                values_out(u)
                stack_evac(dve, u, 1)
                if u == 4:
                    quant_scales(dve, wam, W_FLOOR, "car", "csf", "csc", 1)
                if u == 6:
                    dve.wait_ge(g["cs1"], 1)
                    round_step(dve, cw[:, :, :], cm[:, :, :], "cs2", "cs3", 1)
            for step in range(STEPS):
                if step < NB * NPAIR:
                    n = step
                    b, hp = n // NPAIR, n % NPAIR
                    dve.wait_ge(g["s_ready"], n + 1)
                    dve.tensor_reduce(mx[:, b, 0, 2 * hp:2 * hp + 2], SB[:, :, 0:P], AX.X, ALU.max
                                      ).then_inc(g["s_max"], 1)
                    dve.tensor_reduce(mx[:, b, 1, 2 * hp:2 * hp + 2], SB[:, :, S:2 * S], AX.X, ALU.max
                                      ).then_inc(g["s_max"], 1)
                b = rows_of(step, "N")
                if b is not None:
                    dve.wait_ge(g["av_ready"], NPAIR * (b + 1))
                    o4 = OB[:, :, 0:NH * VW].rearrange("p q (h w) -> p q h w", w=VW)
                    dve.reciprocal(rinv[:, b], o4[:, :, :, DH]).then_inc(g["rin"], 1)
                    dve.wait_ge(g["rin"], b + 1)
                    for q in range(2):
                        dve.tensor_tensor(avn[:, 2 * b + q, :].rearrange("p (h d) -> p h d", h=NH),
                                          o4[:, q, :, 0:DH],
                                          rinv[:, b, q].unsqueeze(2).to_broadcast([P, NH, DH]), ALU.mult
                                          ).then_inc(g["avt_n"], 1)
                b = rows_of(step, "A")
                if b is not None:
                    dve.wait_ge(g["ah"], b + 1)
                    dve.tensor_tensor(ztl[:, :, bs(b)], ps[:, M0, :].rearrange("p (k s) -> p k s", k=KT),
                                      zth[:, :, bs(b)].bitcast(F32), ALU.subtract).then_inc(g["al"], 1)
                b = rows_of(step, "W")
                if b is not None:
                    dve.wait_ge(g["wo"], b + 1)
                    if b == 0:
                        dve.wait_ge(g["bias_x"], NT)
                        dve.wait_ge(g["wlo"], 2)
                    dve.tensor_tensor(xs[:, 2 * b:2 * b + 2, :], ps[:, M1, :].rearrange("p (t d) -> p t d", t=2),
                                      xs[:, 2 * b:2 * b + 2, :], ALU.add).then_inc(g["x1"], 1)
                    dve.wait_ge(g["x1"], b + 1)
                    stats_of(1, b)
                    normalise(1, b)
                    dve.wait_ge(ln_zn[1], 2 * b + 2)
                    z4 = zs[:, 2 * b:2 * b + 2, :].rearrange("p t (k c) -> p (t k) c", c=P)
                    xa = xam[:, b]
                    dve.tensor_reduce(xa[:, 0, :], z4, AX.X, ALU.max, apply_absolute_value=True).then_inc(g["qam"], 1)
                    quant_scales(dve, xa, ACT_FLOOR, "qam", "qsf", "qsc", b + 1)
                    o = b % 2
                    dve.tensor_tensor(xq1[:, o], z4, xa[:, 4, :].unsqueeze(2).to_broadcast([P, 4, P]), ALU.mult
                                      ).then_inc(g["qs1"], 1)
                    dve.wait_ge(g["qs1"], b + 1)
                    round_step(dve, xq1[:, o], xq2[:, o], "qs2", "qs3", b + 1)
                    dve.wait_ge(g["qs3"], b + 1)
                    dve.tensor_tensor(xq3[:, o], xq1[:, o], xq2[:, o], ALU.add).then_inc(g["qs4"], 1)
                    for kb in range(KT):
                        dve.tensor_tensor(
                            xsc[:, b].rearrange("p (t k) n -> p t k n", k=KT)[:, :, kb, :],
                            xa[:, 3, :].rearrange("p (t k) -> p t k", k=KT)[:, :, kb:kb + 1].to_broadcast([P, 2, 2]),
                            wam[:, 3, 4 * b + kb:4 * b + kb + 3:2].unsqueeze(1).to_broadcast([P, 2, 2]),
                            ALU.mult).then_inc(g["xscs"], 1)
                    dve.wait_ge(g["qs4"], b + 1)
                    dve.tensor_tensor(xqb[:, o], xq3[:, o], xq2[:, o], ALU.subtract).then_inc(g["qsb"], 1)
                b = rows_of(step, "X")
                if b is not None:
                    dve.wait_ge(g["xscs"], 2 * b + 2)
                    for kb in range(KT):
                        if kb:
                            dve.wait_ge(g["x2"], 8 * b + 4)
                        for t in range(2):
                            if kb == 0:
                                dve.wait_ge(g["xmm"], 2 * b + t + 1)
                            for nb in range(2):
                                xo = xs[:, 2 * b + t, nb * P:(nb + 1) * P]
                                ins = dve.scalar_tensor_tensor(
                                    out=xo, in0=ps[:, M0 + t, kb * D + nb * P:kb * D + (nb + 1) * P],
                                    scalar=xsc[:, b, 2 * t + kb, nb:nb + 1], in1=xo, op0=ALU.mult, op1=ALU.add)
                                ins.then_inc(g["x2"], 1)
                    dve.wait_ge(g["x2"], 8 * b + 8)
                    stats_of(2, b)
                    normalise(2, b)
                b = rows_of(step, "Y")
                if b is not None:
                    dve.wait_ge(g["yh"], b + 1)
                    dve.tensor_tensor(ztl[:, :, bs(b)], ps[:, M0, :].rearrange("p (k s) -> p k s", k=KT),
                                      zth[:, :, bs(b)].bitcast(F32), ALU.subtract).then_inc(g["yl"], 1)
                b = rows_of(step, "R")
                if b is not None:
                    route(dve, b)
            dve_experts(dve)
            for b in range(NB):
                dve.wait_ge(g["ftp"], b + 1)
                dve.tensor_tensor(xs[:, 2 * b:2 * b + 2, :], ps[:, b, :].rearrange("p (t d) -> p t d", t=2),
                                  xs[:, 2 * b:2 * b + 2, :], ALU.add).then_inc(g["fin"], 1)


def kernel(**inputs):
    import numpy as _np
    import concourse.bacc as _bacc
    from concourse import mybir as _mybir
    from concourse.bass_utils import run_bass_kernel_spmd as _run

    nc = _bacc.Bacc("TRN2", target_bir_lowering=False, num_devices=1)
    names = ["x", "ctx_2048"] + ["L0_attn_" + n for n in
                                 ("ln_g", "ln_b", "Wq", "bq", "Wk", "bk", "Wv", "bv", "Wo", "bo")]
    names += ["L0_ffn_" + n for n in ("router_w", "w_gate", "w_up", "w_down")]
    arrays = {"in_consts": host_constants()}
    args = [nc.dram_tensor("in_consts", arrays["in_consts"].shape, _mybir.dt.float32, kind="ExternalInput").ap()]
    for name in names:
        a = _np.ascontiguousarray(inputs[name])
        arrays["in_" + name] = a
        args.append(nc.dram_tensor("in_" + name, a.shape, _mybir.dt.from_np(a.dtype), kind="ExternalInput").ap())
    args.append(nc.dram_tensor("out_x", (NB, S, D), _mybir.dt.float32, kind="ExternalOutput").ap())
    decoder_layer(nc, *args)
    r = _run(nc, [arrays], core_ids=[0])
    return r.results[0]["out_x"]
```

```python
from contextlib import ExitStack

import concourse.bass as bass
from concourse import mybir

F32 = mybir.dt.float32
F32R = mybir.dt.float32r
BF16 = mybir.dt.bfloat16
F16 = mybir.dt.float16
U32 = mybir.dt.uint32
ALU = mybir.AluOpType
ACT = mybir.ActivationFunctionType
AX = mybir.AxisListType

P = 128
NB, S, D = 4, 256, 256
T = NB * S
NT = T // P
KT = D // P
HALF = T // 2
NH, DH = 16, 16
NPAIR = NH // 2
ROWS = 64
MAXROW = 3 * DH
VW = DH + 1
EPS = 1e-5
FP8_MAX, ACT_FLOOR, W_FLOOR = 448.0, 1e-4, 1e-6
NE, TOPK, NI = 32, 8, 96
GE = 4
GROUPS = NE // GE
GW = GE * NI
CH = GW // P
PERIOD = 2
NEG = -1e30
C_ID, C_QH, C_QL, C_KH, C_KL, C_MS, C_MT, C_ONE = range(8)
LAG = 11
AV_LAG = 3
UNITS = {4: (0, 1, 1, 2), 5: (3, 4, 4, 4), 6: (7, 8, 9, 6), 7: (10, 11, 12, 9)}
PROJECT, STACK0, STACK1, VALUES = range(4)
CTX_T = 14
BIAS_X = 7
AT = {"divide": 0, "transpose": 1, "low": 2, "project": 2, "residual": 3, "deviation1": 3, "LN2": 4,
      "scales": 5, "round": 6, "turn": 8, "context": 9, "residual2": 9, "stats3": 10, "deviation2": 10, "LN3": 12, "transpose3": 12, "low3": 13,
      "logits": 13, "softmax": 14, "top": 15, "weights": 16}
STEPS = 8 * (NB - 1) + LAG + AV_LAG + 7 + AT["weights"] + 1


def host_constants():
    import numpy as np

    c = np.zeros((P, C_ONE * P + 6), np.float32)
    blk = [c[:, i * P:(i + 1) * P] for i in range(C_ONE)]
    blk[C_ID][:] = np.eye(P)
    r = np.arange(P)[:, None] % 32
    col = np.arange(P)[None, :]
    same = (col // ROWS == r // DH) & (col % DH == r % DH)
    copy = col % ROWS // DH
    blk[C_QH][:] = same & ((copy == 0) | (copy == 1))
    blk[C_QL][:] = same & (copy == 2)
    blk[C_KH][:] = same & ((copy == 0) | (copy == 2))
    blk[C_KL][:] = same & (copy == 1)
    q = np.arange(P)[:, None]
    k = np.arange(P)[None, :]
    blk[C_MS][:] = np.where(k <= q, 0.0, NEG)
    blk[C_MT][:] = np.where(q <= k, 0.0, NEG)
    c[:, C_ONE * P] = np.arange(P) % ROWS // 2 * 2 == MAXROW
    c[:, C_ONE * P + 1] = -0.5
    c[:, C_ONE * P + 2:] = np.arange(P)[:, None] // 32 == np.arange(4)
    return c


def decoder_layer(nc, consts, x, ctx_2048, ln_g, ln_b, Wq, bq, Wk, bk, Wv, bv, Wo, bo,
                  router_w, w_gate, w_up, w_down, out):
    routing_dram = nc.dram_tensor("routing_t", [NE, T], F32).ap()

    base = nc.sbuf_base
    cursor = [base]
    address = {}

    def sb(name, shape, dt, over=None):
        size = {BF16: 2, F16: 2}.get(dt, 4)
        for s in shape[1:]:
            size *= s
        at = (cursor[0] + 31) // 32 * 32 if over is None else over
        cursor[0] = at + size if over is None else cursor[0]
        address[name] = at
        return nc.alloc_sbuf_tensor_at(name, shape, dt, offset=at)

    cst = sb("cst", [P, C_ONE * P + 6], F32)
    R = sb("R", [P, 4, 4, P], F32R)
    ident_bf = sb("ident_bf", [P, P], BF16)
    mask_s = sb("mask_s", [P, 2, P], BF16)
    mask_t = sb("mask_t", [P, 2, P], BF16)
    zeros_bf = sb("zeros_bf", [P, HALF], BF16)
    xs = sb("xs", [P, NT, D], F32)
    zth = sb("zth", [P, KT, T], F32R)
    ztl = sb("ztl", [P, KT, T], F32R)
    prow = sb("prow", [8, P], F32)
    par = sb("par", [P, 8], F32)
    bvb = sb("bvb", [P, D], F32)
    bob = sb("bob", [P, D], F32)
    mx = sb("mx", [P, NB, 2, NH], F32)
    mneg = sb("mneg", [NH, 2, S], F32R)
    stats = sb("stats", [P, 3, NT, 6], F32)
    mv = sb("mv", [P, 3, NT, 2], F32)
    rs_in = sb("rs_in", [P, 3, NT], F32)
    rstd = sb("rstd", [P, 3, NT], F32)
    rinv = sb("rinv", [P, NB, 2, NH], F32)
    cst_half = cst[:, C_ONE * P + 1:C_ONE * P + 2]
    cq = sb("cq", [P, 2 * NB, D], BF16)
    cqt = sb("cqt", [P, NB, KT, D], BF16)
    wam = sb("wam", [P, 6, 16], F32)
    xam = sb("xam", [P, NB, 5, 4], F32)
    xsc = sb("xsc", [P, NB, 4, 2], F32)
    xqb = sb("xqb", [P, 2, 4, P], BF16)
    xqt = sb("xqt", [P, 2, KT, S], BF16)
    rw_sb = sb("rw_sb", [NE, D], F32)
    rwt = sb("rwt", [P, KT, NE], F32)
    lmx = sb("lmx", [P, NT], F32)
    esum = sb("esum", [P, NT], F32)
    erec = sb("erec", [P, NT], F32)
    ex = sb("ex", [P, NT, NE], F32)
    prob = sb("prob", [P, NT, NE], F32)
    top = sb("top", [P, NT, 8], F32)
    rep = sb("rep", [P, NT, NE], F32)
    wun = sb("wun", [P, NT, NE], F32)
    wsum = sb("wsum", [P, NT], F32)
    wrec = sb("wrec", [P, NT], F32)
    wrt = sb("wrt", [P, NT, NE], F32)
    shared = cursor[0]
    zs = sb("zs", [P, NT, D], F32)
    zf = sb("zf", [P, 2, KT, S], F32)
    pf = sb("pf", [P, 2, HALF], F32)
    ph = sb("ph", [P, 2, HALF], F32R)
    pl = sb("pl", [P, 2, HALF], F32R)
    wraw = sb("wraw", [P, 4, KT, D], F32)
    wstage = sb("wstage", [P, 2, 3, 768], F32, over=address["pf"])
    wh = sb("wh", [P, 4, KT, D], F32R)
    wl = sb("wl", [P, 4, KT, D], F32R)
    xq3 = sb("xq3", [P, 2, 4, P], F32, over=address["zf"])
    xq1 = sb("xq1", [P, 2, 4, P], F32, over=address["wh"])
    xq2 = sb("xq2", [P, 2, 4, P], F32, over=address["wl"])
    qst = sb("qst", [P, NPAIR, T], F32R)
    kst = sb("kst", [P, NPAIR, T], F32R)
    vf = sb("vf", [P, 2, D], F32)
    vr = sb("vr", [P, 2, 2, D], F32)
    vs = sb("vs", [P, NT, NH, 3, VW], BF16)
    pt = sb("pt", [P, 2, 2, 384], F32)
    pth = [sb(f"pth{i}", [P, 2, 384], F16) for i in range(2)] + [sb("pth2", [P, 2, 384], F16, over=address["R"])]
    ptl = [sb(f"ptl{i}", [P, 2, 384], F16) for i in range(2)]
    ptl.append(sb("ptl2", [P, 2, 384], F16, over=address["R"] + 2 * 384 * 2))
    cw = sb("cw", [P, 2 * NB, D], F32, over=address["pt"])
    cm = sb("cm", [P, 2 * NB, D], F32, over=address["zs"])
    avn = zs
    cursor[0] = address["wstage"] + 2 * 3 * 768 * 4
    gh = sb("gh", [P, 2, 3, 768], F32R)
    gl = sb("gl", [P, 2, 3, 768], F32R)
    wb = sb("wb", [P, 2, CH, T], F32)
    sg = sb("sg", [P, 2, T], F32)
    tg = sb("tg", [P, 2, T], F32)
    hf = sb("hf", [P, 2, T], F32)
    hh = sb("hh", [P, 2, T], F32R)
    hl = sb("hl", [P, 2, T], F32R)
    yt = sb("yt", [P, KT, T], F32)
    wT_sb = sb("wT_sb", [NE, T], F32)
    ident = cst[:, C_ID * P:(C_ID + 1) * P]

    with ExitStack() as ctx:
        ps = ctx.enter_context(nc.psum_tensor("ps", [P, 8, 512], F32))

        def sem(name):
            return ctx.enter_context(nc.semaphore(name))

        SB = ps[:, 0:2, :]
        TB = ps[:, 2:4, :]
        OB = ps[:, 4:6, :]
        M0, M1 = 6, 7

        d_const, d_par, d_bias, d_ctx, d_rw = (sem(n) for n in ("d_const", "d_par", "d_bias", "d_ctx", "d_rw"))
        d_x = [sem(f"d_x{b}") for b in range(NB)]
        d_w = [sem(f"d_w{i}") for i in range(4)]
        d_max = [sem(f"d_max{b}") for b in range(NB)]
        d_wst = [sem(f"d_wst{i}") for i in range(2)]
        d_wb = [sem(f"d_wb{i}") for i in range(2)]
        d_rt, d_out = sem("d_rt"), sem("d_out")
        cvt = sem("cvt")
        names = ("ah al atp av_ready avt_n bias_x cab car cev cs1 cs2 cs3 cs4 csb csc csf ctp down e_ready ers "
                 "exs fin ftp gate ghi glo hhi hlo hmul lg lmxs mng mnl mtp pff ph16 phh pj pl16 pll prb qam qev "
                 "qs1 qs2 qs3 qs4 qsb qsc qsf qtp reps rev rev2 rin rp rtp rwt s_max s_ready silu t_ready tmul "
                 "tps up vsub v3 vev vpj whi wlo wo wrs wrts wss wte wtp wus x1 x2 xmm xscs yev yh yl ytp yzero "
                 "zff zh zl ztp").split()
        g = {n: sem("s_" + n) for n in names}

        ln_bn, ln_ag, ln_ri, ln_rs, ln_zn = ([sem(f"ln{i}_{n}") for i in range(3)]
                                             for n in ("bn", "ag", "ri", "rs", "zn"))

        block = ctx.enter_context(nc.Block())

        def bs(b):
            return slice(b * S, (b + 1) * S)

        def unit_of(step, phase):
            for u, steps in UNITS.items():
                if steps[phase] == step:
                    return u
            return None

        def rows_of(step, name):
            b = step - (LAG + AV_LAG + 7) - AT[name]
            return b // 8 if b >= 0 and b % 8 == 0 and b // 8 < NB else None

        def load_group(sp, n, buf):
            for k, w in enumerate((w_gate, w_up)):
                for kt in range(KT):
                    sp.dma_start(wstage[:, buf, k, kt * GW:(kt + 1) * GW].rearrange("p (e i) -> p e i", e=GE),
                                 w[bass.ds(n * GE, GE), kt * P:(kt + 1) * P, :].rearrange("e p i -> p e i")
                                 ).then_inc(d_wst[buf], 16)
            sp.dma_start(wstage[:, buf, 2, :].rearrange("p (c d) -> p c d", c=CH),
                         w_down.rearrange("e i d -> (e i) d")[bass.ds(n * GW, GW), :]
                         .rearrange("(c p) d -> p c d", p=P)).then_inc(d_wst[buf], 16)

        def load_routing(sp, n, buf):
            for c in range(CH):
                lo = c * P
                while lo < (c + 1) * P:
                    e = lo // NI
                    hi = min((e + 1) * NI, (c + 1) * P)
                    sp.dma_start(wb[lo - c * P:hi - c * P, buf, c, :],
                                 routing_dram[bass.ds(n * GE + e, 1), :].partition_broadcast(hi - lo)
                                 ).then_inc(d_wb[buf], 16)
                    lo = hi

        WB_DMAS = 6
        WST_DMAS = 5

        def heads(v):
            return v.rearrange("p (h d) -> p h d", h=NH)

        def value_part(act, t, i):
            o = t % 2
            if i == 0:
                act.wait_ge(g["vev"], t + 1)
            else:
                act.wait_ge(g["vsub"], 2 * t + i)
            src = vf[:, o] if i == 0 else vr[:, o, i - 1]
            act.activation(vs[:, t, :, i, 0:DH], heads(src), ACT.Copy).then_inc(g["v3"], 1)

        def value_rest(pool, t, i):
            o = t % 2
            pool.wait_ge(g["v3"], 3 * t + i + 1)
            src = vf[:, o] if i == 0 else vr[:, o, 0]
            pool.tensor_tensor(heads(vr[:, o, i]), heads(src), vs[:, t, :, i, 0:DH], ALU.subtract
                               ).then_inc(g["vsub"], 1)

        def row_blocks(b):
            return zs[:, 2 * b:2 * b + 2, :].rearrange("p t (k c) -> p (t k) c", c=P)

        def rsqrt(pool, ln, b):
            pool.wait_ge(ln_ri[ln], b + 1)
            t = slice(2 * b, 2 * b + 2)
            pool.tensor_tensor(rstd[:, ln, t], rs_in[:, ln, t], cst_half.to_broadcast([P, 2]), ALU.pow
                               ).then_inc(ln_rs[ln], 1)

        def add_output_bias(pool, t):
            pool.tensor_tensor(xs[:, t], xs[:, t], bob[:, :], ALU.add).then_inc(g["bias_x"], 1)

        def split_lo(pool, n, buf, part):
            pool.wait_ge(g["ghi"], 3 * n + part + 1)
            pool.tensor_tensor(gl[:, buf, part], wstage[:, buf, part], gh[:, buf, part].bitcast(F32), ALU.subtract
                               ).then_inc(g["glo"], 1)

        def pool_experts(pool):
            for part in range(3):
                split_lo(pool, 0, 0, part)

            def period(i, last):
                for pg in range(PERIOD):
                    n = i * PERIOD + pg
                    pool.wait_ge(d_wb[pg], (i + 1) * (16 * WB_DMAS))
                    for c in range(CH):
                        for h in range(2):
                            k = (n * CH + c) * 2 + h
                            hs = slice(h * HALF, (h + 1) * HALF)
                            j = (pg * CH + c) % 2
                            pool.wait_ge(g["silu"], k + 1)
                            pool.tensor_tensor(tg[:, j, hs], sg[:, j, hs], wb[:, pg, c, hs], ALU.mult
                                               ).then_inc(g["tmul"], 1)
                        if not (last and pg == PERIOD - 1):
                            split_lo(pool, n + 1, 1 - pg, c)

            with pool.Fori(0, GROUPS // PERIOD - 1) as i:
                period(i, False)
            period(GROUPS // PERIOD - 1, True)

        def bf16_bank(bank):
            return ps[:, bank, 0:256].bitcast(BF16)

        def project_bank(u):
            return u % 2 if u < 4 else 2 + u % 2 if u < 7 else M0

        def stack_bank(u, lp):
            return 2 + lp if u < 4 else 4 + lp % 2 if u < 7 else M0 + lp % 2

        def stack_evac(eng, u, which_eng, part=None):
            half, which, mt = u // 4, u % 4 // 2, u % 2
            dst = kst if which else qst
            for lp in range(which_eng, 4, 2):
                if part not in (None, lp // 2):
                    continue
                k = 4 * u + lp
                eng.wait_ge(g["rp"], k + 1)
                o = dst[:, 4 * mt + lp, half * HALF:(half + 1) * HALF]
                i = ps[:, stack_bank(u, lp), :]
                one = cst[:, C_ONE * P:C_ONE * P + 1]
                if which_eng == 0:
                    if which:
                        ins = eng.activation(o, i, ACT.Identity, bias=one)
                    else:
                        ins = eng.activation(o, i, ACT.Copy)
                    ins.then_inc(g["rev"], 1)
                else:
                    if which:
                        ins = eng.tensor_scalar(o, i, one, None, ALU.add)
                    else:
                        ins = eng.tensor_copy(o, i)
                    ins.then_inc(g["rev2"], 1)

        def act_experts(act):
            def period(i):
                for pg in range(PERIOD):
                    for c in range(CH):
                        n = (i * PERIOD + pg) * CH + c
                        j = (pg * CH + c) % 2
                        for h in range(2):
                            hs = slice(h * HALF, (h + 1) * HALF)
                            act.wait_ge(g["gate"], n * 2 + (h + 1))
                            act.activation(sg[:, j, hs], ps[:, h, :], ACT.Silu).then_inc(g["silu"], 1)
                        for h in range(2):
                            hs = slice(h * HALF, (h + 1) * HALF)
                            act.wait_ge(g["hmul"], n * 2 + (h + 1))
                            act.activation(hh[:, j, hs], hf[:, j, hs], ACT.Copy).then_inc(g["hhi"], 1)

            with act.Fori(0, GROUPS // PERIOD) as i:
                period(i)

        def pe_experts(pe, f32_product):
            ks = range(KT)

            def hidden(n, buf, c, first=False):
                for h in range(2):
                    hs = slice(h * HALF, (h + 1) * HALF)
                    for part, done in ((0, "silu"), (1, "hmul")):
                        if not first:
                            pe.wait_ge(g[done], (n - 1) * 2 + (h + 1))
                        cs = [slice(k * GW + c * P, k * GW + (c + 1) * P) for k in ks]
                        f32_product(ps[:, 2 * part + h, :], [gh[:, buf, part, s] for s in cs],
                                    [gl[:, buf, part, s] for s in cs], [zth[:, k, hs] for k in ks],
                                    [ztl[:, k, hs] for k in ks], True, True
                                    ).then_inc(g["gate" if part == 0 else "up"], 1)

            def output(n, buf, c):
                j = (buf * CH + c) % 2
                for h in range(2):
                    hs = slice(h * HALF, (h + 1) * HALF)
                    pe.wait_ge(g["hhi"], n * 2 + (h + 1))
                    pe.wait_ge(g["hlo"], n * 2 + (h + 1))
                    for k in ks:
                        w = slice(c * D + k * P, c * D + (k + 1) * P)
                        mm = f32_product(ps[:, 4 + 2 * k + h, :], [gh[:, buf, 2, w]], [gl[:, buf, 2, w]],
                                         [hh[:, j, hs]], [hl[:, j, hs]], False, True)
                mm.then_inc(g["down"], 1)

            def weights(n, part):
                pe.wait_ge(g["ghi"], n * 3 + (part + 1))
                pe.wait_ge(g["glo"], n * 3 + (part + 1))

            pe.wait_ge(g["wte"], 2)
            pe.wait_ge(g["yzero"], 3)
            pe.wait_ge(g["avt_n"], 2 * NB)
            for k in range(4):
                mm = pe.matmul(ps[:, 4 + k, :], zeros_bf[:, 0:P], zeros_bf[:, :], start=True, stop=False,
                               skip_group_check=True)
            mm.then_inc(g["down"], 1)
            pe.wait_ge(g["yh"], NB)
            pe.wait_ge(g["yl"], NB)
            weights(0, 1)
            hidden(0, 0, 0, first=True)

            def period(i, last):
                for pg in range(PERIOD):
                    for c in range(CH):
                        grp = i * PERIOD + pg
                        n = grp * CH + c
                        if not (last and pg == PERIOD - 1 and c == CH - 1):
                            if c == CH - 1:
                                weights(grp + 1, 1)
                                hidden(n + 1, 1 - pg, 0)
                            else:
                                hidden(n + 1, pg, c + 1)
                        if c == 0:
                            weights(grp, 2)
                        output(n, pg, c)

            with pe.Fori(0, GROUPS // PERIOD - 1) as i:
                period(i, False)
            period(GROUPS // PERIOD - 1, True)

        def quant_scales(dve, am, floor, ready, s_safe, s_scale, n):
            src = am[:, 1, :] if ready == "car" else am[:, 0, :]
            dve.wait_ge(g[ready], n)
            dve.tensor_scalar(am[:, 2, :], src, floor, None, ALU.max).then_inc(g[s_safe], 1)
            dve.wait_ge(g[s_safe], 3 * n - 2)
            dve.tensor_scalar(am[:, 3, :], am[:, 2, :], 1.0 / FP8_MAX, None, ALU.mult).then_inc(g[s_safe], 1)
            dve.reciprocal(am[:, 0, :], am[:, 2, :]).then_inc(g[s_safe], 1)
            dve.wait_ge(g[s_safe], 3 * n)
            dve.tensor_scalar(am[:, 4, :], am[:, 0, :], FP8_MAX, None, ALU.mult).then_inc(g[s_scale], 1)
            dve.wait_ge(g[s_scale], n)

        def round_step(dve, src, dst, s_exp, s_magic, n):
            dve.tensor_scalar(dst.bitcast(U32), src.bitcast(U32), 0x7F800000, None, ALU.bitwise_and
                              ).then_inc(g[s_exp], 1)
            dve.wait_ge(g[s_exp], n)
            dve.tensor_scalar(dst, dst, 2.0 ** -6, 1.5 * 2.0 ** 20, ALU.max, ALU.mult).then_inc(g[s_magic], 1)

        def route(dve, b, stage):
            t2 = slice(2 * b, 2 * b + 2)
            if stage == "softmax":
                dve.wait_ge(g["lg"], b + 1)
                dve.tensor_reduce(lmx[:, t2], ps[:, M1, 0:2 * NE].rearrange("p (t e) -> p t e", t=2), AX.X, ALU.max,
                                  negate=True).then_inc(g["lmxs"], 1)
            if stage == "top":
                dve.wait_ge(g["exs"], 2 * b + 2)
                dve.reciprocal(erec[:, t2], esum[:, t2]).then_inc(g["ers"], 1)
                dve.wait_ge(g["ers"], b + 1)
                for t in (2 * b, 2 * b + 1):
                    dve.tensor_scalar(prob[:, t], ex[:, t], erec[:, t:t + 1], None, ALU.mult).then_inc(g["prb"], 1)
                dve.wait_ge(g["prb"], 2 * b + 2)
                for t in (2 * b, 2 * b + 1):
                    dve.max(top[:, t], prob[:, t]).then_inc(g["tps"], 1)
                dve.wait_ge(g["tps"], 2 * b + 2)
                for t in (2 * b, 2 * b + 1):
                    dve.match_replace(rep[:, t], top[:, t], prob[:, t], -1.0).then_inc(g["reps"], 1)
            if stage == "weights":
                dve.wait_ge(g["reps"], 2 * b + 2)
                dve.scalar_tensor_tensor(out=wun[:, t2], in0=rep[:, t2], scalar=0.0, in1=prob[:, t2],
                                         op0=ALU.is_lt, op1=ALU.mult).then_inc(g["wus"], 1)
                dve.wait_ge(g["wus"], b + 1)
                dve.tensor_reduce(wsum[:, t2], wun[:, t2], AX.X, ALU.add).then_inc(g["wss"], 1)
                dve.wait_ge(g["wss"], b + 1)
                dve.reciprocal(wrec[:, t2], wsum[:, t2]).then_inc(g["wrs"], 1)
                dve.wait_ge(g["wrs"], b + 1)
                for t in (2 * b, 2 * b + 1):
                    dve.tensor_scalar(wrt[:, t], wun[:, t], wrec[:, t:t + 1], None, ALU.mult
                                      ).then_inc(g["wrts"], 1)

        def split_hi(dve, n, buf, part, i):
            dve.wait_ge(d_wst[buf], (i + 1) * (16 * WST_DMAS))
            dve.tensor_copy(gh[:, buf, part], wstage[:, buf, part]).then_inc(g["ghi"], 1)

        def dve_experts(dve):
            for part in range(3):
                split_hi(dve, 0, 0, part, 0)

            def period(i, last):
                for pg in range(PERIOD):
                    for c in range(CH):
                        n = (i * PERIOD + pg) * CH + c
                        j = (pg * CH + c) % 2
                        for h in range(2):
                            hs = slice(h * HALF, (h + 1) * HALF)
                            dve.wait_ge(g["up"], n * 2 + (h + 1))
                            dve.wait_ge(g["tmul"], n * 2 + (h + 1))
                            dve.tensor_tensor(hf[:, j, hs], ps[:, 2 + h, :], tg[:, j, hs], ALU.mult
                                              ).then_inc(g["hmul"], 1)
                        for h in range(2):
                            hs = slice(h * HALF, (h + 1) * HALF)
                            dve.wait_ge(g["hhi"], n * 2 + (h + 1))
                            dve.tensor_tensor(hl[:, j, hs], hf[:, j, hs], hh[:, j, hs].bitcast(F32), ALU.subtract
                                              ).then_inc(g["hlo"], 1)
                        if not (last and pg == PERIOD - 1):
                            if c == 0:
                                dve.wait_ge(g["down"], (i * PERIOD + pg) * CH + 1)
                            split_hi(dve, 0, 1 - pg, c, i if pg == 0 else i + 1)

            with dve.Fori(0, GROUPS // PERIOD - 1) as i:
                period(i, False)
            period(GROUPS // PERIOD - 1, True)

        @block.sync
        def _(sp):
            for b in range(NB):
                sp.dma_start(xs[:, 2 * b:2 * b + 2, :], x[b].rearrange("(t p) d -> p t d", p=P)).then_inc(d_x[b], 16)
            for i, w in enumerate((Wq, Wk, Wv, Wo)):
                sp.dma_start(wraw[:, i], w.rearrange("(t p) n -> p t n", p=P)).then_inc(d_w[i], 16)
            sp.dma_start(cw[:, :, :], ctx_2048.rearrange("e (a p) k -> p (e a) k", p=P)).then_inc(d_ctx, 16)
            for b in range(NB):
                sp.wait_ge(g["mnl"], b + 1)
                for a in range(2):
                    for j in range(2):
                        r0 = ROWS * a + MAXROW + j
                        sp.dma_start(qst[r0:r0 + 1, :, bs(b)].bitcast(F32),
                                     mneg[a:NH:2, j, :].bitcast(F32)).then_inc(d_max[b], 16)
                if b == 0:
                    sp.wait_ge(g["wlo"], 2)
                    sp.wait_ge(g["rp"], 32)
                    for par_g in range(2):
                        load_group(sp, par_g, par_g)
            sp.wait_ge(g["wte"], 2)
            sp.dma_start(routing_dram, wT_sb[:, :]).then_inc(d_rt, 16)
            sp.wait_ge(d_rt, 16)
            for par_g in range(2):
                load_routing(sp, par_g, par_g)
            with sp.Fori(0, GROUPS // PERIOD - 1) as i:
                for pg in range(PERIOD):
                    done = i * PERIOD + (pg + 1)
                    sp.wait_ge(g["ghi"], done * 3)
                    sp.wait_ge(g["glo"], done * 3)
                    load_group(sp, (i + 1) * PERIOD + pg, pg)
                    sp.wait_ge(g["tmul"], done * (2 * CH))
                    load_routing(sp, (i + 1) * PERIOD + pg, pg)
            for b in range(NB):
                sp.wait_ge(g["fin"], b + 1)
                sp.dma_start(out[b].rearrange("(t p) d -> p t d", p=P), xs[:, 2 * b:2 * b + 2, :]).then_inc(d_out, 16)
            sp.wait_ge(d_out, 16 * NB)

        @block.gpsimd
        def _(pool):
            pool.memset(zeros_bf[:, :], 0.0).then_inc(g["yzero"], 1)
            pool.memset(vs[:, :, :, 0, DH:VW], 1.0).then_inc(g["yzero"], 1)
            pool.memset(vs[:, :, :, 1:3, DH:VW], 0.0).then_inc(g["yzero"], 1)
            pool.wait_ge(d_const, 16)
            rsqrt(pool, 0, 0)
            for b in range(NB):
                if b + 1 < NB:
                    rsqrt(pool, 0, b + 1)
                pool.wait_ge(g["zh"], b + 1)
                pool.tensor_tensor(ztl[:, :, bs(b)], zf[:, b % 2], zth[:, :, bs(b)].bitcast(F32), ALU.subtract
                                   ).then_inc(g["zl"], 1)
            pool.wait_ge(g["yzero"], 3)
            for i in (2, 3):
                pool.wait_ge(g["whi"], i + 1)
                pool.tensor_tensor(wl[:, i], wraw[:, i], wh[:, i].bitcast(F32), ALU.subtract).then_inc(g["wlo"], 1)
            pool.wait_ge(g["cab"], 1)
            pool.partition_all_reduce(wam[:, 1, :], wam[:, 0, :], P, bass.bass_isa.ReduceOp.max).then_inc(g["car"], 1)
            cw4 = cw[:, :, :].rearrange("p a (k c) -> p (a k) c", c=P)
            for t in range(2):
                for i in range(2):
                    value_rest(pool, t, i)
            pool.wait_ge(d_bias, 32)
            pool.wait_ge(ln_zn[0], NT)
            for t in range(4):
                add_output_bias(pool, t)
            pool.wait_ge(g["csc"], 1)
            pool.tensor_tensor(cw4, cw4, wam[:, 4, :].unsqueeze(2).to_broadcast([P, 16, P]), ALU.mult
                               ).then_inc(g["cs1"], 1)
            for t in range(2, 4):
                for i in range(2):
                    value_rest(pool, t, i)
            for step in range(STEPS):
                for i in range(2):
                    u = unit_of(step - i, VALUES)
                    if u is not None:
                        value_rest(pool, u, i)
                e = step - 1
                if 0 <= e < NB:
                    pool.wait_ge(g["cs3"], e + 1)
                    if e == 0:
                        pool.wait_ge(g["cs1"], 1)
                    e2 = slice(2 * e, 2 * e + 2)
                    pool.tensor_tensor(cw[:, e2, :], cw[:, e2, :], cm[:, e2, :], ALU.add).then_inc(g["cs4"], 1)
                e = step - NB - 1
                if 0 <= e < NB:
                    pool.wait_ge(g["cs4"], e + 1)
                    e2 = slice(2 * e, 2 * e + 2)
                    pool.tensor_tensor(cq[:, e2, :], cw[:, e2, :], cm[:, e2, :], ALU.subtract).then_inc(g["csb"], 1)
                if BIAS_X <= step < BIAS_X + 4:
                    add_output_bias(pool, step - BIAS_X + 4)
                for ln in (1, 2):
                    b = rows_of(step, f"deviation{ln}")
                    if b is not None:
                        rsqrt(pool, ln, b)
                b = rows_of(step, "scales")
                if b is not None:
                    if b == 0:
                        pool.wait_ge(g["pj"], 8)
                    pool.wait_ge(g["qsc"], b + 1)
                    pool.tensor_tensor(xq1[:, b % 2], row_blocks(b),
                                       xam[:, b, 4, :].unsqueeze(2).to_broadcast([P, 4, P]), ALU.mult
                                       ).then_inc(g["qs1"], 1)
                b = rows_of(step, "round")
                if b is not None:
                    o = b % 2
                    pool.wait_ge(g["qs3"], b + 1)
                    pool.tensor_tensor(xq3[:, o], xq1[:, o], xq2[:, o], ALU.add).then_inc(g["qs4"], 1)
                    pool.wait_ge(g["qs4"], b + 1)
                    pool.tensor_tensor(xqb[:, o], xq3[:, o], xq2[:, o], ALU.subtract).then_inc(g["qsb"], 1)
                m = step - LAG
                if 0 <= m < NB * NPAIR:
                    for a in range(2):
                        pool.wait_ge(g["ph16"], 2 * m + a + 1)
                        pool.tensor_tensor(ptl[m % 3][:, a], pt[:, m % 2, a], pth[m % 3][:, a], ALU.subtract
                                           ).then_inc(g["pl16"], 1)
            pool_experts(pool)

        @block.scalar
        def _(act):
            act.dma_start(cst[:, :], consts).then_inc(d_const, 16)
            for i, v in enumerate((ln_g, ln_b, bq, bk)):
                act.dma_start(prow[2 * i:2 * i + 2, :], v.rearrange("(t p) -> t p", p=P)).then_inc(d_par, 16)
            for dst, v in ((bvb, bv), (bob, bo)):
                act.dma_start(dst[:, :], v.rearrange("(a n) -> a n", a=1).partition_broadcast(P)).then_inc(d_bias, 16)
            act.dma_start(rw_sb[:, :], router_w).then_inc(d_rw, 16)
            act.wait_ge(g["rtp"], 1)
            act.activation(par[:, :], ps[:, M1, KT * NE:KT * NE + 8], ACT.Copy).then_inc(g["rwt"], 1)
            act.activation(rwt[:, :, :], ps[:, M1, 0:KT * NE].rearrange("p (k e) -> p k e", k=KT), ACT.Copy
                           ).then_inc(g["rwt"], 1)
            for i in range(4):
                act.wait_ge(d_w[i], 16)
                act.activation(wh[:, i], wraw[:, i], ACT.Copy).then_inc(g["whi"], 1)
            for b in range(NB):
                act.wait_ge(g["zff"], 2 * b + 2)
                act.activation(zth[:, :, bs(b)], zf[:, b % 2], ACT.Copy).then_inc(g["zh"], 1)
            act.wait_ge(g["rwt"], 1)
            def projected(u):
                which, mt = u % 4 // 2, u % 2
                act.wait_ge(g["pj"], u + 1)
                if u >= 2:
                    act.wait_ge(g["pll"], u - 1)
                act.activation(pf[:, u % 2], ps[:, project_bank(u), :], ACT.Identity,
                               bias=par[:, 4 + 2 * which + mt:5 + 2 * which + mt]).then_inc(g["pff"], 1)

            def stacked(u):
                for i in range(3):
                    value_part(act, u, i)
                    if i < 2:
                        stack_evac(act, u, 0, i)

            for u in range(4):
                projected(u)
                if u >= 1:
                    stacked(u - 1)
            stacked(3)
            for step in range(STEPS):
                for i in range(2):
                    u = unit_of(step, STACK0 + i)
                    if u is not None:
                        stack_evac(act, u, 0, i)
                u = unit_of(step, PROJECT)
                if u is not None:
                    projected(u)
                for i in (2, 1, 0):
                    u = unit_of(step - i, VALUES)
                    if u is not None:
                        value_part(act, u, i)
                b = rows_of(step, "turn")
                if b is not None:
                    act.wait_ge(g["qtp"], b + 1)
                    act.activation(xqt[:, b % 2].rearrange("p k s -> p (k s)"), bf16_bank(M0), ACT.Copy
                                   ).then_inc(g["qev"], 1)
                m = step - LAG
                if 0 <= m < NB * NPAIR:
                    if m == 0:
                        act.wait_ge(g["csb"], NB)
                    act.wait_ge(g["t_ready"], m + 1)
                    if m >= 2:
                        act.wait_ge(g["pl16"], 2 * (m - 1))
                    act.activation(pt[:, m % 2], TB[:, :, P:512], ACT.Exp, scale=DH ** -0.5).then_inc(g["e_ready"], 1)
                    act.wait_ge(g["e_ready"], m + 1)
                    if m == 2:
                        act.wait_ge(g["rp"], 32)
                    if m >= 3:
                        act.wait_ge(g["av_ready"], m - 2)
                    for a in range(2):
                        act.activation(pth[m % 3][:, a], pt[:, m % 2, a], ACT.Copy).then_inc(g["ph16"], 1)
                if step % 8 == 0 and 1 <= step // 8 <= NB:
                    b = step // 8 - 1
                    act.wait_ge(g["mtp"], b + 1)
                    if b:
                        act.wait_ge(d_max[b - 1], 64)
                    act.activation(mneg[:, 0, :], ps[0:NH, M1, 0:S], ACT.Copy, scale=-1.0
                                   ).then_inc(g["mng"], 1)
                e = step - CTX_T
                if 0 <= e < NB:
                    act.wait_ge(g["ctp"], e + 1)
                    act.activation(cqt[:, e].rearrange("p k n -> p (k n)"), bf16_bank(M0), ACT.Copy
                                   ).then_inc(g["cev"], 1)
                b = rows_of(step, "transpose")
                if b is not None:
                    act.wait_ge(g["atp"], b + 1)
                    act.activation(zth[:, :, bs(b)], ps[:, M0, :].rearrange("p (k s) -> p k s", k=KT), ACT.Copy
                                   ).then_inc(g["ah"], 1)
                b = rows_of(step, "transpose3")
                if b is not None:
                    act.wait_ge(g["ytp"], b + 1)
                    act.activation(zth[:, :, bs(b)], ps[:, M0, :].rearrange("p (k s) -> p k s", k=KT), ACT.Copy
                                   ).then_inc(g["yh"], 1)
                b = rows_of(step, "softmax")
                if b is not None:
                    act.wait_ge(g["lmxs"], b + 1)
                    for t in range(2):
                        act.activation(ex[:, 2 * b + t], ps[:, M1, t * NE:(t + 1) * NE], ACT.Exp,
                                       bias=lmx[:, 2 * b + t:2 * b + t + 1],
                                       accum_out=esum[:, 2 * b + t:2 * b + t + 1]).then_inc(g["exs"], 1)
            for h in range(2):
                act.wait_ge(g["wtp"], h + 1)
                act.activation(wT_sb[:, h * HALF:(h + 1) * HALF], ps[0:NE, M0 + h, :], ACT.Copy).then_inc(g["wte"], 1)
            act_experts(act)
            for k in range(KT):
                for h in range(2):
                    if k + h == 0:
                        act.wait_ge(g["down"], GROUPS * CH + 1)
                    act.activation(yt[:, k, h * HALF:(h + 1) * HALF], ps[:, 4 + 2 * k + h, :], ACT.Copy
                                   ).then_inc(g["yev"], 1)

        @block.tensor
        def _(pe):
            last_read = {}

            def take(bank, reader, count):
                if bank in last_read:
                    pe.wait_ge(*last_read[bank])
                last_read[bank] = (g[reader], count)

            def f32_product(dst, lh, ll, rh, rl, first, last, check=False):
                n = len(lh)
                for k in range(n):
                    for j, (a, b) in enumerate(((lh[k], rh[k]), (lh[k], rl[k]), (ll[k], rh[k]))):
                        mm = pe.matmul(dst, a, b, start=first and k == 0 and j == 0,
                                       stop=last and k == n - 1 and j == 2, skip_group_check=True)
                return mm

            pe.wait_ge(d_const, 16)
            pe.wait_ge(d_rw, 16)
            take(M1, "rwt", 2)
            for k in range(KT):
                pe.transpose(ps[:, M1, k * NE:(k + 1) * NE], rw_sb[:, k * P:(k + 1) * P], ident[0:NE, 0:NE])
            pe.wait_ge(d_par, 64)
            pe.transpose(ps[:, M1, KT * NE:KT * NE + 8], prow[:, :], ident[0:8, 0:8]).then_inc(g["rtp"], 1)
            for b in range(NB):
                if b >= 2:
                    pe.wait_ge(g["zff"], 2 * (b - 1))
                for t in range(2):
                    pe.wait_ge(ln_zn[0], 2 * b + t + 1)
                    for k in range(KT):
                        mm = pe.transpose(OB[:, b % 2, k * S + t * P:k * S + (t + 1) * P],
                                          zs[:, 2 * b + t, k * P:(k + 1) * P], ident)
                mm.then_inc(g["ztp"], 1)

            def project(u):
                half, which, mt = u // 4, u % 4 // 2, u % 2
                if u % 4 == 0:
                    pe.wait_ge(g["zl"], 2 * half + 2)
                    pe.wait_ge(g["zh"], 2 * half + 2)
                if u < 4 and mt == 0:
                    pe.wait_ge(g["whi"], which + 1)
                    pe.wait_ge(cvt, which + 1)
                if u in (4, 5):
                    pe.wait_ge(g["rev" if u == 4 else "rev2"], 7)
                if u == 7:
                    take(M0, "pff", u + 1)
                elif u >= 2:
                    pe.wait_ge(g["pff"], u - 1)
                ks = range(KT)
                hs = slice(half * HALF, (half + 1) * HALF)
                ms = slice(mt * P, (mt + 1) * P)
                f32_product(ps[:, project_bank(u), :], [wh[:, which, k, ms] for k in ks], [wl[:, which, k, ms] for k in ks],
                            [zth[:, k, hs] for k in ks], [ztl[:, k, hs] for k in ks], True, True
                            ).then_inc(g["pj"], 1)

            def stack(u, lps):
                which = u % 4 // 2
                if u == 0 and lps[0] == 0:
                    pe.wait_ge(cvt, 9)
                    pe.wait_ge(g["zff"], 2 * NB)
                pe.wait_ge(g["pll"], u + 1)
                for lp in lps:
                    k = 4 * u + lp
                    bank, copied = stack_bank(u, lp), "rev" if lp % 2 == 0 else "rev2"
                    if u == 7:
                        take(bank, copied, 2 * u + lp // 2 + 1)
                    elif k >= 4:
                        pe.wait_ge(g[copied], 2 * (u - 1) + lp // 2 + 1 if u < 4 else 2 * u + lp // 2)
                    pe.matmul(ps[:, bank, :], R[:, lp, 2 * which], ph[:, u % 2], start=True, stop=False)
                    pe.matmul(ps[:, bank, :], R[:, lp, 2 * which + 1], pl[:, u % 2], start=False, stop=True
                              ).then_inc(g["rp"], 1)

            def values(t):
                take(M0 + t % 2, "vev", t + 1)
                if t == 0:
                    pe.wait_ge(g["whi"], 3)
                    pe.wait_ge(g["wlo"], 1)
                ks = range(KT)
                ts = slice(t * P, (t + 1) * P)
                f32_product(ps[:, M0 + t % 2, 0:D], [zth[:, k, ts] for k in ks], [ztl[:, k, ts] for k in ks],
                            [wh[:, 2, k] for k in ks], [wl[:, 2, k] for k in ks], True, True
                            ).then_inc(g["vpj"], 1)

            project(0)
            for u in range(4):
                if u < 3:
                    project(u + 1)
                values(u)
                stack(u, range(4))

            def scores(n):
                b, hp = n // NPAIR, n % NPAIR
                if n in (0, 16):
                    pe.wait_ge(g["rev"], 8 if n == 0 else 16)
                    pe.wait_ge(g["rev2"], 8 if n == 0 else 16)
                if n:
                    pe.wait_ge(g["s_max"], 2 * n)
                for a in range(2):
                    rs = slice(ROWS * a, ROWS * (a + 1))
                    for qt in range(2):
                        c0 = b * S + qt * P
                        pe.matmul(SB[:, a, qt * S:(qt + 1) * S], qst[rs, hp, c0:c0 + P], kst[rs, hp, bs(b)],
                                  start=(qt == 0), stop=False, skip_group_check=True)
                for a in range(2):
                    blocks = SB[:, a, :].rearrange("p (n c) -> p n c", c=P)[:, 0:4:3, :]
                    mm = pe.matmul(blocks, ident_bf[:, :], mask_s[:, :, :], start=False, stop=True,
                                   skip_group_check=True)
                mm.then_inc(g["s_ready"], 1)

            def scores_t(m):
                b, hp = m // NPAIR, m % NPAIR
                if hp == 0:
                    pe.wait_ge(d_max[b], 64)
                if m == 0:
                    pe.wait_ge(g["pff"], 7)
                if m:
                    pe.wait_ge(g["e_ready"], m)
                for a in range(2):
                    rs = slice(ROWS * a, ROWS * (a + 1))
                    for half in range(2):
                        c0 = b * S + (1 - half) * P
                        pe.matmul(TB[:, a, half * S:(half + 1) * S], kst[rs, hp, c0:c0 + P], qst[rs, hp, bs(b)],
                                  start=(half == 0), stop=False, skip_group_check=True)
                for a in range(2):
                    mm = pe.matmul(TB[:, a, P:P + 2 * P], ident_bf[:, :],
                                   mask_t[:, :, :].rearrange("p n c -> p (n c)"), start=False, stop=True,
                                   skip_group_check=True)
                mm.then_inc(g["t_ready"], 1)

            def attend(m):
                b, hp = m // NPAIR, m % NPAIR
                if hp == 0 and b:
                    pe.wait_ge(g["avt_n"], 2 * b)
                if m == 0:
                    pe.wait_ge(g["v3"], 3 * NT)
                    pe.wait_ge(g["rev"], 14)
                    pe.wait_ge(g["rev2"], 14)
                for a in range(2):
                    h = 2 * hp + a
                    pe.wait_ge(g["ph16"], 2 * m + a + 1)
                    pe.wait_ge(g["pl16"], 2 * m + a + 1)
                    for qt, kt, blk in ((0, 0, 1), (1, 0, 2), (1, 1, 0)):
                        for j, prob in enumerate((pth, ptl)):
                            for i in range(3):
                                mm = pe.matmul(OB[:, qt, h * VW:(h + 1) * VW],
                                               prob[m % 3][:, a, blk * P:(blk + 1) * P],
                                               vs[:, 2 * b + kt, h, i, :],
                                               start=(h == 0 and kt == 0 and j == 0 and i == 0),
                                               stop=True, skip_group_check=True)
                mm.then_inc(g["av_ready"], 1)

            for step in range(STEPS):
                if step < NB * NPAIR:
                    scores(step)
                for i in range(2):
                    u = unit_of(step, STACK0 + i)
                    if u is not None:
                        stack(u, (2 * i, 2 * i + 1))
                u = unit_of(step, VALUES)
                if u is not None:
                    values(u)
                u = unit_of(step, PROJECT)
                if u is not None:
                    project(u)
                if 0 <= step - LAG - AV_LAG < NB * NPAIR:
                    attend(step - LAG - AV_LAG)
                b = rows_of(step, "context")
                if b is not None:
                    pe.wait_ge(g["qev"], b + 1)
                    if b == 0:
                        pe.wait_ge(g["cev"], NB)
                    for t in range(2):
                        take(M0 + t, "x2", 8 * b + 4 * (t + 1))
                        for k in range(KT):
                            mm = pe.matmul(ps[:, M0 + t, k * D:(k + 1) * D], xqt[:, b % 2, k, t * P:(t + 1) * P],
                                           cqt[:, b, k], start=(k == 0), stop=True, skip_group_check=True)
                        mm.then_inc(g["xmm"], 1)
                if 0 <= step - LAG < NB * NPAIR:
                    scores_t(step - LAG)
                b = rows_of(step, "turn")
                if b is not None:
                    take(M0, "qev", b + 1)
                    pe.wait_ge(g["qsb"], b + 1)
                    for t in range(2):
                        for k in range(KT):
                            mm = pe.transpose(bf16_bank(M0)[:, k * S + t * P:k * S + (t + 1) * P],
                                              xqb[:, b % 2, 2 * t + k], ident_bf[:, :])
                    mm.then_inc(g["qtp"], 1)
                if step % 8 == 0 and 1 <= step // 8 <= NB:
                    b = step // 8 - 1
                    take(M1, "mnl", b + 1)
                    pe.wait_ge(g["s_max"], 2 * NPAIR * (b + 1))
                    for qt in range(2):
                        mm = pe.transpose(ps[0:NH, M1, qt * P:(qt + 1) * P], mx[:, b, qt], ident)
                    mm.then_inc(g["mtp"], 1)
                e = step - CTX_T
                if 0 <= e < NB:
                    take(M0, "cev", e + 1)
                    pe.wait_ge(g["csb"], e + 1)
                    for kb in range(KT):
                        for nb in range(2):
                            mm = pe.transpose(bf16_bank(M0)[:, kb * D + nb * P:kb * D + (nb + 1) * P],
                                              cq[:, 2 * e + nb, kb * P:(kb + 1) * P], ident_bf[:, :])
                    mm.then_inc(g["ctp"], 1)
                b = rows_of(step, "transpose")
                if b is not None:
                    take(M0, "al", b + 1)
                    pe.wait_ge(g["avt_n"], 2 * b + 2)
                    for t in range(2):
                        for k in range(KT):
                            mm = pe.transpose(ps[:, M0, k * S + t * P:k * S + (t + 1) * P],
                                              avn[:, 2 * b + t, k * P:(k + 1) * P], ident)
                    mm.then_inc(g["atp"], 1)
                b = rows_of(step, "project")
                if b is not None:
                    take(M1, "x1", b + 1)
                    if b == 0:
                        pe.wait_ge(g["whi"], 4)
                        pe.wait_ge(g["wlo"], 2)
                    pe.wait_ge(g["ah"], b + 1)
                    pe.wait_ge(g["al"], b + 1)
                    ks = range(KT)
                    for t in range(2):
                        ts = slice((2 * b + t) * P, (2 * b + t + 1) * P)
                        mm = f32_product(ps[:, M1, t * D:(t + 1) * D], [zth[:, k, ts] for k in ks],
                                         [ztl[:, k, ts] for k in ks], [wh[:, 3, k] for k in ks],
                                         [wl[:, 3, k] for k in ks], t == 0, True)
                    mm.then_inc(g["wo"], 1)
                b = rows_of(step, "transpose3")
                if b is not None:
                    take(M0, "yl", b + 1)
                    pe.wait_ge(ln_zn[2], 2 * b + 2)
                    for t in range(2):
                        for k in range(KT):
                            mm = pe.transpose(ps[:, M0, k * S + t * P:k * S + (t + 1) * P],
                                              zs[:, 2 * b + t, k * P:(k + 1) * P], ident)
                    mm.then_inc(g["ytp"], 1)
                b = rows_of(step, "logits")
                if b is not None:
                    take(M1, "exs", 2 * b + 2)
                    pe.wait_ge(g["yh"], b + 1)
                    pe.wait_ge(g["yl"], b + 1)
                    for t in range(2):
                        ts = slice((2 * b + t) * P, (2 * b + t + 1) * P)
                        for j, z in enumerate((zth, ztl)):
                            for k in range(KT):
                                mm = pe.matmul(ps[:, M1, t * NE:(t + 1) * NE], z[:, k, ts].bitcast(F32), rwt[:, k],
                                               start=(t == 0 and j == 0 and k == 0), stop=True,
                                               skip_group_check=True)
                    mm.then_inc(g["lg"], 1)
            for h in range(2):
                take(M0 + h, "wte", h + 1)
                pe.wait_ge(g["wrts"], 4 * (h + 1))
                for t in range(4):
                    mm = pe.transpose(ps[0:NE, M0 + h, t * P:(t + 1) * P], wrt[:, 4 * h + t, :], ident)
                mm.then_inc(g["wtp"], 1)
            pe_experts(pe, f32_product)
            for b in range(NB):
                pe.wait_ge(g["yev"], 4)
                for t in range(2):
                    for k in range(KT):
                        mm = pe.transpose(ps[:, b, t * D + k * P:t * D + (k + 1) * P],
                                          yt[:, k, (2 * b + t) * P:(2 * b + t + 1) * P], ident)
                mm.then_inc(g["ftp"], 1)

        @block.vector
        def _(dve):
            dve.wait_ge(d_const, 16)

            def stats_of(ln, b):
                for t in (2 * b, 2 * b + 1):
                    dve.bn_stats(stats[:, ln, t], xs[:, t]).then_inc(ln_bn[ln], 1)
                dve.wait_ge(ln_bn[ln], 2 * b + 2)
                for t in (2 * b, 2 * b + 1):
                    dve.bn_aggr(mv[:, ln, t], stats[:, ln, t]).then_inc(ln_ag[ln], 1)
                dve.wait_ge(ln_ag[ln], 2 * b + 2)
                m, a = (1.0 + EPS, EPS * EPS) if ln == 0 else (1.0, EPS)
                dve.tensor_scalar(rs_in[:, ln, 2 * b:2 * b + 2], mv[:, ln, 2 * b:2 * b + 2, 1], m, a,
                                  ALU.mult, ALU.add).then_inc(ln_ri[ln], 1)

            def normalise(ln, b):
                dve.wait_ge(ln_rs[ln], b + 1)
                for t in (2 * b, 2 * b + 1):
                    dve.tensor_scalar(zs[:, t], xs[:, t], mv[:, ln, t, 0:1], rstd[:, ln, t:t + 1],
                                      ALU.subtract, ALU.mult).then_inc(ln_zn[ln], 1)

            dve.wait_ge(d_x[0], 16)
            stats_of(0, 0)
            for i in (0, 1):
                dve.wait_ge(g["whi"], i + 1)
                dve.tensor_tensor(wl[:, i], wraw[:, i], wh[:, i].bitcast(F32), ALU.subtract).then_inc(cvt, 1)
            normalise(0, 0)
            for lp in range(4):
                dve.tensor_scalar(R[:, lp].rearrange("p k c -> p (k c)"), cst[:, C_QH * P:(C_KL + 1) * P],
                                  cst[:, C_ONE * P + 2 + lp:C_ONE * P + 3 + lp], None, ALU.mult).then_inc(cvt, 1)
            dve.tensor_copy(ident_bf[:, :], ident).then_inc(cvt, 1)
            for dst, i in ((mask_s, C_MS), (mask_t, C_MT)):
                dve.tensor_copy(dst[:, :, :], cst[:, i * P:(i + 1) * P].unsqueeze(1).to_broadcast([P, 2, P])
                                ).then_inc(cvt, 1)
            dve.wait_ge(g["rwt"], 1)

            def scaled(b):
                dve.wait_ge(g["ztp"], b + 1)
                if b >= 2:
                    dve.wait_ge(g["zl"], b - 1)
                for k in range(KT):
                    dve.tensor_scalar(zf[:, b % 2, k], OB[:, b % 2, k * S:(k + 1) * S], par[:, k:k + 1],
                                      par[:, 2 + k:3 + k], ALU.mult, ALU.add).then_inc(g["zff"], 1)

            for b in range(1, NB):
                dve.wait_ge(d_x[b], 16)
                stats_of(0, b)
                scaled(b - 1)
                normalise(0, b)
            scaled(NB - 1)
            dve.wait_ge(d_ctx, 16)
            cw4 = cw[:, :, :].rearrange("p a (k c) -> p (a k) c", c=P)
            dve.tensor_reduce(wam[:, 0, :], cw4, AX.X, ALU.max, apply_absolute_value=True).then_inc(g["cab"], 1)
            dve.wait_ge(d_bias, 32)

            def values_out(t):
                dve.wait_ge(g["vpj"], t + 1)
                if t >= 2:
                    dve.wait_ge(g["vsub"], 2 * (t - 1))
                dve.tensor_tensor(vf[:, t % 2], ps[:, M0 + t % 2, 0:D], bvb[:, :], ALU.add).then_inc(g["vev"], 1)

            def projected(u):
                dve.wait_ge(g["pff"], u + 1)
                if u >= 2:
                    dve.wait_ge(g["rp"], 4 * (u - 1))
                dve.tensor_copy(ph[:, u % 2], pf[:, u % 2]).then_inc(g["phh"], 1)
                dve.wait_ge(g["phh"], u + 1)
                dve.tensor_tensor(pl[:, u % 2], pf[:, u % 2], ph[:, u % 2].bitcast(F32), ALU.subtract
                                  ).then_inc(g["pll"], 1)

            for u in range(4):
                projected(u)
                values_out(u)
                stack_evac(dve, u, 1)
                if u == 1:
                    quant_scales(dve, wam, W_FLOOR, "car", "csf", "csc", 1)
            for step in range(STEPS):
                if step < NB * NPAIR:
                    n = step
                    b, hp = n // NPAIR, n % NPAIR
                    dve.wait_ge(g["s_ready"], n + 1)
                    dve.tensor_reduce(mx[:, b, 0, 2 * hp:2 * hp + 2], SB[:, :, 0:P], AX.X, ALU.max
                                      ).then_inc(g["s_max"], 1)
                    dve.tensor_reduce(mx[:, b, 1, 2 * hp:2 * hp + 2], SB[:, :, S:2 * S], AX.X, ALU.max
                                      ).then_inc(g["s_max"], 1)
                b = rows_of(step, "low")
                if b is not None:
                    dve.wait_ge(g["ah"], b + 1)
                    dve.tensor_tensor(ztl[:, :, bs(b)], ps[:, M0, :].rearrange("p (k s) -> p k s", k=KT),
                                      zth[:, :, bs(b)].bitcast(F32), ALU.subtract).then_inc(g["al"], 1)
                b = rows_of(step, "low3")
                if b is not None:
                    dve.wait_ge(g["yh"], b + 1)
                    dve.tensor_tensor(ztl[:, :, bs(b)], ps[:, M0, :].rearrange("p (k s) -> p k s", k=KT),
                                      zth[:, :, bs(b)].bitcast(F32), ALU.subtract).then_inc(g["yl"], 1)
                b = rows_of(step, "LN3")
                if b is not None:
                    normalise(2, b)
                if step % 8 == 1 and 1 <= step // 8 <= NB:
                    b = step // 8 - 1
                    dve.wait_ge(g["mng"], b + 1)
                    dve.scalar_tensor_tensor(out=mneg[:, 1, :], in0=ps[0:NH, M1, 0:S], scalar=-1.0,
                                             in1=mneg[:, 0, :].bitcast(F32), op0=ALU.mult, op1=ALU.subtract
                                             ).then_inc(g["mnl"], 1)
                for i in range(2):
                    u = unit_of(step, STACK0 + i)
                    if u is not None:
                        stack_evac(dve, u, 1, i)
                u = unit_of(step, VALUES)
                if u is not None:
                    values_out(u)
                u = unit_of(step, PROJECT)
                if u is not None:
                    projected(u)
                if step < NB:
                    dve.wait_ge(g["cs1"], 1)
                    e2 = slice(2 * step, 2 * step + 2)
                    round_step(dve, cw[:, e2, :], cm[:, e2, :], "cs2", "cs3", step + 1)
                b = rows_of(step, "divide")
                if b is not None:
                    dve.wait_ge(g["av_ready"], NPAIR * (b + 1))
                    o4 = OB[:, :, 0:NH * VW].rearrange("p q (h w) -> p q h w", w=VW)
                    dve.reciprocal(rinv[:, b], o4[:, :, :, DH]).then_inc(g["rin"], 1)
                    dve.wait_ge(g["rin"], b + 1)
                    for q in range(2):
                        dve.tensor_tensor(avn[:, 2 * b + q, :].rearrange("p (h d) -> p h d", h=NH),
                                          o4[:, q, :, 0:DH],
                                          rinv[:, b, q].unsqueeze(2).to_broadcast([P, NH, DH]), ALU.mult
                                          ).then_inc(g["avt_n"], 1)
                b = rows_of(step, "residual")
                if b is not None:
                    dve.wait_ge(g["wo"], b + 1)
                    if b == 0:
                        dve.wait_ge(g["bias_x"], NT)
                    dve.tensor_tensor(xs[:, 2 * b:2 * b + 2, :], ps[:, M1, :].rearrange("p (t d) -> p t d", t=2),
                                      xs[:, 2 * b:2 * b + 2, :], ALU.add).then_inc(g["x1"], 1)
                    dve.wait_ge(g["x1"], b + 1)
                    stats_of(1, b)
                b = rows_of(step, "LN2")
                if b is not None:
                    normalise(1, b)
                    dve.wait_ge(ln_zn[1], 2 * b + 2)
                    dve.tensor_reduce(xam[:, b, 0, :], row_blocks(b), AX.X, ALU.max, apply_absolute_value=True
                                      ).then_inc(g["qam"], 1)
                b = rows_of(step, "scales")
                if b is not None:
                    xa = xam[:, b]
                    quant_scales(dve, xa, ACT_FLOOR, "qam", "qsf", "qsc", b + 1)
                    for kb in range(KT):
                        dve.tensor_tensor(
                            xsc[:, b].rearrange("p (t k) n -> p t k n", k=KT)[:, :, kb, :],
                            xa[:, 3, :].rearrange("p (t k) -> p t k", k=KT)[:, :, kb:kb + 1].to_broadcast([P, 2, 2]),
                            wam[:, 3, 4 * b + kb:4 * b + kb + 3:2].unsqueeze(1).to_broadcast([P, 2, 2]),
                            ALU.mult).then_inc(g["xscs"], 1)
                b = rows_of(step, "round")
                if b is not None:
                    dve.wait_ge(g["qs1"], b + 1)
                    round_step(dve, xq1[:, b % 2], xq2[:, b % 2], "qs2", "qs3", b + 1)
                b = rows_of(step, "residual2")
                if b is not None:
                    dve.wait_ge(g["xscs"], 2 * b + 2)
                    for t in range(2):
                        dve.wait_ge(g["xmm"], 2 * b + t + 1)
                        for kb in range(KT):
                            if kb:
                                dve.wait_ge(g["x2"], 8 * b + 4 * t + 2)
                            for nb in range(2):
                                xo = xs[:, 2 * b + t, nb * P:(nb + 1) * P]
                                dve.scalar_tensor_tensor(
                                    out=xo, in0=ps[:, M0 + t, kb * D + nb * P:kb * D + (nb + 1) * P],
                                    scalar=xsc[:, b, 2 * t + kb, nb:nb + 1], in1=xo, op0=ALU.mult, op1=ALU.add
                                ).then_inc(g["x2"], 1)
                b = rows_of(step, "stats3")
                if b is not None:
                    dve.wait_ge(g["x2"], 8 * b + 8)
                    stats_of(2, b)
                for stage in ("softmax", "top", "weights"):
                    b = rows_of(step, stage)
                    if b is not None:
                        route(dve, b, stage)
            dve_experts(dve)
            for b in range(NB):
                dve.wait_ge(g["ftp"], b + 1)
                dve.tensor_tensor(xs[:, 2 * b:2 * b + 2, :], ps[:, b, :].rearrange("p (t d) -> p t d", t=2),
                                  xs[:, 2 * b:2 * b + 2, :], ALU.add).then_inc(g["fin"], 1)


def kernel(**inputs):
    import numpy as _np
    import concourse.bacc as _bacc
    from concourse import mybir as _mybir
    from concourse.bass_utils import run_bass_kernel_spmd as _run

    nc = _bacc.Bacc("TRN2", target_bir_lowering=False, num_devices=1)
    names = ["x", "ctx_2048"] + ["L0_attn_" + n for n in
                                 ("ln_g", "ln_b", "Wq", "bq", "Wk", "bk", "Wv", "bv", "Wo", "bo")]
    names += ["L0_ffn_" + n for n in ("router_w", "w_gate", "w_up", "w_down")]
    arrays = {"in_consts": host_constants()}
    args = [nc.dram_tensor("in_consts", arrays["in_consts"].shape, _mybir.dt.float32, kind="ExternalInput").ap()]
    for name in names:
        a = _np.ascontiguousarray(inputs[name])
        arrays["in_" + name] = a
        args.append(nc.dram_tensor("in_" + name, a.shape, _mybir.dt.from_np(a.dtype), kind="ExternalInput").ap())
    args.append(nc.dram_tensor("out_x", (NB, S, D), _mybir.dt.float32, kind="ExternalOutput").ap())
    decoder_layer(nc, *args)
    r = _run(nc, [arrays], core_ids=[0])
    return r.results[0]["out_x"]
```

```python
from contextlib import ExitStack

import concourse.bass as bass
from concourse import mybir

F32 = mybir.dt.float32
F32R = mybir.dt.float32r
BF16 = mybir.dt.bfloat16
F16 = mybir.dt.float16
U32 = mybir.dt.uint32
ALU = mybir.AluOpType
ACT = mybir.ActivationFunctionType
AX = mybir.AxisListType

P = 128
NB, S, D = 4, 256, 256
T = NB * S
NT = T // P
KT = D // P
HALF = T // 2
NH, DH = 16, 16
NPAIR = NH // 2
ROWS = 64
MAXROW = 3 * DH
VW = DH + 1
EPS = 1e-5
FP8_MAX, ACT_FLOOR, W_FLOOR = 448.0, 1e-4, 1e-6
NE, TOPK, NI = 32, 8, 96
GE = 4
GROUPS = NE // GE
GW = GE * NI
CH = GW // P
PERIOD = 2
NEG = -1e30
C_ID, C_QH, C_QL, C_KH, C_KL, C_MS, C_MT, C_ONE = range(8)
LAG = 11
AV_LAG = 3
UNITS = {4: (0, 1, 3, 1), 5: (2, 4, 5, 4), 6: (7, 8, 9, 7), 7: (11, 12, 13, 10)}
PROJECT, STACK0, STACK1, VALUES = range(4)
CTX_T = 16
BIAS_X = 4
AT = {"divide": 0, "transpose": 1, "low": 2, "project": 2, "residual": 3, "deviation1": 3, "LN2": 4, "scales": 5,
      "round": 6, "turn": 8, "context": 9, "residual2": 9, "stats3": 10, "deviation2": 10, "LN3": 12,
      "transpose3": 12, "low3": 13, "logits": 13, "softmax": 14, "top": 15, "weights": 16}
AT_BEFORE_LAST = {"divide": 0, "transpose": 1, "low": 2, "project": 2, "residual": 3, "deviation1": 3, "LN2": 4,
                  "scales": 5, "round": 6, "turn": 8, "context": 9, "residual2": 9, "stats3": 10,
                  "deviation2": 10, "LN3": 12, "transpose3": 12, "low3": 14, "logits": 14, "softmax": 15,
                  "top": 16, "weights": 17}
AT_LAST = {"divide": 0, "transpose": 1, "low": 2, "project": 1, "residual": 3, "deviation1": 3, "LN2": 3,
           "scales": 5, "round": 7, "turn": 8, "context": 9, "residual2": 10, "stats3": 10, "deviation2": 11,
           "LN3": 12, "transpose3": 12, "low3": 13, "logits": 13, "softmax": 13, "top": 14, "weights": 14}
TAIL = 49
GATE_AT = {0: 48, 1: 48, 2: 50, 3: 52, 4: 55, 5: 56, 6: 60, 7: 61}
UP_AT = {0: 48, 1: 50, 2: 51, 3: 53, 4: 56, 5: 59, 6: 60, 7: 61}
OUTPUT_AT = {0: 52, 1: 52, 2: 55, 3: 58, 4: 59, 5: 62}
GATING_AT = {0: 49, 1: 51, 2: 53, 3: 54, 4: 58, 5: 60}
ROUTE_AT = (46, 59)
SPLIT_HI_AT = {42: 0, 43: 1}
SPLIT_LO_AT = {43: ((0, 0), (0, 1)), 44: ((0, 2),), 47: ((1, 0),), 49: ((1, 1),), 50: ((1, 2),)}
STEPS = 63


def host_constants():
    import numpy as np

    c = np.zeros((P, C_ONE * P + 6), np.float32)
    blk = [c[:, i * P:(i + 1) * P] for i in range(C_ONE)]
    blk[C_ID][:] = np.eye(P)
    r = np.arange(P)[:, None] % 32
    col = np.arange(P)[None, :]
    same = (col // ROWS == r // DH) & (col % DH == r % DH)
    copy = col % ROWS // DH
    blk[C_QH][:] = same & ((copy == 0) | (copy == 1))
    blk[C_QL][:] = same & (copy == 2)
    blk[C_KH][:] = same & ((copy == 0) | (copy == 2))
    blk[C_KL][:] = same & (copy == 1)
    q = np.arange(P)[:, None]
    k = np.arange(P)[None, :]
    blk[C_MS][:] = np.where(k <= q, 0.0, NEG)
    blk[C_MT][:] = np.where(q <= k, 0.0, NEG)
    c[:, C_ONE * P] = np.arange(P) % ROWS // 2 * 2 == MAXROW
    c[:, C_ONE * P + 1] = -0.5
    c[:, C_ONE * P + 2:] = np.arange(P)[:, None] // 32 == np.arange(4)
    return c


def decoder_layer(nc, consts, x, ctx_2048, ln_g, ln_b, Wq, bq, Wk, bk, Wv, bv, Wo, bo,
                  router_w, w_gate, w_up, w_down, out):
    routing_dram = nc.dram_tensor("routing_t", [NE, T], F32).ap()

    base = nc.sbuf_base
    cursor = [base]
    address = {}

    def sb(name, shape, dt, over=None):
        size = {BF16: 2, F16: 2}.get(dt, 4)
        for s in shape[1:]:
            size *= s
        at = (cursor[0] + 31) // 32 * 32 if over is None else over
        cursor[0] = at + size if over is None else cursor[0]
        address[name] = at
        return nc.alloc_sbuf_tensor_at(name, shape, dt, offset=at)

    cst = sb("cst", [P, C_ONE * P + 6], F32)
    R = sb("R", [P, 4, 4, P], F32R)
    ident_bf = sb("ident_bf", [P, P], BF16)
    mask_s = sb("mask_s", [P, 2, P], BF16)
    mask_t = sb("mask_t", [P, 2, P], BF16)
    zeros_bf = sb("zeros_bf", [P, HALF], BF16)
    xs = sb("xs", [P, NT, D], F32)
    zth = sb("zth", [P, KT, T], F32R)
    ztl = sb("ztl", [P, KT, T], F32R)
    prow = sb("prow", [8, P], F32)
    par = sb("par", [P, 8], F32)
    bvb = sb("bvb", [P, D], F32)
    bob = sb("bob", [P, D], F32)
    mx = sb("mx", [P, NB, 2, NH], F32)
    mneg = sb("mneg", [NH, 2, S], F32R)
    stats = sb("stats", [P, 3, NT, 6], F32)
    mv = sb("mv", [P, 3, NT, 2], F32)
    rs_in = sb("rs_in", [P, 3, NT], F32)
    rstd = sb("rstd", [P, 3, NT], F32)
    rinv = sb("rinv", [P, NB, 2, NH], F32)
    cst_half = cst[:, C_ONE * P + 1:C_ONE * P + 2]
    cq = sb("cq", [P, 2 * NB, D], BF16)
    cqt = sb("cqt", [P, NB, KT, D], BF16)
    wam = sb("wam", [P, 6, 16], F32)
    xam = sb("xam", [P, NB, 5, 4], F32)
    xsc = sb("xsc", [P, NB, 4, 2], F32)
    xqb = sb("xqb", [P, 2, 4, P], BF16)
    xqt = sb("xqt", [P, 2, KT, S], BF16)
    rw_sb = sb("rw_sb", [NE, D], F32)
    rwt = sb("rwt", [P, KT, NE], F32)
    lmx = sb("lmx", [P, NT], F32)
    esum = sb("esum", [P, NT], F32)
    erec = sb("erec", [P, NT], F32)
    ex = sb("ex", [P, NT, NE], F32)
    prob = sb("prob", [P, NT, NE], F32)
    top = sb("top", [P, NT, 8], F32)
    rep = sb("rep", [P, NT, NE], F32)
    wun = sb("wun", [P, NT, NE], F32)
    wsum = sb("wsum", [P, NT], F32)
    wrec = sb("wrec", [P, NT], F32)
    wrt = sb("wrt", [P, NT, NE], F32)
    shared = cursor[0]
    zs = sb("zs", [P, NT, D], F32)
    zf = sb("zf", [P, 2, KT, S], F32)
    pf = sb("pf", [P, 2, HALF], F32)
    ph = sb("ph", [P, 2, HALF], F32R)
    pl = sb("pl", [P, 2, HALF], F32R)
    wraw = sb("wraw", [P, 4, KT, D], F32)
    wstage = sb("wstage", [P, 2, 3, 768], F32, over=address["pf"])
    wh = sb("wh", [P, 4, KT, D], F32R)
    wl = sb("wl", [P, 4, KT, D], F32R)
    xq3 = sb("xq3", [P, 2, 4, P], F32, over=address["zf"])
    xq1 = sb("xq1", [P, 2, 4, P], F32, over=address["wh"])
    xq2 = sb("xq2", [P, 2, 4, P], F32, over=address["wl"])
    qst = sb("qst", [P, NPAIR, T], F32R)
    kst = sb("kst", [P, NPAIR, T], F32R)
    vf = sb("vf", [P, 2, D], F32)
    vr = sb("vr", [P, 2, 2, D], F32)
    vs = sb("vs", [P, NT, NH, 3, VW], BF16)
    pt = sb("pt", [P, 2, 2, 384], F32)
    pth = [sb(f"pth{i}", [P, 2, 384], F16) for i in range(2)] + [sb("pth2", [P, 2, 384], F16, over=address["R"])]
    ptl = [sb(f"ptl{i}", [P, 2, 384], F16) for i in range(2)]
    ptl.append(sb("ptl2", [P, 2, 384], F16, over=address["R"] + 2 * 384 * 2))
    cw = sb("cw", [P, 2 * NB, D], F32, over=address["pt"])
    cm = sb("cm", [P, 2 * NB, D], F32, over=address["zs"])
    avn = zs
    cursor[0] = address["qst"]
    gh = sb("gh", [P, 2, 3, 768], F32R)
    gl = sb("gl", [P, 2, 3, 768], F32R)
    wb = sb("wb", [P, 2, CH, T], F32)
    tg = sb("tg", [P, 2, T], F32)
    hf = sb("hf", [P, 2, T], F32)
    hh = sb("hh", [P, 2, T], F32R)
    hl = sb("hl", [P, 2, T], F32R)
    sg = sb("sg", [P, 2, T], F32, over=address["R"])
    yt = sb("yt", [P, KT, T], F32, over=address["wstage"] + 2 * 3 * 768 * 4)
    wT_sb = sb("wT_sb", [NE, T], F32, over=address["cq"])
    ident = cst[:, C_ID * P:(C_ID + 1) * P]

    with ExitStack() as ctx:
        ps = ctx.enter_context(nc.psum_tensor("ps", [P, 8, 512], F32))

        def sem(name):
            return ctx.enter_context(nc.semaphore(name))

        SB = ps[:, 0:2, :]
        TB = ps[:, 2:4, :]
        OB = ps[:, 4:6, :]
        M0, M1 = 6, 7
        ROUTE_BANK = (3, M0)

        d_const, d_par, d_bias, d_ctx, d_rw = (sem(n) for n in ("d_const", "d_par", "d_bias", "d_ctx", "d_rw"))
        d_x = [sem(f"d_x{b}") for b in range(NB)]
        d_w = [sem(f"d_w{i}") for i in range(4)]
        d_max = [sem(f"d_max{b}") for b in range(NB)]
        d_wst = [sem(f"d_wst{i}") for i in range(2)]
        d_wb = [sem(f"d_wb{i}") for i in range(2)]
        d_rt, d_out = sem("d_rt"), sem("d_out")
        cvt = sem("cvt")
        names = ("ah al atp av_ready avt_n bias_x cab car cev cs1 cs2 cs3 cs4 csb csc csf ctp down down0 e_ready ers "
                 "exs fin ftp gate ghi glo hhi hlo hmul lg lmxs mng mnl mtp pff ph16 phh pj pl16 pll prb qam qev "
                 "qs1 qs2 qs3 qs4 qsb qsc qsf qtp reps rev rev2 rin rp rtp rwt s_max s_ready silu t_ready tmul "
                 "tps up vsub v3 vev vpj whi wlo wo wrs wrts wss wte wtp wus x1 x2 xmm xscs yev yev1 yh yl ytp yzero "
                 "zff zh zl ztp").split()
        g = {n: sem("s_" + n) for n in names}

        ln_bn, ln_ag, ln_ri, ln_rs, ln_zn = ([sem(f"ln{i}_{n}") for i in range(3)]
                                             for n in ("bn", "ag", "ri", "rs", "zn"))

        block = ctx.enter_context(nc.Block())

        def bs(b):
            return slice(b * S, (b + 1) * S)

        def unit_of(step, phase):
            for u, steps in UNITS.items():
                if steps[phase] == step:
                    return u
            return None

        def rows_of(step, name):
            for b in range(NB):
                at = AT_LAST if b == NB - 1 else AT_BEFORE_LAST if b == NB - 2 else AT
                if step == NPAIR * b + (LAG + AV_LAG + NPAIR - 1) + at[name]:
                    return b
            return None

        def load_group(sp, n, buf):
            for k, w in enumerate((w_gate, w_up)):
                for kt in range(KT):
                    sp.dma_start(wstage[:, buf, k, kt * GW:(kt + 1) * GW].rearrange("p (e i) -> p e i", e=GE),
                                 w[bass.ds(n * GE, GE), kt * P:(kt + 1) * P, :].rearrange("e p i -> p e i")
                                 ).then_inc(d_wst[buf], 16)
            sp.dma_start(wstage[:, buf, 2, :].rearrange("p (c d) -> p c d", c=CH),
                         w_down.rearrange("e i d -> (e i) d")[bass.ds(n * GW, GW), :]
                         .rearrange("(c p) d -> p c d", p=P)).then_inc(d_wst[buf], 16)

        def load_routing(sp, n, buf, ts=slice(0, T)):
            for c in range(CH):
                lo = c * P
                while lo < (c + 1) * P:
                    e = lo // NI
                    hi = min((e + 1) * NI, (c + 1) * P)
                    sp.dma_start(wb[lo - c * P:hi - c * P, buf, c, ts],
                                 routing_dram[bass.ds(n * GE + e, 1), ts].partition_broadcast(hi - lo)
                                 ).then_inc(d_wb[buf], 16)
                    lo = hi

        WB_DMAS = 6
        WST_DMAS = 5

        def heads(v):
            return v.rearrange("p (h d) -> p h d", h=NH)

        def value_part(act, t, i):
            o = t % 2
            if i == 0:
                act.wait_ge(g["vev"], t + 1)
            else:
                act.wait_ge(g["vsub"], 2 * t + i)
            src = vf[:, o] if i == 0 else vr[:, o, i - 1]
            act.activation(vs[:, t, :, i, 0:DH], heads(src), ACT.Copy).then_inc(g["v3"], 1)

        def value_rest(pool, t, i):
            o = t % 2
            pool.wait_ge(g["v3"], 3 * t + i + 1)
            src = vf[:, o] if i == 0 else vr[:, o, 0]
            pool.tensor_tensor(heads(vr[:, o, i]), heads(src), vs[:, t, :, i, 0:DH], ALU.subtract
                               ).then_inc(g["vsub"], 1)

        def row_blocks(b):
            return zs[:, 2 * b:2 * b + 2, :].rearrange("p t (k c) -> p (t k) c", c=P)

        def rsqrt(pool, ln, b):
            pool.wait_ge(ln_ri[ln], b + 1)
            t = slice(2 * b, 2 * b + 2)
            pool.tensor_tensor(rstd[:, ln, t], rs_in[:, ln, t], cst_half.to_broadcast([P, 2]), ALU.pow
                               ).then_inc(ln_rs[ln], 1)

        def add_output_bias(pool, t):
            pool.tensor_tensor(xs[:, t], xs[:, t], bob[:, :], ALU.add).then_inc(g["bias_x"], 1)

        def split_lo(pool, n, buf, part):
            pool.wait_ge(g["ghi"], 3 * n + part + 1)
            pool.tensor_tensor(gl[:, buf, part], wstage[:, buf, part], gh[:, buf, part].bitcast(F32), ALU.subtract
                               ).then_inc(g["glo"], 1)

        TURNS = 2 * PERIOD * CH

        def turn(q):
            h, k = divmod(q, PERIOD * CH)
            return k // CH, k % CH, slice(h * HALF, (h + 1) * HALF), k % 2

        def turn_tmul(pool, q):
            grp, c, hs, j = turn(q)
            if c == 0:
                pool.wait_ge(d_wb[grp], 16 * WB_DMAS * (q // (TURNS // 2) + 1))
            pool.wait_ge(g["silu"], q + 1)
            pool.tensor_tensor(tg[:, j, hs], sg[:, j, hs], wb[:, grp, c, hs], ALU.mult).then_inc(g["tmul"], 1)

        def pool_experts(pool):
            for q in range(TURNS // 2, TURNS):
                turn_tmul(pool, q)
                if q >= TURNS - CH:
                    split_lo(pool, PERIOD, 0, q - (TURNS - CH))

            def period(i, last):
                for pg in range(PERIOD):
                    n = i * PERIOD + pg
                    pool.wait_ge(d_wb[pg], (i + 2) * (16 * WB_DMAS))
                    for c in range(CH):
                        for h in range(2):
                            k = (n * CH + c) * 2 + h
                            hs = slice(h * HALF, (h + 1) * HALF)
                            j = (pg * CH + c) % 2
                            pool.wait_ge(g["silu"], k + 1)
                            pool.tensor_tensor(tg[:, j, hs], sg[:, j, hs], wb[:, pg, c, hs], ALU.mult
                                               ).then_inc(g["tmul"], 1)
                        if not (last and pg == PERIOD - 1):
                            split_lo(pool, n + 1, 1 - pg, c)

            with pool.Fori(1, GROUPS // PERIOD - 1) as i:
                period(i, False)
            period(GROUPS // PERIOD - 1, True)

        def bf16_bank(bank):
            return ps[:, bank, 0:256].bitcast(BF16)

        def project_bank(u):
            return u % 2 if u < 4 else 2 + u % 2 if u < 7 else M0

        def stack_bank(u, lp):
            return 2 + lp if u < 4 else 4 + lp % 2 if u < 7 else M0 + lp % 2

        def stack_evac(eng, u, which_eng, part=None):
            half, which, mt = u // 4, u % 4 // 2, u % 2
            dst = kst if which else qst
            for lp in range(which_eng, 4, 2):
                if part not in (None, lp // 2):
                    continue
                k = 4 * u + lp
                eng.wait_ge(g["rp"], k + 1)
                o = dst[:, 4 * mt + lp, half * HALF:(half + 1) * HALF]
                i = ps[:, stack_bank(u, lp), :]
                one = cst[:, C_ONE * P:C_ONE * P + 1]
                if which_eng == 0:
                    if which:
                        ins = eng.activation(o, i, ACT.Identity, bias=one)
                    else:
                        ins = eng.activation(o, i, ACT.Copy)
                    ins.then_inc(g["rev"], 1)
                else:
                    if which:
                        ins = eng.tensor_scalar(o, i, one, None, ALU.add)
                    else:
                        ins = eng.tensor_copy(o, i)
                    ins.then_inc(g["rev2"], 1)

        def turn_silu(act, q):
            _, _, hs, j = turn(q)
            act.wait_ge(g["gate"], q + 1)
            act.activation(sg[:, j, hs], ps[:, q % 2, :], ACT.Silu).then_inc(g["silu"], 1)

        def turn_hhi(act, q):
            _, _, hs, j = turn(q)
            act.wait_ge(g["hmul"], q + 1)
            act.activation(hh[:, j, hs], hf[:, j, hs], ACT.Copy).then_inc(g["hhi"], 1)

        def evacuate_output(eng, k):
            for h in range(2):
                eng.wait_ge(g["down0" if h == 0 else "down"], 1 if h == 0 else GROUPS * CH + 1)
                dst, src = yt[:, k, h * HALF:(h + 1) * HALF], ps[:, 4 + 2 * h + k, :]
                if k == 0:
                    eng.activation(dst, src, ACT.Copy).then_inc(g["yev"], 1)
                else:
                    eng.tensor_copy(dst, src).then_inc(g["yev1"], 1)

        def act_experts(act):
            for q in range(TURNS // 2, TURNS):
                if q > max(GATE_AT):
                    turn_silu(act, q)
                turn_hhi(act, q)

            def period(i):
                for pg in range(PERIOD):
                    for c in range(CH):
                        n = (i * PERIOD + pg) * CH + c
                        j = (pg * CH + c) % 2
                        for h in range(2):
                            hs = slice(h * HALF, (h + 1) * HALF)
                            act.wait_ge(g["gate"], n * 2 + (h + 1))
                            act.activation(sg[:, j, hs], ps[:, h, :], ACT.Silu).then_inc(g["silu"], 1)
                        for h in range(2):
                            hs = slice(h * HALF, (h + 1) * HALF)
                            act.wait_ge(g["hmul"], n * 2 + (h + 1))
                            act.activation(hh[:, j, hs], hf[:, j, hs], ACT.Copy).then_inc(g["hhi"], 1)

            with act.Fori(1, GROUPS // PERIOD) as i:
                period(i)

        def f32_product(pe, dst, lh, ll, rh, rl, first, last):
            n = len(lh)
            for k in range(n):
                for j, (a, b) in enumerate(((lh[k], rh[k]), (lh[k], rl[k]), (ll[k], rh[k]))):
                    mm = pe.matmul(dst, a, b, start=first and k == 0 and j == 0,
                                   stop=last and k == n - 1 and j == 2, skip_group_check=True)
            return mm

        def hidden_product(pe, bank, part, buf, c, hs):
            cs = [slice(k * GW + c * P, k * GW + (c + 1) * P) for k in range(KT)]
            f32_product(pe, ps[:, bank, :], [gh[:, buf, part, s] for s in cs], [gl[:, buf, part, s] for s in cs],
                        [zth[:, k, hs] for k in range(KT)], [ztl[:, k, hs] for k in range(KT)], True, True
                        ).then_inc(g["gate" if part == 0 else "up"], 1)

        def output_product(pe, buf, c, j, h):
            hs = slice(h * HALF, (h + 1) * HALF)
            for k in range(KT):
                w = slice(c * D + k * P, c * D + (k + 1) * P)
                mm = f32_product(pe, ps[:, 4 + 2 * h + k, :], [gh[:, buf, 2, w]], [gl[:, buf, 2, w]],
                                 [hh[:, j, hs]], [hl[:, j, hs]], False, True)
            return mm

        def weights_ready(pe, n, part):
            pe.wait_ge(g["ghi"], n * 3 + (part + 1))
            pe.wait_ge(g["glo"], n * 3 + (part + 1))

        def output_zero(pe, h):
            for k in range(KT):
                mm = pe.matmul(ps[:, 4 + 2 * h + k, :], zeros_bf[:, 0:P], zeros_bf[:, :], start=True, stop=False,
                               skip_group_check=True)
            return mm

        def turn_hidden(pe, q, part):
            grp, c, hs, j = turn(q)
            if q < 2 and part == 0:
                pe.wait_ge(g["s_max"], 2 * NB * NPAIR)
                pe.wait_ge(g["e_ready"], NB * NPAIR)
            if q % (TURNS // 2) == 0 and part == 0:
                h = q // (TURNS // 2)
                pe.wait_ge(g["yh"], NB // 2 * (h + 1))
                pe.wait_ge(g["yl"], NB // 2 * (h + 1))
            if c == 0:
                weights_ready(pe, grp, part)
            if q >= 2:
                pe.wait_ge(g["silu" if part == 0 else "hmul"], q - 1)
            hidden_product(pe, 2 * part + q % 2, part, grp, c, hs)

        def turn_output(pe, q):
            grp, c, hs, j = turn(q)
            if c == 0:
                weights_ready(pe, grp, 2)
            pe.wait_ge(g["hhi"], q + 1)
            pe.wait_ge(g["hlo"], q + 1)
            mm = output_product(pe, grp, c, j, q // (TURNS // 2))
            if q >= TURNS // 2:
                mm.then_inc(g["down"], 1)

        def pe_experts(pe):
            output_zero(pe, 1).then_inc(g["down"], 1)

            def hidden(n, buf, c):
                for h in range(2):
                    hs = slice(h * HALF, (h + 1) * HALF)
                    for part, done in ((0, "silu"), (1, "hmul")):
                        pe.wait_ge(g[done], (n - 1) * 2 + (h + 1))
                        hidden_product(pe, 2 * part + h, part, buf, c, hs)

            def output(n, buf, c, final=False):
                for h in range(2):
                    pe.wait_ge(g["hhi"], n * 2 + (h + 1))
                    pe.wait_ge(g["hlo"], n * 2 + (h + 1))
                    mm = output_product(pe, buf, c, (buf * CH + c) % 2, h)
                    if final and h == 0:
                        mm.then_inc(g["down0"], 1)
                mm.then_inc(g["down"], 1)

            for q in range(TURNS // 2, TURNS):
                if q == TURNS - 1:
                    weights_ready(pe, PERIOD, 1)
                    hidden(PERIOD * CH, 0, 0)
                turn_output(pe, q)
                if q + 2 < TURNS:
                    turn_hidden(pe, q + 2, 0)
                    turn_hidden(pe, q + 2, 1)

            def period(i, last):
                for pg in range(PERIOD):
                    for c in range(CH):
                        grp = i * PERIOD + pg
                        n = grp * CH + c
                        if not (last and pg == PERIOD - 1 and c == CH - 1):
                            if c == CH - 1:
                                weights_ready(pe, grp + 1, 1)
                                hidden(n + 1, 1 - pg, 0)
                            else:
                                hidden(n + 1, pg, c + 1)
                        if c == 0:
                            weights_ready(pe, grp, 2)
                        output(n, pg, c, last and pg == PERIOD - 1 and c == CH - 1)

            with pe.Fori(1, GROUPS // PERIOD - 1) as i:
                period(i, False)
            period(GROUPS // PERIOD - 1, True)

        def quant_scales(dve, am, floor, ready, s_safe, s_scale, n):
            src = am[:, 1, :] if ready == "car" else am[:, 0, :]
            dve.wait_ge(g[ready], n)
            dve.tensor_scalar(am[:, 2, :], src, floor, None, ALU.max).then_inc(g[s_safe], 1)
            dve.wait_ge(g[s_safe], 3 * n - 2)
            dve.tensor_scalar(am[:, 3, :], am[:, 2, :], 1.0 / FP8_MAX, None, ALU.mult).then_inc(g[s_safe], 1)
            dve.reciprocal(am[:, 0, :], am[:, 2, :]).then_inc(g[s_safe], 1)
            dve.wait_ge(g[s_safe], 3 * n)
            dve.tensor_scalar(am[:, 4, :], am[:, 0, :], FP8_MAX, None, ALU.mult).then_inc(g[s_scale], 1)
            dve.wait_ge(g[s_scale], n)

        def round_step(dve, src, dst, s_exp, s_magic, n):
            dve.tensor_scalar(dst.bitcast(U32), src.bitcast(U32), 0x7F800000, None, ALU.bitwise_and
                              ).then_inc(g[s_exp], 1)
            dve.wait_ge(g[s_exp], n)
            dve.tensor_scalar(dst, dst, 2.0 ** -6, 1.5 * 2.0 ** 20, ALU.max, ALU.mult).then_inc(g[s_magic], 1)

        def route(dve, b, stage):
            t2 = slice(2 * b, 2 * b + 2)
            if stage == "softmax":
                dve.wait_ge(g["lg"], b + 1)
                dve.tensor_reduce(lmx[:, t2], ps[:, M1, 0:2 * NE].rearrange("p (t e) -> p t e", t=2), AX.X, ALU.max,
                                  negate=True).then_inc(g["lmxs"], 1)
            if stage == "top":
                dve.wait_ge(g["exs"], 2 * b + 2)
                dve.reciprocal(erec[:, t2], esum[:, t2]).then_inc(g["ers"], 1)
                dve.wait_ge(g["ers"], b + 1)
                for t in (2 * b, 2 * b + 1):
                    dve.tensor_scalar(prob[:, t], ex[:, t], erec[:, t:t + 1], None, ALU.mult).then_inc(g["prb"], 1)
                dve.wait_ge(g["prb"], 2 * b + 2)
                for t in (2 * b, 2 * b + 1):
                    dve.max(top[:, t], prob[:, t]).then_inc(g["tps"], 1)
                dve.wait_ge(g["tps"], 2 * b + 2)
                for t in (2 * b, 2 * b + 1):
                    dve.match_replace(rep[:, t], top[:, t], prob[:, t], -1.0).then_inc(g["reps"], 1)
            if stage == "weights":
                dve.wait_ge(g["reps"], 2 * b + 2)
                dve.scalar_tensor_tensor(out=wun[:, t2], in0=rep[:, t2], scalar=0.0, in1=prob[:, t2],
                                         op0=ALU.is_lt, op1=ALU.mult).then_inc(g["wus"], 1)
                dve.wait_ge(g["wus"], b + 1)
                dve.tensor_reduce(wsum[:, t2], wun[:, t2], AX.X, ALU.add).then_inc(g["wss"], 1)
                dve.wait_ge(g["wss"], b + 1)
                dve.reciprocal(wrec[:, t2], wsum[:, t2]).then_inc(g["wrs"], 1)
                dve.wait_ge(g["wrs"], b + 1)
                for t in (2 * b, 2 * b + 1):
                    dve.tensor_scalar(wrt[:, t], wun[:, t], wrec[:, t:t + 1], None, ALU.mult
                                      ).then_inc(g["wrts"], 1)

        def split_hi(dve, n, buf, part, i):
            dve.wait_ge(d_wst[buf], (i + 1) * (16 * WST_DMAS))
            dve.tensor_copy(gh[:, buf, part], wstage[:, buf, part]).then_inc(g["ghi"], 1)

        def turn_hmul(dve, q):
            _, _, hs, j = turn(q)
            dve.wait_ge(g["up"], q + 1)
            dve.wait_ge(g["tmul"], q + 1)
            dve.tensor_tensor(hf[:, j, hs], ps[:, 2 + q % 2, :], tg[:, j, hs], ALU.mult).then_inc(g["hmul"], 1)

        def turn_hlo(dve, q):
            _, _, hs, j = turn(q)
            dve.wait_ge(g["hhi"], q + 1)
            dve.tensor_tensor(hl[:, j, hs], hf[:, j, hs], hh[:, j, hs].bitcast(F32), ALU.subtract
                              ).then_inc(g["hlo"], 1)

        def dve_experts(dve):
            for q in range(TURNS // 2, TURNS):
                turn_hmul(dve, q)
                turn_hlo(dve, q)
                if q >= TURNS - CH:
                    if q == TURNS - CH:
                        dve.wait_ge(g["down"], CH + 1)
                    split_hi(dve, PERIOD, 0, q - (TURNS - CH), 1)

            def period(i, last):
                for pg in range(PERIOD):
                    for c in range(CH):
                        n = (i * PERIOD + pg) * CH + c
                        j = (pg * CH + c) % 2
                        for h in range(2):
                            hs = slice(h * HALF, (h + 1) * HALF)
                            dve.wait_ge(g["up"], n * 2 + (h + 1))
                            dve.wait_ge(g["tmul"], n * 2 + (h + 1))
                            dve.tensor_tensor(hf[:, j, hs], ps[:, 2 + h, :], tg[:, j, hs], ALU.mult
                                              ).then_inc(g["hmul"], 1)
                        for h in range(2):
                            hs = slice(h * HALF, (h + 1) * HALF)
                            dve.wait_ge(g["hhi"], n * 2 + (h + 1))
                            dve.tensor_tensor(hl[:, j, hs], hf[:, j, hs], hh[:, j, hs].bitcast(F32), ALU.subtract
                                              ).then_inc(g["hlo"], 1)
                        if not (last and pg == PERIOD - 1):
                            if c == 0:
                                dve.wait_ge(g["down"], (i * PERIOD + pg) * CH + 1)
                            split_hi(dve, 0, 1 - pg, c, i if pg == 0 else i + 1)

            with dve.Fori(1, GROUPS // PERIOD - 1) as i:
                period(i, False)
            period(GROUPS // PERIOD - 1, True)

        @block.sync
        def _(sp):
            def load_rows(b):
                sp.dma_start(xs[:, 2 * b:2 * b + 2, :], x[b].rearrange("(t p) d -> p t d", p=P)).then_inc(d_x[b], 16)

            load_rows(0)
            for i, w in enumerate((Wq, Wk)):
                sp.dma_start(wraw[:, i], w.rearrange("(t p) n -> p t n", p=P)).then_inc(d_w[i], 16)
            for b in range(1, NB):
                load_rows(b)
            for i, w in ((2, Wv), (3, Wo)):
                sp.dma_start(wraw[:, i], w.rearrange("(t p) n -> p t n", p=P)).then_inc(d_w[i], 16)
            sp.dma_start(cw[:, :, :], ctx_2048.rearrange("e (a p) k -> p (e a) k", p=P)).then_inc(d_ctx, 16)
            for b in range(NB):
                sp.wait_ge(g["mnl"], b + 1)
                for a in range(2):
                    for j in range(2):
                        r0 = ROWS * a + MAXROW + j
                        sp.dma_start(qst[r0:r0 + 1, :, bs(b)].bitcast(F32),
                                     mneg[a:NH:2, j, :].bitcast(F32)).then_inc(d_max[b], 16)
                if b == 0:
                    sp.wait_ge(g["wlo"], 2)
                    sp.wait_ge(g["rp"], 32)
                    for par_g in range(2):
                        load_group(sp, par_g, par_g)
            sp.wait_ge(g["t_ready"], NB * NPAIR)
            for h in range(2):
                hs = slice(h * HALF, (h + 1) * HALF)
                sp.wait_ge(g["wte"], h + 1)
                sp.dma_start(routing_dram[:, hs], wT_sb[:, hs]).then_inc(d_rt, 16)
                sp.wait_ge(d_rt, 16 * (h + 1))
                for par_g in range(2):
                    load_routing(sp, par_g, par_g, hs)
                if h == 0:
                    for par_g in range(2):
                        sp.wait_ge(g["ghi"], (par_g + 1) * 3)
                        sp.wait_ge(g["glo"], (par_g + 1) * 3)
                        load_group(sp, PERIOD + par_g, par_g)
            for par_g in range(2):
                sp.wait_ge(g["tmul"], TURNS // 2 + (par_g + 1) * CH)
                load_routing(sp, PERIOD + par_g, par_g)
            with sp.Fori(1, GROUPS // PERIOD - 1) as i:
                for pg in range(PERIOD):
                    done = i * PERIOD + (pg + 1)
                    sp.wait_ge(g["ghi"], done * 3)
                    sp.wait_ge(g["glo"], done * 3)
                    load_group(sp, (i + 1) * PERIOD + pg, pg)
                    sp.wait_ge(g["tmul"], done * (2 * CH))
                    load_routing(sp, (i + 1) * PERIOD + pg, pg)
            for b in range(NB):
                sp.wait_ge(g["fin"], b + 1)
                sp.dma_start(out[b].rearrange("(t p) d -> p t d", p=P), xs[:, 2 * b:2 * b + 2, :]).then_inc(d_out, 16)
            sp.wait_ge(d_out, 16 * NB)

        @block.gpsimd
        def _(pool):
            pool.memset(zeros_bf[:, :], 0.0).then_inc(g["yzero"], 1)
            pool.memset(vs[:, :, :, 0, DH:VW], 1.0).then_inc(g["yzero"], 1)
            pool.memset(vs[:, :, :, 1:3, DH:VW], 0.0).then_inc(g["yzero"], 1)
            pool.wait_ge(d_const, 16)
            rsqrt(pool, 0, 0)
            for b in range(NB):
                if b + 1 < NB:
                    rsqrt(pool, 0, b + 1)
                pool.wait_ge(g["zh"], b + 1)
                pool.tensor_tensor(ztl[:, :, bs(b)], zf[:, b % 2], zth[:, :, bs(b)].bitcast(F32), ALU.subtract
                                   ).then_inc(g["zl"], 1)
            pool.wait_ge(g["yzero"], 3)
            for i in (2, 3):
                pool.wait_ge(g["whi"], i + 1)
                pool.tensor_tensor(wl[:, i], wraw[:, i], wh[:, i].bitcast(F32), ALU.subtract).then_inc(g["wlo"], 1)
            pool.wait_ge(g["cab"], 1)
            pool.partition_all_reduce(wam[:, 1, :], wam[:, 0, :], P, bass.bass_isa.ReduceOp.max).then_inc(g["car"], 1)
            for t in range(4):
                for i in range(2):
                    value_rest(pool, t, i)
            for step in range(STEPS):
                for i in range(2):
                    u = unit_of(step - i, VALUES)
                    if u is not None:
                        value_rest(pool, u, i)
                if step < NB:
                    pool.wait_ge(g["csc"], 1)
                    c4 = cw[:, 2 * step:2 * step + 2, :].rearrange("p a (k c) -> p (a k) c", c=P)
                    pool.tensor_tensor(c4, c4, wam[:, 4, 4 * step:4 * step + 4].unsqueeze(2).to_broadcast([P, 4, P]),
                                       ALU.mult).then_inc(g["cs1"], 1)
                e = step - 2
                if 0 <= e < NB:
                    pool.wait_ge(g["cs3"], e + 1)
                    e2 = slice(2 * e, 2 * e + 2)
                    pool.tensor_tensor(cw[:, e2, :], cw[:, e2, :], cm[:, e2, :], ALU.add).then_inc(g["cs4"], 1)
                e = step - NB - 2
                if 0 <= e < NB:
                    pool.wait_ge(g["cs4"], e + 1)
                    e2 = slice(2 * e, 2 * e + 2)
                    pool.tensor_tensor(cq[:, e2, :], cw[:, e2, :], cm[:, e2, :], ALU.subtract).then_inc(g["csb"], 1)
                if BIAS_X <= step < BIAS_X + NT:
                    if step == BIAS_X:
                        pool.wait_ge(d_bias, 32)
                        pool.wait_ge(ln_zn[0], NT)
                    add_output_bias(pool, step - BIAS_X)
                due = {name: rows_of(step, name) for name in ("deviation1", "scales", "round", "deviation2")}
                for name, b in sorted(((n, b) for n, b in due.items() if b is not None), key=lambda d: -d[1]):
                    if name in ("deviation1", "deviation2"):
                        rsqrt(pool, int(name[-1]), b)
                    elif name == "scales":
                        if b == 0:
                            pool.wait_ge(g["pj"], 8)
                        pool.wait_ge(g["qsc"], b + 1)
                        pool.tensor_tensor(xq1[:, b % 2], row_blocks(b),
                                           xam[:, b, 4, :].unsqueeze(2).to_broadcast([P, 4, P]), ALU.mult
                                           ).then_inc(g["qs1"], 1)
                    else:
                        o = b % 2
                        pool.wait_ge(g["qs3"], b + 1)
                        pool.tensor_tensor(xq3[:, o], xq1[:, o], xq2[:, o], ALU.add).then_inc(g["qs4"], 1)
                        pool.wait_ge(g["qs4"], b + 1)
                        pool.tensor_tensor(xqb[:, o], xq3[:, o], xq2[:, o], ALU.subtract).then_inc(g["qsb"], 1)
                m = step - LAG
                if 0 <= m < NB * NPAIR:
                    for a in range(2):
                        pool.wait_ge(g["ph16"], 2 * m + a + 1)
                        pool.tensor_tensor(ptl[m % 3][:, a], pt[:, m % 2, a], pth[m % 3][:, a], ALU.subtract
                                           ).then_inc(g["pl16"], 1)
                for grp, part in SPLIT_LO_AT.get(step, ()):
                    split_lo(pool, grp, grp, part)
                for q, at in GATING_AT.items():
                    if at == step:
                        turn_tmul(pool, q)
            pool_experts(pool)

        @block.scalar
        def _(act):
            act.dma_start(cst[:, :], consts).then_inc(d_const, 16)
            for i, v in enumerate((ln_g, ln_b, bq, bk)):
                act.dma_start(prow[2 * i:2 * i + 2, :], v.rearrange("(t p) -> t p", p=P)).then_inc(d_par, 16)
            for dst, v in ((bvb, bv), (bob, bo)):
                act.dma_start(dst[:, :], v.rearrange("(a n) -> a n", a=1).partition_broadcast(P)).then_inc(d_bias, 16)
            act.dma_start(rw_sb[:, :], router_w).then_inc(d_rw, 16)
            for i in range(4):
                act.wait_ge(d_w[i], 16)
                act.activation(wh[:, i], wraw[:, i], ACT.Copy).then_inc(g["whi"], 1)
            act.wait_ge(g["rtp"], 1)
            act.activation(par[:, :], ps[:, M1, KT * NE:KT * NE + 8], ACT.Copy).then_inc(g["rwt"], 1)
            act.activation(rwt[:, :, :], ps[:, M1, 0:KT * NE].rearrange("p (k e) -> p k e", k=KT), ACT.Copy
                           ).then_inc(g["rwt"], 1)
            for b in range(NB):
                act.wait_ge(g["zff"], 2 * b + 2)
                act.activation(zth[:, :, bs(b)], zf[:, b % 2], ACT.Copy).then_inc(g["zh"], 1)
            act.wait_ge(g["rwt"], 1)
            def projected(u):
                which, mt = u % 4 // 2, u % 2
                act.wait_ge(g["pj"], u + 1)
                if u >= 2:
                    act.wait_ge(g["pll"], u - 1)
                act.activation(pf[:, u % 2], ps[:, project_bank(u), :], ACT.Identity,
                               bias=par[:, 4 + 2 * which + mt:5 + 2 * which + mt]).then_inc(g["pff"], 1)

            def stacked(u):
                for i in range(3):
                    value_part(act, u, i)
                    if i < 2:
                        stack_evac(act, u, 0, i)

            def routing_out(h):
                act.wait_ge(g["wtp"], h + 1)
                act.activation(wT_sb[:, h * HALF:(h + 1) * HALF], ps[0:NE, ROUTE_BANK[h], :], ACT.Copy
                               ).then_inc(g["wte"], 1)

            for u in range(4):
                projected(u)
                if u >= 1:
                    stacked(u - 1)
            stacked(3)
            for step in range(STEPS):
                for i in range(2):
                    u = unit_of(step, STACK0 + i)
                    if u is not None:
                        stack_evac(act, u, 0, i)
                u = unit_of(step, PROJECT)
                if u is not None:
                    projected(u)
                for i in (2, 1, 0):
                    u = unit_of(step - i, VALUES)
                    if u is not None:
                        value_part(act, u, i)
                b = rows_of(step, "turn")
                if b is not None:
                    act.wait_ge(g["qtp"], b + 1)
                    act.activation(xqt[:, b % 2].rearrange("p k s -> p (k s)"), bf16_bank(M0), ACT.Copy
                                   ).then_inc(g["qev"], 1)
                m = step - LAG
                if 0 <= m < NB * NPAIR:
                    if m == 0:
                        act.wait_ge(g["csb"], NB)
                    act.wait_ge(g["t_ready"], m + 1)
                    if m >= 2:
                        act.wait_ge(g["pl16"], 2 * (m - 1))
                    act.activation(pt[:, m % 2], TB[:, :, P:512], ACT.Exp, scale=DH ** -0.5).then_inc(g["e_ready"], 1)
                    act.wait_ge(g["e_ready"], m + 1)
                    if m == 2:
                        act.wait_ge(g["rp"], 32)
                    if m >= 3:
                        act.wait_ge(g["av_ready"], m - 2)
                    for a in range(2):
                        act.activation(pth[m % 3][:, a], pt[:, m % 2, a], ACT.Copy).then_inc(g["ph16"], 1)
                if step % 8 == 0 and 1 <= step // 8 <= NB:
                    b = step // 8 - 1
                    act.wait_ge(g["mtp"], b + 1)
                    if b:
                        act.wait_ge(d_max[b - 1], 64)
                    act.activation(mneg[:, 0, :], ps[0:NH, M1, 0:S], ACT.Copy, scale=-1.0
                                   ).then_inc(g["mng"], 1)
                e = step - CTX_T
                if 0 <= e < NB:
                    act.wait_ge(g["ctp"], e + 1)
                    act.activation(cqt[:, e].rearrange("p k n -> p (k n)"), bf16_bank(M0), ACT.Copy
                                   ).then_inc(g["cev"], 1)
                b = rows_of(step, "transpose")
                if b is not None:
                    act.wait_ge(g["atp"], b + 1)
                    act.activation(zth[:, :, bs(b)], ps[:, M0, :].rearrange("p (k s) -> p k s", k=KT), ACT.Copy
                                   ).then_inc(g["ah"], 1)
                b = rows_of(step, "transpose3")
                if b is not None:
                    act.wait_ge(g["ytp"], b + 1)
                    act.activation(zth[:, :, bs(b)], ps[:, M0, :].rearrange("p (k s) -> p k s", k=KT), ACT.Copy
                                   ).then_inc(g["yh"], 1)
                b = rows_of(step, "softmax")
                if b is not None:
                    act.wait_ge(g["lmxs"], b + 1)
                    for t in range(2):
                        act.activation(ex[:, 2 * b + t], ps[:, M1, t * NE:(t + 1) * NE], ACT.Exp,
                                       bias=lmx[:, 2 * b + t:2 * b + t + 1],
                                       accum_out=esum[:, 2 * b + t:2 * b + t + 1]).then_inc(g["exs"], 1)
                for q, at in GATING_AT.items():
                    if at + 1 == step:
                        turn_hhi(act, q)
                if step in ROUTE_AT:
                    routing_out(ROUTE_AT.index(step))
                for q, at in GATE_AT.items():
                    if at == step:
                        turn_silu(act, q)
            act_experts(act)
            evacuate_output(act, 0)

        @block.tensor
        def _(pe):
            last_read = {}

            def take(bank, reader, count):
                if bank in last_read:
                    pe.wait_ge(*last_read[bank])
                last_read[bank] = (g[reader], count)

            pe.wait_ge(d_const, 16)
            pe.wait_ge(d_rw, 16)
            take(M1, "rwt", 2)
            for k in range(KT):
                pe.transpose(ps[:, M1, k * NE:(k + 1) * NE], rw_sb[:, k * P:(k + 1) * P], ident[0:NE, 0:NE])
            pe.wait_ge(d_par, 64)
            pe.transpose(ps[:, M1, KT * NE:KT * NE + 8], prow[:, :], ident[0:8, 0:8]).then_inc(g["rtp"], 1)
            def transposed(b):
                if b >= 2:
                    pe.wait_ge(g["zff"], 2 * (b - 1))
                for t in range(2):
                    pe.wait_ge(ln_zn[0], 2 * b + t + 1)
                    for k in range(KT):
                        mm = pe.transpose(OB[:, b % 2, k * S + t * P:k * S + (t + 1) * P],
                                          zs[:, 2 * b + t, k * P:(k + 1) * P], ident)
                mm.then_inc(g["ztp"], 1)

            def project(u):
                half, which, mt = u // 4, u % 4 // 2, u % 2
                if u % 4 == 0:
                    pe.wait_ge(g["zl"], 2 * half + 2)
                    pe.wait_ge(g["zh"], 2 * half + 2)
                if u < 4 and mt == 0:
                    pe.wait_ge(g["whi"], which + 1)
                    pe.wait_ge(cvt, 8 + which)
                if u in (4, 5):
                    pe.wait_ge(g["rev" if u == 4 else "rev2"], 7)
                if u == 7:
                    take(M0, "pff", u + 1)
                elif u >= 2:
                    pe.wait_ge(g["pff"], u - 1)
                ks = range(KT)
                hs = slice(half * HALF, (half + 1) * HALF)
                ms = slice(mt * P, (mt + 1) * P)
                f32_product(pe, ps[:, project_bank(u), :], [wh[:, which, k, ms] for k in ks],
                            [wl[:, which, k, ms] for k in ks],
                            [zth[:, k, hs] for k in ks], [ztl[:, k, hs] for k in ks], True, True
                            ).then_inc(g["pj"], 1)

            def stack(u, lps):
                which = u % 4 // 2
                if u == 0 and lps[0] == 0:
                    pe.wait_ge(cvt, 9)
                    pe.wait_ge(g["zff"], 2 * NB)
                pe.wait_ge(g["pll"], u + 1)
                for lp in lps:
                    k = 4 * u + lp
                    bank, copied = stack_bank(u, lp), "rev" if lp % 2 == 0 else "rev2"
                    if u == 7:
                        take(bank, copied, 2 * u + lp // 2 + 1)
                    elif k >= 4:
                        pe.wait_ge(g[copied], 2 * (u - 1) + lp // 2 + 1 if u < 4 else 2 * u + lp // 2)
                    pe.matmul(ps[:, bank, :], R[:, lp, 2 * which], ph[:, u % 2], start=True, stop=False)
                    pe.matmul(ps[:, bank, :], R[:, lp, 2 * which + 1], pl[:, u % 2], start=False, stop=True
                              ).then_inc(g["rp"], 1)

            def values(t):
                take(M0 + t % 2, "vev", t + 1)
                if t == 0:
                    pe.wait_ge(g["whi"], 3)
                    pe.wait_ge(g["wlo"], 1)
                ks = range(KT)
                ts = slice(t * P, (t + 1) * P)
                f32_product(pe, ps[:, M0 + t % 2, 0:D], [zth[:, k, ts] for k in ks], [ztl[:, k, ts] for k in ks],
                            [wh[:, 2, k] for k in ks], [wl[:, 2, k] for k in ks], True, True
                            ).then_inc(g["vpj"], 1)

            for b in range(NB):
                transposed(b)
            project(0)
            for u in range(4):
                if u < 3:
                    project(u + 1)
                values(u)
                stack(u, range(4))

            def routing_in(h):
                pe.wait_ge(g["wrts"], 4 * (h + 1))
                for t in range(4):
                    mm = pe.transpose(ps[0:NE, ROUTE_BANK[h], t * P:(t + 1) * P], wrt[:, 4 * h + t, :], ident)
                mm.then_inc(g["wtp"], 1)

            def scores(n):
                b, hp = n // NPAIR, n % NPAIR
                if n in (0, 16):
                    pe.wait_ge(g["rev"], 8 if n == 0 else 16)
                    pe.wait_ge(g["rev2"], 8 if n == 0 else 16)
                if n:
                    pe.wait_ge(g["s_max"], 2 * n)
                for a in range(2):
                    rs = slice(ROWS * a, ROWS * (a + 1))
                    for qt in range(2):
                        c0 = b * S + qt * P
                        pe.matmul(SB[:, a, qt * S:(qt + 1) * S], qst[rs, hp, c0:c0 + P], kst[rs, hp, bs(b)],
                                  start=(qt == 0), stop=False, skip_group_check=True)
                for a in range(2):
                    blocks = SB[:, a, :].rearrange("p (n c) -> p n c", c=P)[:, 0:4:3, :]
                    mm = pe.matmul(blocks, ident_bf[:, :], mask_s[:, :, :], start=False, stop=True,
                                   skip_group_check=True)
                mm.then_inc(g["s_ready"], 1)

            def scores_t(m):
                b, hp = m // NPAIR, m % NPAIR
                if hp == 0:
                    pe.wait_ge(d_max[b], 64)
                if m == 0:
                    pe.wait_ge(g["pff"], 7)
                if m:
                    pe.wait_ge(g["e_ready"], m)
                for a in range(2):
                    rs = slice(ROWS * a, ROWS * (a + 1))
                    for half in range(2):
                        c0 = b * S + (1 - half) * P
                        pe.matmul(TB[:, a, half * S:(half + 1) * S], kst[rs, hp, c0:c0 + P], qst[rs, hp, bs(b)],
                                  start=(half == 0), stop=False, skip_group_check=True)
                for a in range(2):
                    mm = pe.matmul(TB[:, a, P:P + 2 * P], ident_bf[:, :],
                                   mask_t[:, :, :].rearrange("p n c -> p (n c)"), start=False, stop=True,
                                   skip_group_check=True)
                mm.then_inc(g["t_ready"], 1)

            def attend(m):
                b, hp = m // NPAIR, m % NPAIR
                if hp == 0 and b:
                    pe.wait_ge(g["avt_n"], 2 * b)
                if m == 0:
                    pe.wait_ge(g["v3"], 3 * NT)
                    pe.wait_ge(g["rev"], 14)
                    pe.wait_ge(g["rev2"], 14)
                for a in range(2):
                    h = 2 * hp + a
                    pe.wait_ge(g["ph16"], 2 * m + a + 1)
                    pe.wait_ge(g["pl16"], 2 * m + a + 1)
                    for qt, kt, blk in ((0, 0, 1), (1, 0, 2), (1, 1, 0)):
                        for j, prob in enumerate((pth, ptl)):
                            for i in range(3):
                                mm = pe.matmul(OB[:, qt, h * VW:(h + 1) * VW],
                                               prob[m % 3][:, a, blk * P:(blk + 1) * P],
                                               vs[:, 2 * b + kt, h, i, :],
                                               start=(h == 0 and kt == 0 and j == 0 and i == 0),
                                               stop=True, skip_group_check=True)
                mm.then_inc(g["av_ready"], 1)

            for step in range(STEPS):
                if step == ROUTE_AT[0]:
                    pe.wait_ge(g["e_ready"], NB * NPAIR)
                    routing_in(0)
                if step == ROUTE_AT[1]:
                    take(M0, "wte", 2)
                    routing_in(1)
                if step < NB * NPAIR:
                    scores(step)
                for i in range(2):
                    u = unit_of(step, STACK0 + i)
                    if u is not None:
                        stack(u, (2 * i, 2 * i + 1))
                u = unit_of(step, VALUES)
                if u is not None:
                    values(u)
                u = unit_of(step, PROJECT)
                if u is not None:
                    project(u)
                if 0 <= step - LAG - AV_LAG < NB * NPAIR:
                    attend(step - LAG - AV_LAG)
                b = rows_of(step, "context")
                if b is not None:
                    pe.wait_ge(g["qev"], b + 1)
                    if b == 0:
                        pe.wait_ge(g["cev"], NB)
                    for t in range(2):
                        take(M0 + t, "x2", 8 * b + 4 * (t + 1))
                        for k in range(KT):
                            mm = pe.matmul(ps[:, M0 + t, k * D:(k + 1) * D], xqt[:, b % 2, k, t * P:(t + 1) * P],
                                           cqt[:, b, k], start=(k == 0), stop=True, skip_group_check=True)
                        mm.then_inc(g["xmm"], 1)
                if 0 <= step - LAG < NB * NPAIR:
                    scores_t(step - LAG)
                b = rows_of(step, "turn")
                if b is not None:
                    take(M0, "qev", b + 1)
                    pe.wait_ge(g["qsb"], b + 1)
                    for t in range(2):
                        for k in range(KT):
                            mm = pe.transpose(bf16_bank(M0)[:, k * S + t * P:k * S + (t + 1) * P],
                                              xqb[:, b % 2, 2 * t + k], ident_bf[:, :])
                    mm.then_inc(g["qtp"], 1)
                if step % 8 == 0 and 1 <= step // 8 <= NB:
                    b = step // 8 - 1
                    take(M1, "mnl", b + 1)
                    pe.wait_ge(g["s_max"], 2 * NPAIR * (b + 1))
                    for qt in range(2):
                        mm = pe.transpose(ps[0:NH, M1, qt * P:(qt + 1) * P], mx[:, b, qt], ident)
                    mm.then_inc(g["mtp"], 1)
                e = step - CTX_T
                if 0 <= e < NB:
                    take(M0, "cev", e + 1)
                    pe.wait_ge(g["csb"], e + 1)
                    for kb in range(KT):
                        for nb in range(2):
                            mm = pe.transpose(bf16_bank(M0)[:, kb * D + nb * P:kb * D + (nb + 1) * P],
                                              cq[:, 2 * e + nb, kb * P:(kb + 1) * P], ident_bf[:, :])
                    mm.then_inc(g["ctp"], 1)
                b = rows_of(step, "transpose")
                if b is not None:
                    take(M0, "al", b + 1)
                    pe.wait_ge(g["avt_n"], 2 * b + 2)
                    for t in range(2):
                        for k in range(KT):
                            mm = pe.transpose(ps[:, M0, k * S + t * P:k * S + (t + 1) * P],
                                              avn[:, 2 * b + t, k * P:(k + 1) * P], ident)
                    mm.then_inc(g["atp"], 1)
                b = rows_of(step, "project")
                if b is not None:
                    take(M1, "x1", b + 1)
                    if b == 0:
                        pe.wait_ge(g["whi"], 4)
                        pe.wait_ge(g["wlo"], 2)
                    pe.wait_ge(g["ah"], b + 1)
                    pe.wait_ge(g["al"], b + 1)
                    ks = range(KT)
                    for t in range(2):
                        ts = slice((2 * b + t) * P, (2 * b + t + 1) * P)
                        mm = f32_product(pe, ps[:, M1, t * D:(t + 1) * D], [zth[:, k, ts] for k in ks],
                                         [ztl[:, k, ts] for k in ks], [wh[:, 3, k] for k in ks],
                                         [wl[:, 3, k] for k in ks], t == 0, True)
                    mm.then_inc(g["wo"], 1)
                b = rows_of(step, "transpose3")
                if b is not None:
                    take(M0, "yl", b + 1)
                    pe.wait_ge(ln_zn[2], 2 * b + 2)
                    for t in range(2):
                        for k in range(KT):
                            mm = pe.transpose(ps[:, M0, k * S + t * P:k * S + (t + 1) * P],
                                              zs[:, 2 * b + t, k * P:(k + 1) * P], ident)
                    mm.then_inc(g["ytp"], 1)
                b = rows_of(step, "logits")
                if b is not None:
                    take(M1, "exs", 2 * b + 2)
                    pe.wait_ge(g["yh"], b + 1)
                    pe.wait_ge(g["yl"], b + 1)
                    for t in range(2):
                        ts = slice((2 * b + t) * P, (2 * b + t + 1) * P)
                        for j, z in enumerate((zth, ztl)):
                            for k in range(KT):
                                mm = pe.matmul(ps[:, M1, t * NE:(t + 1) * NE], z[:, k, ts].bitcast(F32), rwt[:, k],
                                               start=(t == 0 and j == 0 and k == 0), stop=True,
                                               skip_group_check=True)
                    mm.then_inc(g["lg"], 1)
                if step == OUTPUT_AT[0]:
                    pe.wait_ge(g["yzero"], 3)
                    pe.wait_ge(g["avt_n"], 2 * NB)
                    output_zero(pe, 0)
                for q, at in UP_AT.items():
                    if at == step and GATE_AT[q] < step:
                        turn_hidden(pe, q, 1)
                for q, at in OUTPUT_AT.items():
                    if at == step:
                        turn_output(pe, q)
                for q, at in GATE_AT.items():
                    if at == step:
                        if q == 1:
                            pe.wait_ge(g["wte"], 1)
                        turn_hidden(pe, q, 0)
                        if UP_AT[q] == step:
                            turn_hidden(pe, q, 1)
            take(M1, "wte", 2)
            take(M0, "wte", 2)
            pe_experts(pe)
            for b in range(NB):
                pe.wait_ge(g["yev"], b // 2 + 1)
                pe.wait_ge(g["yev1"], b // 2 + 1)
                for t in range(2):
                    for k in range(KT):
                        mm = pe.transpose(ps[:, b, t * D + k * P:t * D + (k + 1) * P],
                                          yt[:, k, (2 * b + t) * P:(2 * b + t + 1) * P], ident)
                mm.then_inc(g["ftp"], 1)

        @block.vector
        def _(dve):
            dve.wait_ge(d_const, 16)

            def stats_of(ln, b):
                for t in (2 * b, 2 * b + 1):
                    dve.bn_stats(stats[:, ln, t], xs[:, t]).then_inc(ln_bn[ln], 1)
                dve.wait_ge(ln_bn[ln], 2 * b + 2)
                for t in (2 * b, 2 * b + 1):
                    dve.bn_aggr(mv[:, ln, t], stats[:, ln, t]).then_inc(ln_ag[ln], 1)
                dve.wait_ge(ln_ag[ln], 2 * b + 2)
                m, a = (1.0 + EPS, EPS * EPS) if ln == 0 else (1.0, EPS)
                dve.tensor_scalar(rs_in[:, ln, 2 * b:2 * b + 2], mv[:, ln, 2 * b:2 * b + 2, 1], m, a,
                                  ALU.mult, ALU.add).then_inc(ln_ri[ln], 1)

            def normalise(ln, b):
                dve.wait_ge(ln_rs[ln], b + 1)
                for t in (2 * b, 2 * b + 1):
                    dve.tensor_scalar(zs[:, t], xs[:, t], mv[:, ln, t, 0:1], rstd[:, ln, t:t + 1],
                                      ALU.subtract, ALU.mult).then_inc(ln_zn[ln], 1)

            dve.wait_ge(d_x[0], 16)
            stats_of(0, 0)
            normalise(0, 0)
            for lp in range(4):
                dve.tensor_scalar(R[:, lp].rearrange("p k c -> p (k c)"), cst[:, C_QH * P:(C_KL + 1) * P],
                                  cst[:, C_ONE * P + 2 + lp:C_ONE * P + 3 + lp], None, ALU.mult).then_inc(cvt, 1)
            dve.tensor_copy(ident_bf[:, :], ident).then_inc(cvt, 1)
            for dst, i in ((mask_s, C_MS), (mask_t, C_MT)):
                dve.tensor_copy(dst[:, :, :], cst[:, i * P:(i + 1) * P].unsqueeze(1).to_broadcast([P, 2, P])
                                ).then_inc(cvt, 1)
            for i in (0, 1):
                dve.wait_ge(g["whi"], i + 1)
                dve.tensor_tensor(wl[:, i], wraw[:, i], wh[:, i].bitcast(F32), ALU.subtract).then_inc(cvt, 1)
            dve.wait_ge(g["rwt"], 1)

            def scaled(b):
                dve.wait_ge(g["ztp"], b + 1)
                if b >= 2:
                    dve.wait_ge(g["zl"], b - 1)
                for k in range(KT):
                    dve.tensor_scalar(zf[:, b % 2, k], OB[:, b % 2, k * S:(k + 1) * S], par[:, k:k + 1],
                                      par[:, 2 + k:3 + k], ALU.mult, ALU.add).then_inc(g["zff"], 1)

            for b in range(1, NB):
                dve.wait_ge(d_x[b], 16)
                stats_of(0, b)
                scaled(b - 1)
                normalise(0, b)
            scaled(NB - 1)
            dve.wait_ge(d_ctx, 16)
            cw4 = cw[:, :, :].rearrange("p a (k c) -> p (a k) c", c=P)
            dve.tensor_reduce(wam[:, 0, :], cw4, AX.X, ALU.max, apply_absolute_value=True).then_inc(g["cab"], 1)
            dve.wait_ge(d_bias, 32)

            def values_out(t):
                dve.wait_ge(g["vpj"], t + 1)
                if t >= 2:
                    dve.wait_ge(g["vsub"], 2 * (t - 1))
                dve.tensor_tensor(vf[:, t % 2], ps[:, M0 + t % 2, 0:D], bvb[:, :], ALU.add).then_inc(g["vev"], 1)

            def projected(u):
                dve.wait_ge(g["pff"], u + 1)
                if u >= 2:
                    dve.wait_ge(g["rp"], 4 * (u - 1))
                dve.tensor_copy(ph[:, u % 2], pf[:, u % 2]).then_inc(g["phh"], 1)
                dve.wait_ge(g["phh"], u + 1)
                dve.tensor_tensor(pl[:, u % 2], pf[:, u % 2], ph[:, u % 2].bitcast(F32), ALU.subtract
                                  ).then_inc(g["pll"], 1)

            for u in range(4):
                projected(u)
                values_out(u)
                stack_evac(dve, u, 1)
                if u == 1:
                    quant_scales(dve, wam, W_FLOOR, "car", "csf", "csc", 1)

            def divide_rows(b):
                dve.wait_ge(g["av_ready"], NPAIR * (b + 1))
                o4 = OB[:, :, 0:NH * VW].rearrange("p q (h w) -> p q h w", w=VW)
                dve.reciprocal(rinv[:, b], o4[:, :, :, DH]).then_inc(g["rin"], 1)
                dve.wait_ge(g["rin"], b + 1)
                for q in range(2):
                    dve.tensor_tensor(avn[:, 2 * b + q, :].rearrange("p (h d) -> p h d", h=NH),
                                      o4[:, q, :, 0:DH],
                                      rinv[:, b, q].unsqueeze(2).to_broadcast([P, NH, DH]), ALU.mult
                                      ).then_inc(g["avt_n"], 1)

            def low_rows(b):
                dve.wait_ge(g["ah"], b + 1)
                dve.tensor_tensor(ztl[:, :, bs(b)], ps[:, M0, :].rearrange("p (k s) -> p k s", k=KT),
                                  zth[:, :, bs(b)].bitcast(F32), ALU.subtract).then_inc(g["al"], 1)

            def residual_rows(b):
                dve.wait_ge(g["wo"], b + 1)
                if b == 0:
                    dve.wait_ge(g["bias_x"], NT)
                dve.tensor_tensor(xs[:, 2 * b:2 * b + 2, :], ps[:, M1, :].rearrange("p (t d) -> p t d", t=2),
                                  xs[:, 2 * b:2 * b + 2, :], ALU.add).then_inc(g["x1"], 1)
                dve.wait_ge(g["x1"], b + 1)
                stats_of(1, b)

            def ln2_rows(b):
                normalise(1, b)
                dve.wait_ge(ln_zn[1], 2 * b + 2)
                dve.tensor_reduce(xam[:, b, 0, :], row_blocks(b), AX.X, ALU.max, apply_absolute_value=True
                                  ).then_inc(g["qam"], 1)

            def scale_rows(b):
                xa = xam[:, b]
                quant_scales(dve, xa, ACT_FLOOR, "qam", "qsf", "qsc", b + 1)
                for kb in range(KT):
                    dve.tensor_tensor(
                        xsc[:, b].rearrange("p (t k) n -> p t k n", k=KT)[:, :, kb, :],
                        xa[:, 3, :].rearrange("p (t k) -> p t k", k=KT)[:, :, kb:kb + 1].to_broadcast([P, 2, 2]),
                        wam[:, 3, 4 * b + kb:4 * b + kb + 3:2].unsqueeze(1).to_broadcast([P, 2, 2]),
                        ALU.mult).then_inc(g["xscs"], 1)

            def round_rows(b):
                dve.wait_ge(g["qs1"], b + 1)
                round_step(dve, xq1[:, b % 2], xq2[:, b % 2], "qs2", "qs3", b + 1)

            def residual2_rows(b):
                dve.wait_ge(g["xscs"], 2 * b + 2)
                for t in range(2):
                    dve.wait_ge(g["xmm"], 2 * b + t + 1)
                    for kb in range(KT):
                        if kb:
                            dve.wait_ge(g["x2"], 8 * b + 4 * t + 2)
                        for nb in range(2):
                            xo = xs[:, 2 * b + t, nb * P:(nb + 1) * P]
                            dve.scalar_tensor_tensor(
                                out=xo, in0=ps[:, M0 + t, kb * D + nb * P:kb * D + (nb + 1) * P],
                                scalar=xsc[:, b, 2 * t + kb, nb:nb + 1], in1=xo, op0=ALU.mult, op1=ALU.add
                            ).then_inc(g["x2"], 1)

            def stats3_rows(b):
                dve.wait_ge(g["x2"], 8 * b + 8)
                stats_of(2, b)

            def ln3_rows(b):
                normalise(2, b)

            def low3_rows(b):
                dve.wait_ge(g["yh"], b + 1)
                dve.tensor_tensor(ztl[:, :, bs(b)], ps[:, M0, :].rearrange("p (k s) -> p k s", k=KT),
                                  zth[:, :, bs(b)].bitcast(F32), ALU.subtract).then_inc(g["yl"], 1)

            def softmax_rows(b):
                route(dve, b, "softmax")

            def top_rows(b):
                route(dve, b, "top")

            def weights_rows(b):
                route(dve, b, "weights")

            stages = {"divide": divide_rows, "low": low_rows, "residual": residual_rows, "LN2": ln2_rows,
                      "scales": scale_rows, "round": round_rows, "low3": low3_rows,
                      "residual2": residual2_rows, "stats3": stats3_rows, "LN3": ln3_rows,
                      "softmax": softmax_rows, "top": top_rows, "weights": weights_rows}

            def run(step, names):
                for name in names:
                    b = rows_of(step, name)
                    if b is not None:
                        stages[name](b)

            for step in range(STEPS):
                if step < NB * NPAIR:
                    n = step
                    b, hp = n // NPAIR, n % NPAIR
                    dve.wait_ge(g["s_ready"], n + 1)
                    dve.tensor_reduce(mx[:, b, 0, 2 * hp:2 * hp + 2], SB[:, :, 0:P], AX.X, ALU.max
                                      ).then_inc(g["s_max"], 1)
                    dve.tensor_reduce(mx[:, b, 1, 2 * hp:2 * hp + 2], SB[:, :, S:2 * S], AX.X, ALU.max
                                      ).then_inc(g["s_max"], 1)
                if step < TAIL:
                    run(step, ("low", "low3", "LN3"))
                if step % 8 == 1 and 1 <= step // 8 <= NB:
                    b = step // 8 - 1
                    dve.wait_ge(g["mng"], b + 1)
                    dve.scalar_tensor_tensor(out=mneg[:, 1, :], in0=ps[0:NH, M1, 0:S], scalar=-1.0,
                                             in1=mneg[:, 0, :].bitcast(F32), op0=ALU.mult, op1=ALU.subtract
                                             ).then_inc(g["mnl"], 1)
                for i in range(2):
                    u = unit_of(step, STACK0 + i)
                    if u is not None:
                        stack_evac(dve, u, 1, i)
                u = unit_of(step, VALUES)
                if u is not None:
                    values_out(u)
                u = unit_of(step, PROJECT)
                if u is not None:
                    projected(u)
                e = step - 1
                if 0 <= e < NB:
                    dve.wait_ge(g["cs1"], e + 1)
                    e2 = slice(2 * e, 2 * e + 2)
                    round_step(dve, cw[:, e2, :], cm[:, e2, :], "cs2", "cs3", e + 1)
                if step < TAIL:
                    run(step, ("divide", "residual", "LN2", "scales", "round", "residual2", "stats3", "softmax",
                               "top", "weights"))
                else:
                    run(step, ["low3"])
                    for b in reversed(range(NB)):
                        run(step, [name for name in stages if name != "low3" and rows_of(step, name) == b])
                if step in SPLIT_HI_AT:
                    grp = SPLIT_HI_AT[step]
                    if grp == 0:
                        dve.wait_ge(g["t_ready"], NB * NPAIR)
                    for part in range(3):
                        split_hi(dve, grp, grp, part, 0)
                for q, at in GATING_AT.items():
                    if at + 1 == step:
                        turn_hlo(dve, q)
                for q, at in GATING_AT.items():
                    if at == step:
                        turn_hmul(dve, q)
            dve_experts(dve)
            evacuate_output(dve, 1)
            for b in range(NB):
                dve.wait_ge(g["ftp"], b + 1)
                dve.tensor_tensor(xs[:, 2 * b:2 * b + 2, :], ps[:, b, :].rearrange("p (t d) -> p t d", t=2),
                                  xs[:, 2 * b:2 * b + 2, :], ALU.add).then_inc(g["fin"], 1)


def kernel(**inputs):
    import numpy as _np
    import concourse.bacc as _bacc
    from concourse import mybir as _mybir
    from concourse.bass_utils import run_bass_kernel_spmd as _run

    nc = _bacc.Bacc("TRN2", target_bir_lowering=False, num_devices=1)
    names = ["x", "ctx_2048"] + ["L0_attn_" + n for n in
                                 ("ln_g", "ln_b", "Wq", "bq", "Wk", "bk", "Wv", "bv", "Wo", "bo")]
    names += ["L0_ffn_" + n for n in ("router_w", "w_gate", "w_up", "w_down")]
    arrays = {"in_consts": host_constants()}
    args = [nc.dram_tensor("in_consts", arrays["in_consts"].shape, _mybir.dt.float32, kind="ExternalInput").ap()]
    for name in names:
        a = _np.ascontiguousarray(inputs[name])
        arrays["in_" + name] = a
        args.append(nc.dram_tensor("in_" + name, a.shape, _mybir.dt.from_np(a.dtype), kind="ExternalInput").ap())
    args.append(nc.dram_tensor("out_x", (NB, S, D), _mybir.dt.float32, kind="ExternalOutput").ap())
    decoder_layer(nc, *args)
    r = _run(nc, [arrays], core_ids=[0])
    return r.results[0]["out_x"]
```
